# Optimizing a Trainium2 kernel written in Bass

```python
import numpy as np
import jax
import jax.numpy as jnp

def _softmax(x, axis=-1):
    return jax.nn.softmax(x, axis=axis)

def _gelu(x):
    return jax.nn.gelu(x, approximate=True)

def _silu(x):
    return jax.nn.silu(x)

def _sigmoid(x):
    return jax.nn.sigmoid(x)

def _layernorm(x, axis=-1, eps=1e-05):
    m = jnp.mean(x, axis=axis, keepdims=True)
    v = jnp.var(x, axis=axis, keepdims=True)
    return (x - m) / jnp.sqrt(v + eps)

def _scatter_add(tgt, idx, src, axis=0):
    return tgt.at[idx].add(src)

def _segment_sum(src, seg, n):
    return jax.ops.segment_sum(src, seg, n)
kernel_name = 'mk_early_fusion_d2_tok_img1024_r4_dbd7f9'

def setup_inputs(seed: int=0):
    np.random.seed(seed)
    _w = jnp.asarray

    def _rec_inputs():
        import jax
        import jax.numpy as jnp
        _rk = jax.random.key(seed)
        x = -0.00016672 + 0.999947 * jax.random.normal(jax.random.fold_in(_rk, 1), (16, 96, 96, 3), jnp.float32)
        txt = -0.000115308 + 1.00019 * jax.random.normal(jax.random.fold_in(_rk, 2), (16, 77, 256), jnp.float32)
        return (x, txt)
    x, txt = _rec_inputs()

    def _L0_tok_setup():
        import jax, jax.numpy as jnp
        import numpy as np
        P = 16
        E = 256

        def patchify(images, patch_size):
            B, H, W, C = images.shape
            hp, wp = (H // patch_size, W // patch_size)
            x = images.reshape(B, hp, patch_size, wp, patch_size, C)
            x = x.transpose(0, 1, 3, 2, 4, 5)
            return x.reshape(B, hp * wp, patch_size * patch_size * C)
        key = jax.random.key(seed)
        k_img, k_w, k_b, k_pos = jax.random.split(key, 4)
        B, H, W, C = (64, 96, 96, 3)
        patch_dim = P * P * C
        patch_count = H // P * (W // P)
        images = jax.random.normal(k_img, (B, H, W, C), dtype=jnp.float32)
        W_proj = jax.random.normal(k_w, (E, patch_dim), dtype=jnp.float32) * patch_dim ** (-0.5)
        b_proj = jax.random.normal(k_b, (E,), dtype=jnp.float32) * 0.02
        pos_emb = jax.random.normal(k_pos, (patch_count, E), dtype=jnp.float32) * 0.02
        return {'images': images, 'W_proj': W_proj, 'b_proj': b_proj, 'pos_emb': pos_emb}
    _L0_tok_all = _L0_tok_setup()
    _L0_tok_in = {k: v for k, v in _L0_tok_all.items() if k in ('W_proj', 'b_proj', 'pos_emb')}
    del _L0_tok_all

    def _L0_attn_setup():
        import jax, jax.numpy as jnp
        import numpy as np
        B, S, D, H = (2, 512, 256, 16)
        HD = D // H
        key = jax.random.key(seed)
        k0, k1, k2 = jax.random.split(key, 3)
        return {'x': jax.random.normal(k0, (B, S, D), jnp.float32), 'qkv_w': jax.random.normal(k1, (D, 3 * D), jnp.float32) / np.sqrt(D).astype(np.float32), 'qkv_b': jnp.zeros((3 * D,), jnp.float32), 'out_w': jax.random.normal(k2, (D, D), jnp.float32) / np.sqrt(D).astype(np.float32), 'out_b': jnp.zeros((D,), jnp.float32)}
    _L0_attn_all = _L0_attn_setup()
    _L0_attn_in = {k: v for k, v in _L0_attn_all.items() if k in ('qkv_w', 'qkv_b', 'out_w', 'out_b')}
    del _L0_attn_all

    def _L0_ffn_setup():
        import jax, jax.numpy as jnp
        import numpy as np
        B, T, C, H, E = (1, 64, 256, 512, 8)
        STD = 0.02
        key = jax.random.key(seed)
        ks = jax.random.split(key, 8)
        f32 = jnp.float32
        return {'x': jax.random.normal(ks[0], (B, T, C), f32), 'up': jax.random.normal(ks[1], (E, H, C), f32) * STD, 'gate': jax.random.normal(ks[2], (E, H, C), f32) * STD, 'down': jax.random.normal(ks[3], (E, C, H), f32) * STD, 'router': jax.random.normal(ks[4], (E, C), f32) * STD, 'w_up_s': jax.random.normal(ks[5], (H, C), f32) * STD, 'w_gate_s': jax.random.normal(ks[6], (H, C), f32) * STD, 'w_down_s': jax.random.normal(ks[7], (C, H), f32) * STD}
    _L0_ffn_all = _L0_ffn_setup()
    _L0_ffn_in = {k: v for k, v in _L0_ffn_all.items() if k in ('up', 'gate', 'down', 'router', 'w_up_s', 'w_gate_s', 'w_down_s')}
    del _L0_ffn_all

    def _L1_attn_setup():
        import jax, jax.numpy as jnp
        import numpy as np
        EMBED = 256
        DSTATE = 16
        DCONV = 4
        DTRANK = 64
        B = 2
        T = 512
        key = jax.random.key(seed)
        ks = jax.random.split(key, 8)

        def w(k, shape, s=0.02):
            return jax.random.normal(k, shape, dtype=jnp.float32) * s
        return dict(x=jax.random.normal(ks[0], (B, T, EMBED), dtype=jnp.float32), in_proj_w=w(ks[1], (2 * EMBED, EMBED)), in_proj_b=jnp.zeros((2 * EMBED,), jnp.float32), conv_w=w(ks[2], (EMBED, 1, DCONV)), conv_b=jnp.zeros((EMBED,), jnp.float32), x_proj_w=w(ks[3], (DTRANK + 2 * DSTATE, EMBED)), x_proj_b=jnp.zeros((DTRANK + 2 * DSTATE,), jnp.float32), dt_proj_w=w(ks[4], (EMBED, DTRANK)), dt_proj_b=jnp.zeros((EMBED,), jnp.float32), A_log=jnp.log(jnp.arange(1, DSTATE + 1, dtype=jnp.float32))[None, :], D_param=jnp.ones((EMBED,), jnp.float32), out_proj_w=w(ks[5], (EMBED, EMBED)), out_proj_b=jnp.zeros((EMBED,), jnp.float32), skip_proj_w=w(ks[6], (EMBED, EMBED)), skip_proj_b=jnp.zeros((EMBED,), jnp.float32))
    _L1_attn_all = _L1_attn_setup()
    _L1_attn_in = {k: v for k, v in _L1_attn_all.items() if k in ('in_proj_w', 'in_proj_b', 'conv_w', 'conv_b', 'x_proj_w', 'x_proj_b', 'dt_proj_w', 'dt_proj_b', 'A_log', 'D_param', 'out_proj_w', 'out_proj_b', 'skip_proj_w', 'skip_proj_b')}
    del _L1_attn_all

    def _L1_ffn_setup():
        import jax, jax.numpy as jnp
        import numpy as np
        QMAX = 127.0

        def _ste_round(v):
            return v + jax.lax.stop_gradient(jnp.round(v) - v)

        def _act_fake_quant(x, clip_factor):
            scale = jax.nn.sigmoid(clip_factor) * jnp.max(jnp.abs(x)) / QMAX
            return jnp.clip(_ste_round(x / scale), -QMAX - 1.0, QMAX) * scale

        def _weight_fake_quant(w):
            scale = jnp.max(jnp.abs(w), axis=1, keepdims=True) / QMAX
            return jnp.clip(_ste_round(w / scale), -QMAX - 1.0, QMAX) * scale
        key = jax.random.key(seed)
        k1, k2, k3, k4 = jax.random.split(key, 4)
        B, S, H, I = (8, 2048, 256, 704)
        return {'x': jax.random.normal(k1, (B, S, H), dtype=jnp.float32), 'clip_x': jnp.full((1,), 4.0, dtype=jnp.float32), 'clip_down': jnp.full((1,), 4.0, dtype=jnp.float32), 'w_gate': jax.random.normal(k2, (I, H), dtype=jnp.float32) * 0.02, 'w_up': jax.random.normal(k3, (I, H), dtype=jnp.float32) * 0.02, 'w_down': jax.random.normal(k4, (H, I), dtype=jnp.float32) * 0.02}
    _L1_ffn_all = _L1_ffn_setup()
    _L1_ffn_in = {k: v for k, v in _L1_ffn_all.items() if k in ('clip_x', 'clip_down', 'w_gate', 'w_up', 'w_down')}
    del _L1_ffn_all
    return {'x': x, 'txt': txt, 'L0_tok_W_proj': _L0_tok_in['W_proj'], 'L0_tok_b_proj': _L0_tok_in['b_proj'], 'L0_tok_pos_emb': _L0_tok_in['pos_emb'], 'L0_attn_qkv_w': _L0_attn_in['qkv_w'], 'L0_attn_qkv_b': _L0_attn_in['qkv_b'], 'L0_attn_out_w': _L0_attn_in['out_w'], 'L0_attn_out_b': _L0_attn_in['out_b'], 'L0_ffn_up': _L0_ffn_in['up'], 'L0_ffn_gate': _L0_ffn_in['gate'], 'L0_ffn_down': _L0_ffn_in['down'], 'L0_ffn_router': _L0_ffn_in['router'], 'L0_ffn_w_up_s': _L0_ffn_in['w_up_s'], 'L0_ffn_w_gate_s': _L0_ffn_in['w_gate_s'], 'L0_ffn_w_down_s': _L0_ffn_in['w_down_s'], 'L1_attn_in_proj_w': _L1_attn_in['in_proj_w'], 'L1_attn_in_proj_b': _L1_attn_in['in_proj_b'], 'L1_attn_conv_w': _L1_attn_in['conv_w'], 'L1_attn_conv_b': _L1_attn_in['conv_b'], 'L1_attn_x_proj_w': _L1_attn_in['x_proj_w'], 'L1_attn_x_proj_b': _L1_attn_in['x_proj_b'], 'L1_attn_dt_proj_w': _L1_attn_in['dt_proj_w'], 'L1_attn_dt_proj_b': _L1_attn_in['dt_proj_b'], 'L1_attn_A_log': _L1_attn_in['A_log'], 'L1_attn_D_param': _L1_attn_in['D_param'], 'L1_attn_out_proj_w': _L1_attn_in['out_proj_w'], 'L1_attn_out_proj_b': _L1_attn_in['out_proj_b'], 'L1_attn_skip_proj_w': _L1_attn_in['skip_proj_w'], 'L1_attn_skip_proj_b': _L1_attn_in['skip_proj_b'], 'L1_ffn_clip_x': _L1_ffn_in['clip_x'], 'L1_ffn_clip_down': _L1_ffn_in['clip_down'], 'L1_ffn_w_gate': _L1_ffn_in['w_gate'], 'L1_ffn_w_up': _L1_ffn_in['w_up'], 'L1_ffn_w_down': _L1_ffn_in['w_down']}

def reference(x, txt, L0_tok_W_proj, L0_tok_b_proj, L0_tok_pos_emb, L0_attn_qkv_w, L0_attn_qkv_b, L0_attn_out_w, L0_attn_out_b, L0_ffn_up, L0_ffn_gate, L0_ffn_down, L0_ffn_router, L0_ffn_w_up_s, L0_ffn_w_gate_s, L0_ffn_w_down_s, L1_attn_in_proj_w, L1_attn_in_proj_b, L1_attn_conv_w, L1_attn_conv_b, L1_attn_x_proj_w, L1_attn_x_proj_b, L1_attn_dt_proj_w, L1_attn_dt_proj_b, L1_attn_A_log, L1_attn_D_param, L1_attn_out_proj_w, L1_attn_out_proj_b, L1_attn_skip_proj_w, L1_attn_skip_proj_b, L1_ffn_clip_x, L1_ffn_clip_down, L1_ffn_w_gate, L1_ffn_w_up, L1_ffn_w_down):
    import jax
    import jax.numpy as jnp

    def _L0_tok_ref(images, W_proj, b_proj, pos_emb):
        import jax, jax.numpy as jnp
        import numpy as np
        P = 16
        E = 256

        def patchify(images, patch_size):
            B, H, W, C = images.shape
            hp, wp = (H // patch_size, W // patch_size)
            x = images.reshape(B, hp, patch_size, wp, patch_size, C)
            x = x.transpose(0, 1, 3, 2, 4, 5)
            return x.reshape(B, hp * wp, patch_size * patch_size * C)
        patches = patchify(images, P)
        out = jnp.einsum('bnd,ed->bne', patches, W_proj) + b_proj + pos_emb[None, :, :]
        return out

    def _L0_attn_ref(x, qkv_w, qkv_b, out_w, out_b):
        import jax, jax.numpy as jnp
        import numpy as np
        B, S, D, H = (2, 512, 256, 16)
        HD = D // H
        b, s, d = x.shape
        h, hd = (H, d // H)
        scale = 1.0 / np.sqrt(hd).astype(np.float32)
        qkv = (x @ qkv_w + qkv_b).reshape(b, s, 3, h, hd)
        q, k, v = (qkv[:, :, 0], qkv[:, :, 1], qkv[:, :, 2])
        logits = jnp.einsum('bqhd,bkhd->bhqk', q, k)
        causal_mask = jnp.triu(jnp.ones((s, s), bool), 1)
        logits = jnp.where(causal_mask, -jnp.inf, logits) * scale
        att = jax.nn.softmax(logits, axis=-1)
        out = jnp.einsum('bhqk,bkhd->bqhd', att, v).reshape(b, s, d)
        return out @ out_w + out_b

    def _L0_ffn_ref(x, up, gate, down, router, w_up_s, w_gate_s, w_down_s):
        import jax, jax.numpy as jnp
        import numpy as np
        B, T, C, H, E = (1, 64, 256, 512, 8)
        STD = 0.02
        b, t, c = x.shape
        x_ = x.reshape(b * t, c)
        logits = x_ @ router.T
        idx = jnp.argmax(logits, axis=-1)
        onehot = jax.nn.one_hot(idx, router.shape[0], dtype=x.dtype)
        u = jnp.einsum('bc,ehc->ebh', x_, up)
        g = jnp.einsum('bc,ehc->ebh', x_, gate)
        h = jax.nn.silu(g) * u
        ye = jnp.einsum('ebh,ech->ebc', h, down)
        y = jnp.einsum('ebc,be->bc', ye, onehot)
        ys = jax.nn.silu(x_ @ w_gate_s.T) * (x_ @ w_up_s.T) @ w_down_s.T
        return (y + ys).reshape(b, t, c)

    def _L1_attn_ref(x, in_proj_w, in_proj_b, conv_w, conv_b, x_proj_w, x_proj_b, dt_proj_w, dt_proj_b, A_log, D_param, out_proj_w, out_proj_b, skip_proj_w, skip_proj_b):
        import jax, jax.numpy as jnp
        import numpy as np
        EMBED = 256
        DSTATE = 16
        DCONV = 4
        DTRANK = 64
        B = 2
        T = 512
        Bsz, Tlen, Dm = x.shape
        xr = x @ in_proj_w.T + in_proj_b
        x_in, res = jnp.split(xr, 2, axis=-1)
        xc = jax.lax.conv_general_dilated(x_in.transpose(0, 2, 1), conv_w, (1,), [(DCONV - 1, 0)], dimension_numbers=('NCH', 'OIH', 'NCH'), feature_group_count=Dm)
        xc = (xc + conv_b[None, :, None]).transpose(0, 2, 1)
        xc = jax.nn.silu(xc)
        ssm = xc @ x_proj_w.T + x_proj_b
        delta, Bp, Cp = jnp.split(ssm, [DTRANK, DTRANK + DSTATE], axis=-1)
        delta = jax.nn.softplus(delta @ dt_proj_w.T + dt_proj_b)
        A = -jnp.exp(A_log)
        dA = jnp.exp(delta[..., None] * A)
        dBu = delta[..., None] * Bp[:, :, None, :] * xc[..., None]

        def op(l, r):
            Ai, Bi = l
            Aj, Bj = r
            return (Aj * Ai, Bj + Aj * Bi)
        _, ys = jax.lax.associative_scan(op, (dA, dBu), axis=1)
        y = (ys * Cp[:, :, None, :]).sum(-1)
        y = y + xc * D_param
        y = y * jax.nn.silu(res)
        return y @ out_proj_w.T + out_proj_b + (x @ skip_proj_w.T + skip_proj_b)

    def _L1_ffn_ref(x, clip_x, clip_down, w_gate, w_up, w_down):
        import jax, jax.numpy as jnp
        import numpy as np
        QMAX = 127.0

        def _ste_round(v):
            return v + jax.lax.stop_gradient(jnp.round(v) - v)

        def _act_fake_quant(x, clip_factor):
            scale = jax.nn.sigmoid(clip_factor) * jnp.max(jnp.abs(x)) / QMAX
            return jnp.clip(_ste_round(x / scale), -QMAX - 1.0, QMAX) * scale

        def _weight_fake_quant(w):
            scale = jnp.max(jnp.abs(w), axis=1, keepdims=True) / QMAX
            return jnp.clip(_ste_round(w / scale), -QMAX - 1.0, QMAX) * scale
        xq = _act_fake_quant(x, clip_x[0])
        gate = jnp.einsum('bsh,ih->bsi', xq, _weight_fake_quant(w_gate))
        up = jnp.einsum('bsh,ih->bsi', xq, _weight_fake_quant(w_up))
        h = _act_fake_quant(jax.nn.silu(gate) * up, clip_down[0])
        return jnp.einsum('bsi,hi->bsh', h, _weight_fake_quant(w_down))
    h = _L0_tok_ref(x, L0_tok_W_proj, L0_tok_b_proj, L0_tok_pos_emb)
    h = jnp.concatenate([h, txt], axis=1)
    h = h + _L0_attn_ref(_layernorm(h, axis=-1), L0_attn_qkv_w, L0_attn_qkv_b, L0_attn_out_w, L0_attn_out_b)
    h = h + _L0_ffn_ref(_layernorm(h, axis=-1), L0_ffn_up, L0_ffn_gate, L0_ffn_down, L0_ffn_router, L0_ffn_w_up_s, L0_ffn_w_gate_s, L0_ffn_w_down_s)
    h = h + _L1_attn_ref(_layernorm(h, axis=-1), L1_attn_in_proj_w, L1_attn_in_proj_b, L1_attn_conv_w, L1_attn_conv_b, L1_attn_x_proj_w, L1_attn_x_proj_b, L1_attn_dt_proj_w, L1_attn_dt_proj_b, L1_attn_A_log, L1_attn_D_param, L1_attn_out_proj_w, L1_attn_out_proj_b, L1_attn_skip_proj_w, L1_attn_skip_proj_b)
    h = h + _L1_ffn_ref(_layernorm(h, axis=-1), L1_ffn_clip_x, L1_ffn_clip_down, L1_ffn_w_gate, L1_ffn_w_up, L1_ffn_w_down)
    return h

_drawn_inputs = setup_inputs


def setup_inputs(seed=0):
    import zlib

    import numpy as np

    out = dict(_drawn_inputs(seed))
    spreads = {'L0_attn_qkv_b': (0.0, 0.1),
     'L0_attn_out_b': (0.0, 0.1),
     'L1_attn_in_proj_b': (0.0, 0.8),
     'L1_attn_conv_b': (0.0, 0.8),
     'L1_attn_x_proj_b': (0.0, 0.8),
     'L1_attn_dt_proj_b': (0.0, 0.8),
     'L1_attn_D_param': (1.0, 0.6),
     'L1_attn_out_proj_b': (0.0, 0.8),
     'L1_attn_skip_proj_b': (0.0, 0.8)}
    factors = {'L0_tok_b_proj': 2.856,
     'L0_tok_pos_emb': 4.069,
     'L1_attn_in_proj_w': 8.0,
     'L1_attn_conv_w': 8.0,
     'L1_attn_x_proj_w': 8.0,
     'L1_attn_dt_proj_w': 8.0,
     'L1_attn_A_log': 8.0,
     'L1_attn_out_proj_w': 8.0,
     'L1_attn_skip_proj_w': 8.0,
     'L1_ffn_w_gate': 8.0,
     'L1_ffn_w_up': 8.0,
     'L1_ffn_w_down': 8.0}
    for name, (base, spread) in spreads.items():
        noise = np.random.default_rng([zlib.crc32(name.encode()), seed]).standard_normal(out[name].shape)
        drawn = base * np.exp(spread * noise) if base else spread * noise
        out[name] = jnp.asarray(drawn.astype(out[name].dtype))
    for name, factor in factors.items():
        out[name] = (out[name] * factor).astype(out[name].dtype)
    return out
```

```python
from contextlib import ExitStack

import numpy as np
import concourse.bass as bass
from concourse import mybir

F32 = mybir.dt.float32
BF16 = mybir.dt.bfloat16
I32 = mybir.dt.int32
ALU = mybir.AluOpType
ACT = mybir.ActivationFunctionType
AX = mybir.AxisListType

P = 128
B, IMG, TXT, D = 16, 36, 77, 256
S = IMG + TXT
T = B * S
KT = D // P
PATCH = 768
PK = PATCH // P
HEADS, HD = 16, 16
QUADS = HEADS // 4
EXPERTS, HID = 8, 512
HT = HID // P
EPS = 1e-5
LN_OPS, LN_VAR = 11, 7
WORK = 9472
NEG = -1e30
UP, GATE, DOWN, EW = 0, KT * HID, 2 * KT * HID, 2 * KT * HID + HT * D
STATES, TAPS, RANK = 16, 4, 64
GB = 2
GROUPS = B // GB
N = GB * S
CHUNKS = STATES // 2
FFN, FT, FP = 704, 8, 88
QMAX = 127.0
ROUND = 1.5 * 2.0 ** 23
S4 = S + S % 2
FG = 4
ETILE = 128
ETILES = (T + EXPERTS * (ETILE - 1)) // ETILE
SLOTS = ETILES * ETILE

C_ID, C_MQ, C_MK, C_UP = 0, 128, 128 + S, 128 + 2 * S
C_REP = C_UP + S
C_E8 = C_REP + 32
C_K128 = C_E8 + EXPERTS
NK128 = (T + ETILE - 1) // ETILE
C_TILE = C_K128 + NK128
C_RES = C_TILE + ETILES
C_RES8 = C_RES + EXPERTS * B
NCONST = C_RES8 + EXPERTS


class Seq:

    def __init__(self, eng, sem, base=0):
        self.eng, self.sem, self.base, self.n = eng, sem, base, 0

    def done(self, instruction):
        instruction.then_inc(self.sem, 1)
        self.n += 1

    def wait(self):
        self.eng.wait_ge(self.sem, self.base + self.n)

    def step(self, instruction):
        self.done(instruction)
        self.wait()


def build(nc, a, out):
    ctx = ExitStack()
    with ctx:
        def sb(name, shape, dt=F32):
            return ctx.enter_context(nc.sbuf_tensor(name, shape, dt))

        def sem(name):
            return ctx.enter_context(nc.semaphore(name))

        ps = ctx.enter_context(nc.psum_tensor("ps", [P, 8, 512], F32))

        resid = sb("resid", [S, B, D])
        const = sb("const", [P, NCONST])
        identb = sb("identb", [P, P], BF16)
        mask_q = sb("mask_q", [S, S], BF16)
        mask_k = sb("mask_k", [S, S], BF16)
        ones2 = sb("ones2", [2, P])
        ones = ones2[0:1, :]
        onesf = sb("onesf", [P, P])
        stats = sb("stats", [S, B, 6])
        lnt = sb("lnt", [S, 6, B])
        mean = sb("mean", [S, B])
        rstd = sb("rstd", [S, B])
        arena = sb("arena", [P, EXPERTS * EW])
        work = sb("work", [P, WORK])
        ident = const[:, C_ID:C_ID + P]

        def psb(bank):
            return ps[:, bank, :].bitcast(BF16)

        def view(store, at, shape, parts=P):
            n = int(np.prod(shape))
            v = store[0:parts, at:at + n]
            if len(shape) > 1:
                names = "abcd"[:len(shape)]
                v = v.rearrange(f"p ({' '.join(names)}) -> p {' '.join(names)}", **{k: s for k, s in zip(names[1:], shape[1:])})
            return v

        class Place:
            def __init__(self, store, at=0):
                self.store, self.at = store, at

            def take(self, shape, parts=P):
                v = view(self.store, self.at, shape, parts)
                self.at += int(np.prod(shape))
                assert self.at <= self.store.shape[1], self.at
                return v

        pl = Place(arena)
        patches = pl.take((PK, B * IMG))
        tok_w = pl.take((PK, D))
        tok_bias = pl.take((KT,))
        pos = pl.take((KT, IMG))
        tokT = pl.take((KT, B * IMG))
        pl = Place(work)
        qk_w = pl.take((KT, 2 * QUADS, P))
        qk_b = pl.take((2 * QUADS,))
        v_w = pl.take((KT, D))
        v_b = pl.take((D,), 1)
        o_w = pl.take((KT, D))
        o_b = pl.take((D,), 1)
        xn = pl.take((D,), S)
        xT = pl.take((KT, S))
        qT = pl.take((QUADS, S))
        kT = pl.take((QUADS, S))
        qmT = pl.take((QUADS, S))
        vh = pl.take((HEADS, HD + 1), S)
        negmax = pl.take((QUADS, 4, 32), S)
        probs = pl.take((2, 4, S), S)
        rsum = pl.take((HEADS, 1), S)
        attn = pl.take((HEADS, HD), S)
        attnT = pl.take((KT, S))
        attn_end = pl.at
        zero = view(work, WORK - D, (D,))

        sh_w = sb("sh_w", [P, EW])
        xn2 = sb("xn2", [S, B, D])
        xT2_flat = sb("xT2", [P, KT * T])
        xT2 = xT2_flat[:, :].rearrange("p (k t) -> p k t", k=KT)
        pl = Place(work)
        router_w = sb("router_w", [P, KT, EXPERTS])
        xt2 = [pl.take((D,), S) for _ in range(2)]
        xtT2 = [pl.take((KT, S)) for _ in range(2)]
        logits = pl.take((B, EXPERTS), S)
        rtop = pl.take((B, 1), S)
        rpick = pl.take((B, EXPERTS), S)
        chosen = pl.take((B, EXPERTS), S)
        prefix = pl.take((B, EXPERTS), S)
        total = pl.take((EXPERTS, B), S)
        summed = pl.take((EXPERTS, B), S)
        etiles = pl.take((EXPERTS, NK128), S)
        ecount = pl.take((EXPERTS,), S)
        esum = pl.take((EXPERTS,), S)
        ebase = pl.take((EXPERTS,), S)
        tile_ge = pl.take((ETILES, EXPERTS), S)
        tile_e = pl.take((ETILES,), S)
        slotf = pl.take((B,), S)
        s_gate = pl.take((2, 4 * S))
        s_hT = pl.take((HT, 4 * S))
        chosenb = sb("chosenb", [S, B, EXPERTS], BF16)
        upperb = sb("upperb", [S, S], BF16)
        onesb = sb("onesb", [S, S], BF16)
        slot = sb("slot", [S, B], I32)
        tile_expert = sb("tile_expert", [1, ETILES], I32)
        xg = [pl.take((D,)) for _ in range(2)]
        xgT = [pl.take((KT, ETILE)) for _ in range(2)]
        e_gate = [pl.take((HID,)) for _ in range(2)]
        e_h = [pl.take((HID,)) for _ in range(2)]
        e_hT = pl.take((HT, ETILE))
        e_y = [pl.take((D,)) for _ in range(2)]
        back = [pl.take((D,), S) for _ in range(2)]
        slots_in = nc.dram_tensor("slots_in", (SLOTS, D), F32).ap()
        slots_out = nc.dram_tensor("slots_out", (SLOTS, D), F32).ap()

        pl = Place(sh_w)
        in_w = pl.take((KT, 2 * D))
        in_b = pl.take((2 * KT,))
        conv_w = pl.take((KT, TAPS))
        conv_b = pl.take((KT,))
        rank_w = pl.take((KT, RANK))
        rank_b = pl.take((1,), RANK)
        bc_w = pl.take((KT, 96))
        bc_b = pl.take((1,), 96)
        dt_w = pl.take((D,), RANK)
        dt_b = pl.take((KT,))
        a_neg = pl.take((STATES,))
        d_par = pl.take((KT,))
        out_w = pl.take((KT, D))
        skip_w = pl.take((KT, D))
        outskip_b = pl.take((D,), 2)
        pl = Place(arena)
        conv_diag = pl.take((KT, TAPS, P))
        d_diag = pl.take((KT, P))
        pick = pl.take((32 * P // 2,), 96).bitcast(BF16).rearrange("p (j m) -> p j m", j=32)
        xn3 = [pl.take((D,), S) for _ in range(GB)]
        x3T = [pl.take((KT, N)) for _ in range(2)]
        xpad = pl.take((KT, GB, TAPS - 1 + S))
        silu_res = [pl.take((KT, N)) for _ in range(2)]
        xc = [pl.take((KT, N)) for _ in range(2)]
        rankT = pl.take((N,), RANK)
        bc = pl.take((N,), 96)
        bc_rest = pl.take((N,), 96)
        bc_hi = pl.take((N // 2,), 96).bitcast(BF16)
        bc_mid = pl.take((N // 2,), 96).bitcast(BF16)
        bc3 = [pl.take((N // 2,), 96).bitcast(BF16) for _ in range(2)]
        sp_abs = pl.take((KT, N))
        sp_relu = pl.take((KT, N))
        delta = [pl.take((KT, N)) for _ in range(2)]
        dx = [pl.take((KT, N)) for _ in range(2)]
        decay = [pl.take((2, KT * GB, S)) for _ in range(2)]
        drive = [pl.take((2, KT, N)) for _ in range(2)]
        state = [pl.take((2, KT, N)) for _ in range(2)]
        c_sb = [pl.take((2, N)) for _ in range(2)]
        read = [pl.take((2, KT, N)) for _ in range(2)]
        yT = pl.take((KT, N))

        gq = sb("gq", [P, KT, FFN], BF16)
        uq = sb("uq", [P, KT, FFN], BF16)
        dq = sb("dq", [FP, FT, D], BF16)
        wscale = sb("wscale", [P, 4, FT])
        winv = sb("winv", [P, 3, FT])
        clips = sb("clips", [P, 2])
        clip_sig = sb("clip_sig", [P, 2])
        raw_g = xn2[0:FP, 0:8, :]
        raw_u = xn2[0:FP, 8:16, :]
        raw_d = xT2_flat[:, 0:KT * FFN].rearrange("p (k i) -> p k i", k=KT)
        pl = Place(arena)
        hid = pl.take((FT, T), FP)
        f_gate = [pl.take((FG * S,), FP) for _ in range(2)]
        fmax = pl.take((FT * FG,), FP)
        amax = pl.take((1,))
        amax1 = pl.take((4,), 1)
        xscale = pl.take((2,))
        hscale = pl.take((2,))
        gscale = pl.take((FT,), FP)
        uscale = pl.take((FT,), FP)
        dscale = pl.take((D,))
        dcol = pl.take((KT,))
        diag_d = pl.take((KT, P))
        answer_f = [pl.take((D,), S) for _ in range(2)]
        xqf = pl.take((4, D), S)
        xqb = [pl.take((4 * D // 2,), S).bitcast(BF16).rearrange("p (b d) -> p b d", b=4) for _ in range(2)]
        xqT = pl.take((KT * T // 2,)).bitcast(BF16).rearrange("p (k t) -> p k t", k=KT)
        pl4 = Place(work)
        hq = pl4.take((FT * T // 2,), FP).bitcast(BF16).rearrange("p (m t) -> p m t", m=FT)
        raw_q = view(xT2_flat, KT * FFN, (FT * D,), FP).bitcast(BF16).rearrange("p (w t d) -> p w t d", w=2, t=FT)
        raw_dq = view(work, attn_end, (KT * FFN // 2,)).bitcast(BF16).rearrange("p (k i) -> p k i", k=KT)

        const_in, tok_in, txt_in, attn_in = sem("const_in"), sem("tok_in"), sem("txt_in"), sem("attn_in")
        cast_done, posb_done, pool_set = sem("cast_done"), sem("posb_done"), sem("pool_set")
        tok_ps, tokT_ready, tokback_ps, img_ready = sem("tok_ps"), sem("tokT_ready"), sem("tokback_ps"), sem("img_ready")
        stats_done, dve_ln, act_ln = sem("stats_done"), sem("dve_ln"), sem("act_ln")
        xn_ready, xnT_ps, xT_ready = sem("xn_ready"), sem("xnT_ps"), sem("xT_ready")
        qk_ps, qk_ready, v_ps, v_ready = sem("qk_ps"), sem("qk_ready"), sem("v_ps"), sem("v_ready")
        score_ps, negmax_ready, nmT_ps, qm_ready = sem("score_ps"), sem("negmax_ready"), sem("nmT_ps"), sem("qm_ready")
        scoreT_ps, probs_ready, av_ps = sem("scoreT_ps"), sem("probs_ready"), sem("av_ps")
        rsum_ready, attn_ready, attnT_ps, attnT_ready = sem("rsum_ready"), sem("attn_ready"), sem("attnT_ps"), sem("attnT_ready")
        oproj_ps, resid1_ready = sem("oproj_ps"), sem("resid1_ready")
        out_done = sem("out_done")
        moe_in, experts_in, zero_set, slots_zeroed = sem("moe_in"), sem("experts_in"), sem("zero_set"), sem("slots_zeroed")
        xn2_ready, xn2T_ps, xT2_ready, xn2_kept, xT2_kept = (sem("xn2_ready"), sem("xn2T_ps"), sem("xT2_ready"),
                                                            sem("xn2_kept"), sem("xT2_kept"))
        logits_ps, route, chosen_ready, counts_ps, slots_ready = (sem("logits_ps"), sem("route"), sem("chosen_ready"),
                                                                 sem("counts_ps"), sem("slots_ready"))
        sgate_ps, sup_ps, sgate_ready, sh_ready = sem("sgate_ps"), sem("sup_ps"), sem("sgate_ready"), sem("sh_ready")
        sdown_ps, sresid_ready = sem("sdown_ps"), sem("sresid_ready")
        scattered, xg_in, xgT_ps, xgT_ready = sem("scattered"), [sem("xg_in0"), sem("xg_in1")], sem("xgT_ps"), sem("xgT_ready")
        egate_ps, eup_ps, egate_ready, eh_ready = sem("egate_ps"), sem("eup_ps"), sem("egate_ready"), sem("eh_ready")
        ehT_ps, ehT_ready, ey_ps, ey_ready, ey_out = (sem("ehT_ps"), sem("ehT_ready"), sem("ey_ps"), sem("ey_ready"),
                                                     [sem("ey_out0"), sem("ey_out1")])
        ssm_in, aneg_done, diag_done, pick_done, pads_zero = (sem("ssm_in"), sem("aneg_done"), sem("diag_done"), sem("pick_done"),
                                                             sem("pads_zero"))
        xn3_ready, x3T_ps, x3T_ready, xin_ps, res_ps = sem("xn3_ready"), sem("x3T_ps"), sem("x3T_ready"), sem("xin_ps"), sem("res_ps")
        xpad_ready, res_ready, conv_ps, xc_ready = sem("xpad_ready"), sem("res_ready"), sem("conv_ps"), sem("xc_ready")
        proj_ps, proj_ready, dt_ps, softplus_ready = sem("proj_ps"), sem("proj_ready"), sem("dt_ps"), sem("softplus_ready")
        sp_step, bc_step, bc3_ready, delta_ready, dx_ready = (sem("sp_step"), sem("bc_step"), sem("bc3_ready"), sem("delta_ready"),
                                                              sem("dx_ready"))
        b_ps, c_ps, decay_ready, c_ready = sem("b_ps"), sem("c_ps"), sem("decay_ready"), sem("c_ready")
        drive_ready, state_ready, read_ready, read_used = sem("drive_ready"), sem("state_ready"), sem("read_ready"), sem("read_used")
        y_ps, yT_ready, ssm_ps, resid3_ready = sem("y_ps"), sem("yT_ready"), sem("ssm_ps"), sem("resid3_ready")
        ffn_in, wq_step, wq_ready, wqT_ps, wqT_ready = sem("ffn_in"), sem("wq_step"), sem("wq_ready"), sem("wqT_ps"), sem("wqT_ready")
        f_step, xn4_ready, amax_ready, amaxT_ps, scale_ready, scale_ps = (sem("f_step"), sem("xn4_ready"), sem("amax_ready"),
                                                                      sem("amaxT_ps"), sem("scale_ready"), sem("scale_ps"))
        dscale_ready, dscaleT_ps, clip_exp = sem("dscale_ready"), sem("dscaleT_ps"), sem("clip_exp")
        xq_step, xq_ready, xqT_ps, xqT_ready = sem("xq_step"), sem("xq_ready"), sem("xqT_ps"), sem("xqT_ready")
        fgate_ps, fup_ps, fgate_ready, hid_ready = sem("fgate_ps"), sem("fup_ps"), sem("fgate_ready"), sem("hid_ready")
        hmax_ready, hq_step, hq_ready, fdown_ps, fy_ready, final_ready = (sem("hmax_ready"), sem("hq_step"), sem("hq_ready"),
                                                                     sem("fdown_ps"), sem("fy_ready"), sem("final_ready"))
        gathered, resid2_ready = [sem("gathered0"), sem("gathered1")], sem("resid2_ready")

        block = ctx.enter_context(nc.Block())

        @block.sync
        def _(sp):
            sp.dma_start(tok_w, a["tok_w"]).then_inc(tok_in, 16)
            sp.dma_start(patches, a["patches"]).then_inc(tok_in, 16)
            sp.dma_start(tok_bias, a["tok_b"]).then_inc(tok_in, 16)
            sp.dma_start(pos, a["pos"]).then_inc(tok_in, 16)
            sp.dma_start(const[:, :], a["const"]).then_inc(const_in, 16)
            sp.dma_start(resid[IMG:S, :, :], a["txt"].rearrange("b s d -> s b d")).then_inc(txt_in, 16)
            for dst, name in ((qk_w, "qk_w"), (qk_b, "qk_b"), (v_w, "v_w"), (v_b, "v_b"), (o_w, "o_w"), (o_b, "o_b")):
                sp.dma_start(dst, a[name]).then_inc(attn_in, 16)
            for dst, name in ((raw_g, "f_gate"), (raw_u, "f_up"), (raw_d, "f_down")):
                sp.dma_start(dst, a[name]).then_inc(ffn_in, 16)
            for c, name in enumerate(("clip_x", "clip_h")):
                sp.dma_start(clips[:, c:c + 1], a[name].broadcast_to([P, 1])).then_inc(ffn_in, 16)
            for dst, name in ((router_w[:, :, :], "router_w"), (sh_w[:, :], "sh_w")):
                sp.dma_start(dst, a[name]).then_inc(moe_in, 16)
            sp.wait_ge(zero_set, 1)
            sp.dma_start(slots_in.rearrange("(t p) d -> p t d", p=P),
                         zero.unsqueeze(1).broadcast_to([P, ETILES, D])).then_inc(slots_zeroed, 16)
            sp.wait_ge(tokback_ps, B // 2)
            for e in range(EXPERTS):
                sp.dma_start(arena[:, e * EW:(e + 1) * EW], a["ex_w"][e]).then_inc(experts_in, 16)
            sp.wait_ge(scattered, 16 * B)

            def load_tile(j, par, first):
                if not first:
                    sp.wait_ge(xgT_ps, j - 1)
                sp.dma_start(xg[par], slots_in[bass.ds(j * ETILE, ETILE), :]).then_inc(xg_in[par], 16)

            def store_tile(j, par):
                sp.wait_ge(ey_ready, j + 2)
                sp.dma_start(slots_out[bass.ds(j * ETILE, ETILE), :], e_y[par]).then_inc(ey_out[par], 16)

            load_tile(0, 0, True)
            load_tile(1, 1, True)
            with sp.Fori(0, (ETILES - 2) // 2) as i:
                j = 2 * i
                for par in range(2):
                    load_tile(j + par + 2, par, False)
                    store_tile(j + par, par)
            for j in (ETILES - 2, ETILES - 1):
                store_tile(j, j % 2)
            sp.wait_ge(sdown_ps, 8)
            for dst, name in ((in_w, "in_w"), (in_b, "in_b"), (conv_w, "conv_w"), (conv_b, "conv_b"), (rank_w, "rank_w"),
                              (rank_b, "rank_b"), (bc_w, "bc_w"), (bc_b, "bc_b"), (dt_w, "dt_w"), (dt_b, "dt_b"),
                              (d_par, "d_par"), (out_w, "out_w"), (skip_w, "skip_w"), (outskip_b, "outskip_b")):
                sp.dma_start(dst, a[name]).then_inc(ssm_in, 16)
            sp.dma_start(a_neg, a["a_log"].broadcast_to([P, STATES])).then_inc(ssm_in, 16)
            for n in range(B // 2):
                sp.wait_ge(final_ready, 2 * n + 2)
                sp.dma_start(out[2 * n:2 * n + 2].rearrange("b s d -> s b d"), resid[:, 2 * n:2 * n + 2, :]).then_inc(out_done, 16)
            sp.wait_ge(out_done, 16 * B // 2)
        def pool_ffn(pool):
            for b in range(B):
                pool.wait_ge(fy_ready, b + 1)
                pool.tensor_tensor(resid[:, b, :], resid[:, b, :], answer_f[b % 2], ALU.add).then_inc(final_ready, 1)

        def pool_ssm(pool):
            pool.wait_ge(ey_ps, ETILES)
            pool.memset(xpad, 0.0).then_inc(pads_zero, 1)
            for d in decay:
                pool.memset(d[:, :, :, 0:1], 0.0).then_inc(pads_zero, 1)

            def split(g, par):
                pool.wait_ge(proj_ready, 4 * g + 4)
                mid, low = slice(32, 64), slice(64, 96)
                pool.tensor_tensor(bc_rest[low, :], bc[low, :], bc_hi[low, :], ALU.subtract).then_inc(bc_step, 1)
                pool.tensor_tensor(bc_mid[low, :], bc[low, :], bc_hi[low, :], ALU.subtract).then_inc(bc_step, 1)
                pool.tensor_tensor(bc3[par][mid, :], bc[mid, :], bc_hi[mid, :], ALU.subtract).then_inc(bc3_ready, 1)
                pool.wait_ge(bc_step, 2 * g + 2)
                pool.tensor_tensor(bc3[par][low, :], bc_rest[low, :], bc_mid[low, :], ALU.subtract).then_inc(bc3_ready, 1)

            def step(g, par, more=True):
                for c in range(CHUNKS):
                    k = g * CHUNKS + c
                    kp = c % 2
                    if more and c == 4:
                        pool.wait_ge(read_ready, k + 2)
                        split(g + 1, 1 - par)
                        pool.wait_ge(bc3_ready, 2 * g + 4)
                    pool.wait_ge(c_ready, k + 3)
                    pool.wait_ge(state_ready, k + 3)
                    pool.wait_ge(read_used, k + 1)
                    pool.tensor_tensor(read[kp], state[kp], c_sb[kp].unsqueeze(2).broadcast_to([P, 2, KT, N]), ALU.mult)\
                        .then_inc(read_ready, 1)

            pool.wait_ge(pads_zero, 3)
            split(0, 0)
            pool.wait_ge(bc3_ready, 2)
            step(0, 0)
            with pool.Fori(0, (GROUPS - 2) // 2) as i:
                for half in range(2):
                    step(2 * i + 1 + half, 1 - half)
            step(GROUPS - 1, 1, more=False)

        @block.gpsimd
        def _(pool):
            pool.memset(zero, 0.0).then_inc(zero_set, 1)
            pool.memset(onesf[:, :], 1.0).then_inc(pool_set, 1)
            pool.memset(ones2[:, :], 1.0).then_inc(pool_set, 1)
            pool.memset(negmax, 0.0).then_inc(pool_set, 1)
            pool.memset(vh, 1.0).then_inc(pool_set, 1)

            with pool.Fori(0, B // 2) as i:
                b = 2 * i
                for par in range(2):
                    pool.wait_ge(xn2_ready, b + par + 1)
                    pool.tensor_copy(xn2[:, b + par, :], xt2[par]).then_inc(xn2_kept, 1)
                    pool.wait_ge(xT2_ready, b + par + 1)
                    pool.tensor_copy(xT2[:, :, bass.ds((b + par) * S, S)], xtT2[par]).then_inc(xT2_kept, 1)
            pool.wait_ge(slots_zeroed, 16)
            pool.wait_ge(slots_ready, 1)
            pool.wait_ge(xn2_kept, B)
            for b in range(B):
                pool.indirect_dma_start(slots_in, bass.IndirectOffsetOnAxis(ap=slot[:, b:b + 1], axis=0), xn2[:, b, :], None).then_inc(scattered, 16)
            for par in range(2):
                pool.wait_ge(ey_out[par], 16 * (ETILES // 2))
            for b in range(B):
                if b >= 2:
                    pool.wait_ge(resid2_ready, b - 1)
                pool.indirect_dma_start(back[b % 2], None, slots_out,
                                        bass.IndirectOffsetOnAxis(ap=slot[:, b:b + 1], axis=0)).then_inc(gathered[b % 2], 16)
            pool_ssm(pool)
            pool_ffn(pool)

        def act_rstd(act, turn):
            act.wait_ge(dve_ln, LN_OPS * turn + LN_VAR)
            act.activation(lnt[:, 3, :], lnt[:, 2, :], ACT.Ln).then_inc(act_ln, 1)
            act.wait_ge(act_ln, 2 * turn + 1)
            act.activation(lnt[:, 3, :], lnt[:, 3, :], ACT.Exp, scale=-0.5).then_inc(act_ln, 1)

        def act_attention(act):
            def front_x(b):
                act.wait_ge(xnT_ps, b + 1)
                act.activation(xT, ps[:, 0, 0:KT * S].rearrange("p (k s) -> p k s", k=KT), ACT.Copy).then_inc(xT_ready, 1)

            def front_v(b):
                act.wait_ge(v_ps, b + 1)
                act.activation(vh[:, :, 0:HD], ps[0:S, 0, 0:D].rearrange("p (h e) -> p h e", h=HEADS), ACT.Copy).then_inc(v_ready, 1)

            def exps(b, rows):
                for r in rows:
                    act.wait_ge(scoreT_ps, 2 * b + r // 2 + 1)
                    if r >= 2:
                        act.wait_ge(av_ps, 4 * b + r - 1)
                    act.activation(probs[:, r % 2], ps[0:S, 3 + r, 0:QUADS * S].rearrange("p (j s) -> p j s", j=QUADS),
                                   ACT.Exp, scale=1.0 / float(HD) ** 0.5).then_inc(probs_ready, 1)

            def back(b):
                act.wait_ge(attnT_ps, b + 1)
                act.activation(attnT, ps[:, 7, 0:KT * S].rearrange("p (k s) -> p k s", k=KT), ACT.Copy).then_inc(attnT_ready, 1)

            act.wait_ge(pool_set, 4)
            front_x(0)
            front_v(0)

            def step(b, more=True):
                exps(b, (0, 1))
                if more:
                    front_x(b + 1)
                exps(b, (2, 3))
                if more:
                    front_v(b + 1)
                back(b)

            with act.Fori(0, B - 1) as b:
                step(b)
            step(B - 1, more=False)

        def act_tokens(act):
            for pair in range(B // 2):
                act.wait_ge(tokback_ps, pair + 1)
                act.activation(resid[0:IMG, 2 * pair:2 * pair + 2, :],
                               ps[0:IMG, 4 + pair % 4, :].rearrange("p (b d) -> p b d", b=2), ACT.Copy).then_inc(img_ready, 1)

        def act_router(act):
            with act.Fori(0, B // 2) as i:
                b = 2 * i
                for par in range(2):
                    act.wait_ge(xn2T_ps, b + par + 1)
                    act.wait_ge(xT2_kept, b + par + 1)
                    act.activation(xtT2[par], ps[:, par, 0:KT * S].rearrange("p (k s) -> p k s", k=KT), ACT.Copy).then_inc(xT2_ready, 1)

        def act_shared(act):
            with act.Fori(0, (4 * HT) // 2) as i:
                n = 2 * i
                for par in range(2):
                    act.wait_ge(sgate_ps, n + par + 1)
                    act.wait_ge(sh_ready, n + par + 1)
                    act.activation(s_gate[:, par, :], ps[:, 3 + 2 * par, 0:4 * S], ACT.Silu).then_inc(sgate_ready, 1)

        def act_experts(act):
            def turn(j, par):
                act.wait_ge(xgT_ps, j + 1)
                act.activation(xgT[par], ps[:, 0, 0:KT * ETILE].rearrange("p (k s) -> p k s", k=KT), ACT.Copy).then_inc(xgT_ready, 1)

            def gate(j, par):
                act.wait_ge(egate_ps, j + 1)
                act.activation(e_gate[par], ps[:, 1 + 2 * par, :], ACT.Silu).then_inc(egate_ready, 1)

            def hidden(j):
                act.wait_ge(ehT_ps, j + 1)
                act.activation(e_hT, ps[:, 5, :].rearrange("p (m s) -> p m s", m=HT), ACT.Copy).then_inc(ehT_ready, 1)

            act.wait_ge(xgT_ps, 1)
            act.activation(xgT[0], ps[:, 0, 0:KT * ETILE].rearrange("p (k s) -> p k s", k=KT), ACT.Copy).then_inc(xgT_ready, 1)
            act.wait_ge(xgT_ps, 2)
            act.activation(xgT[1], ps[:, 0, 0:KT * ETILE].rearrange("p (k s) -> p k s", k=KT), ACT.Copy).then_inc(xgT_ready, 1)
            gate(0, 0)
            with act.Fori(0, (ETILES - 2) // 2) as i:
                j = 2 * i
                for par in range(2):
                    gate(j + par + 1, 1 - par)
                    hidden(j + par)
                    turn(j + par + 2, par)
            gate(ETILES - 1, 1)
            hidden(ETILES - 2)
            hidden(ETILES - 1)

        def act_weights(act):
            act.wait_ge(ffn_in, 5 * 16)
            act.activation(clip_sig[:, :], clips[:, :], ACT.Exp, scale=-1.0).then_inc(clip_exp, 1)
            for n, dst in enumerate((gq, uq)):
                for k in range(KT):
                    act.wait_ge(wqT_ps, 2 * n + k + 1)
                    act.activation(dst[:, k, :], psb(2 * n + k)[:, 0:FFN], ACT.Copy).then_inc(wqT_ready, 1)
            for q in range(2):
                act.wait_ge(wqT_ps, 5 + q)
                act.activation(dq[:, 4 * q:4 * q + 4, :], psb(4 + q)[0:FP, :].rearrange("p (m d) -> p m d", m=4), ACT.Copy).then_inc(wqT_ready, 1)

        def act_ffn(act):
            for g in range(FG):
                for k in range(KT):
                    act.wait_ge(xqT_ps, KT * g + k + 1)
                    act.activation(xqT[:, k, g * 4 * S:(g + 1) * 4 * S].rearrange("p (b s) -> p b s", b=4),
                                   psb(k)[:, 0:4 * S4].rearrange("p (b s) -> p b s", b=4)[:, :, 0:S], ACT.Copy).then_inc(xqT_ready, 1)
            with act.Fori(0, FG) as g:
                for m in range(FT):
                    par = m % 2
                    act.wait_ge(fgate_ps, g * FT + m + 1)
                    act.wait_ge(hid_ready, g * FT + m + 1)
                    act.activation(f_gate[par], ps[0:FP, 2 + 2 * par, 0:4 * S], ACT.Silu, scale=gscale[:, m:m + 1]).then_inc(fgate_ready, 1)

        def act_ssm(act):
            act.wait_ge(ssm_in, 16 * 15)
            act.activation(a_neg, a_neg, ACT.Exp).then_inc(aneg_done, 1)

            def turn(g, par):
                act.wait_ge(x3T_ps, g + 1)
                act.activation(x3T[par], ps[:, 0, 0:KT * N].rearrange("p (k s) -> p k s", k=KT), ACT.Copy).then_inc(x3T_ready, 1)

            def pad(g):
                act.wait_ge(xin_ps, g + 1)
                for m in range(KT):
                    act.activation(xpad[:, m, :, TAPS - 1:], ps[:, 1, m * N:(m + 1) * N].rearrange("p (b s) -> p b s", b=GB),
                                   ACT.Identity, bias=in_b[:, m:m + 1]).then_inc(xpad_ready, 1)

            def silus(g, par, first=False):
                act.wait_ge(res_ps, g + 1)
                act.wait_ge(conv_ps, g + 1)
                if not first:
                    act.wait_ge(yT_ready, g)
                for m in range(KT):
                    act.activation(silu_res[par][:, m, :], ps[:, 0, m * N:(m + 1) * N], ACT.Silu, bias=in_b[:, KT + m:KT + m + 1])\
                        .then_inc(res_ready, 1)
                for m in range(KT):
                    act.activation(xc[par][:, m, :], ps[:, 1, m * N:(m + 1) * N], ACT.Silu, bias=conv_b[:, m:m + 1])\
                        .then_inc(xc_ready, 1)

            def projections(g, par):
                act.wait_ge(proj_ps, g + 1)
                act.activation(rankT, ps[0:RANK, 0, 0:N], ACT.Identity, bias=rank_b).then_inc(proj_ready, 1)
                for dst, rows in ((bc, 96), (bc_hi, 96), (bc3[par], 32)):
                    act.activation(dst[0:rows, :], ps[0:rows, 0, N:2 * N], ACT.Identity, bias=bc_b[0:rows, :]).then_inc(proj_ready, 1)

            def softplus(g):
                q = Seq(act, sp_step, 5 * g)
                act.wait_ge(dt_ps, g + 1)
                for m in range(KT):
                    q.done(act.activation(sp_abs[:, m, :], ps[:, 1, m * N:(m + 1) * N], ACT.Abs, bias=dt_b[:, m:m + 1]))
                for m in range(KT):
                    q.done(act.activation(sp_relu[:, m, :], ps[:, 1, m * N:(m + 1) * N], ACT.Relu, bias=dt_b[:, m:m + 1]))
                q.wait()
                q.step(act.activation(sp_abs, sp_abs, ACT.Exp, scale=-1.0))
                act.activation(sp_abs, sp_abs, ACT.Ln, bias=1.0).then_inc(softplus_ready, 1)

            def step(g, par, more=True):
                for c in range(CHUNKS):
                    k = g * CHUNKS + c
                    kp = c % 2
                    if c == 0:
                        act.wait_ge(delta_ready, g + 1)
                    act.wait_ge(state_ready, k + 1)
                    for n in range(2):
                        act.activation(decay[kp][:, n, :, 1:], delta[par].rearrange("p k (b s) -> p (k b) s", b=GB)[:, :, 1:],
                                       ACT.Exp, scale=a_neg[:, 2 * c + n:2 * c + n + 1]).then_inc(decay_ready, 1)
                    act.wait_ge(c_ps, k + 1)
                    act.wait_ge(read_ready, k + 1)
                    act.activation(c_sb[kp], ps[:, 4 + kp, 0:2 * N].rearrange("p (n s) -> p n s", n=2), ACT.Copy).then_inc(c_ready, 1)
                    if more:
                        if c == 0:
                            turn(g + 1, 1 - par)
                        if c == 1:
                            pad(g + 1)
                        if c == 2:
                            silus(g + 1, 1 - par)
                        if c == 3:
                            projections(g + 1, 1 - par)
                        if c == 4:
                            softplus(g + 1)

            act.wait_ge(pads_zero, 3)
            turn(0, 0)
            pad(0)
            silus(0, 0, first=True)
            projections(0, 0)
            softplus(0)
            act.wait_ge(aneg_done, 2)
            step(0, 0)
            with act.Fori(0, (GROUPS - 2) // 2) as i:
                for half in range(2):
                    step(2 * i + 1 + half, 1 - half)
            step(GROUPS - 1, 1, more=False)

        @block.scalar
        def _(act):
            act_tokens(act)
            act_rstd(act, 0)
            act_weights(act)
            act_attention(act)
            act_rstd(act, 1)
            act_router(act)
            act_shared(act)
            act_experts(act)
            act_rstd(act, 2)
            act_ssm(act)
            act_rstd(act, 3)
            act_ffn(act)


        def dve_layernorm(dve, turn):
            q = Seq(dve, dve_ln, LN_OPS * turn)
            me, qe, mo, qo = (stats[:, :, k] for k in (1, 2, 4, 5))
            q.done(dve.tensor_tensor(lnt[:, 0, :], me, mo, ALU.add))
            q.done(dve.tensor_tensor(lnt[:, 1, :], me, mo, ALU.subtract))
            q.done(dve.tensor_tensor(lnt[:, 2, :], qe, qo, ALU.add))
            q.wait()
            q.done(dve.tensor_scalar(mean[:, :], lnt[:, 0, :], 0.5, None, ALU.mult))
            q.done(dve.tensor_scalar(lnt[:, 2, :], lnt[:, 2, :], 1.0 / D, EPS, ALU.mult, ALU.add))
            q.step(dve.tensor_tensor(lnt[:, 1, :], lnt[:, 1, :], lnt[:, 1, :], ALU.mult))
            q.step(dve.scalar_tensor_tensor(out=lnt[:, 2, :], in0=lnt[:, 1, :], scalar=0.25, in1=lnt[:, 2, :], op0=ALU.mult, op1=ALU.add))
            assert q.n == LN_VAR
            dve.wait_ge(act_ln, 2 * turn + 2)
            y, v, t = lnt[:, 3, :], lnt[:, 2, :], lnt[:, 4, :]
            q.step(dve.tensor_tensor(t, y, y, ALU.mult))
            q.step(dve.tensor_tensor(t, t, v, ALU.mult))
            q.step(dve.tensor_scalar(t, t, -0.5, 1.5, ALU.mult, ALU.add))
            q.step(dve.tensor_tensor(rstd[:, :], y, t, ALU.mult))
            assert q.n == LN_OPS

        def dve_tokens(dve):
            dve.wait_ge(const_in, 16)
            dve.tensor_copy(identb[:, :], ident).then_inc(cast_done, 1)
            for m, c in ((mask_q, C_MQ), (mask_k, C_MK)):
                dve.tensor_copy(m[:, :], const[0:S, c:c + S]).then_inc(cast_done, 1)
            dve.tensor_copy(upperb[:, :], const[0:S, C_UP:C_UP + S]).then_inc(cast_done, 1)
            dve.memset(onesb[:, :], 1.0).then_inc(cast_done, 1)
            dve.wait_ge(tok_in, 64)
            for m in range(KT):
                dve.tensor_scalar(pos[:, m, :], pos[:, m, :], tok_bias[:, m:m + 1], None, ALU.add).then_inc(posb_done, 1)
            dve.wait_ge(posb_done, KT)
            for m in range(KT):
                for c in range(2):
                    dve.wait_ge(tok_ps, 2 * m + c + 1)
                    h = B // 2 * IMG
                    dve.tensor_tensor(tokT[:, m, c * h:(c + 1) * h].rearrange("p (b n) -> p b n", n=IMG),
                                      ps[:, 2 * m + c, 0:h].rearrange("p (b n) -> p b n", n=IMG),
                                      pos[:, m, :].unsqueeze(1).broadcast_to([P, B // 2, IMG]), ALU.add).then_inc(tokT_ready, 1)
            dve.wait_ge(txt_in, 16)
            dve.wait_ge(img_ready, B // 2)
            with dve.Fori(0, B) as b:
                dve.bn_stats(stats[:, b, :], resid[:, b, :]).then_inc(stats_done, 1)
            dve.wait_ge(stats_done, B)

        def dve_attention(dve):
            def normalise(b):
                dve.tensor_scalar(xn, resid[:, b, :], mean[:, bass.ds(b, 1)], rstd[:, bass.ds(b, 1)], ALU.subtract, ALU.mult).then_inc(xn_ready, 1)

            def take_qk(b):
                dve.wait_ge(qk_ps, b + 1)
                for bank, dst, c in ((1, qT, 0), (2, kT, QUADS)):
                    dve.tensor_tensor(dst, ps[:, bank, 0:4 * S].rearrange("p (t s) -> p t s", t=QUADS),
                                      qk_b[:, c:c + QUADS].unsqueeze(2).broadcast_to([P, QUADS, S]), ALU.add).then_inc(qk_ready, 1)

            def maxima(b, half):
                dve.wait_ge(score_ps, 2 * b + half + 1)
                for r in (2 * half, 2 * half + 1):
                    dve.tensor_reduce(negmax[:, :, r, HD:HD + 1], ps[0:S, 3 + r, 0:QUADS * S].rearrange("p (j s) -> p j s", j=QUADS),
                                      AX.X, ALU.max, negate=True).then_inc(negmax_ready, 1)

            def take_qm(b):
                dve.wait_ge(nmT_ps, b + 1)
                dve.tensor_tensor(qmT, ps[:, 1, 0:4 * S].rearrange("p (t s) -> p t s", t=QUADS), qT, ALU.add).then_inc(qm_ready, 1)

            def weigh(b):
                dve.wait_ge(av_ps, QUADS * b + QUADS)
                o = ps[0:S, 7, 0:HEADS * (HD + 1)].rearrange("p (h e) -> p h e", h=HEADS)
                dve.reciprocal(rsum, o[:, :, HD:HD + 1]).then_inc(rsum_ready, 1)
                dve.wait_ge(rsum_ready, b + 1)
                dve.tensor_tensor(attn, o[:, :, 0:HD], rsum.broadcast_to([S, HEADS, HD]), ALU.mult).then_inc(attn_ready, 1)

            def add_resid(b):
                dve.wait_ge(oproj_ps, b + 1)
                dve.tensor_tensor(resid[:, b, :], ps[0:S, 7, 0:D], resid[:, b, :], ALU.add).then_inc(resid1_ready, 1)
                dve.wait_ge(resid1_ready, b + 2)
                dve.bn_stats(stats[:, b, :], resid[:, b, :]).then_inc(stats_done, 1)

            dve.wait_ge(attn_in, 6 * 16)
            normalise(0)
            take_qk(0)
            maxima(0, 0)
            maxima(0, 1)
            take_qm(0)

            def step(b, more=True):
                if more:
                    normalise(b + 1)
                weigh(b)
                if more:
                    take_qk(b + 1)
                    maxima(b + 1, 0)
                add_resid(b)
                if more:
                    maxima(b + 1, 1)
                    take_qm(b + 1)

            with dve.Fori(0, B - 1) as b:
                step(b)
            step(B - 1, more=False)

        def dve_router(dve):
            dve.wait_ge(stats_done, 2 * B)
            dve_layernorm(dve, 1)
            for n, counted in enumerate((xT2_kept, xT2_kept, sh_ready, sh_ready, sresid_ready, sresid_ready, ey_ready)):
                dve.memset(lnt[:, 5, n:n + 1], 0.0).then_inc(counted, 1)
            with dve.Fori(0, B // 2) as i:
                b = 2 * i
                for par in range(2):
                    dve.wait_ge(xT2_kept, b + par + 1)
                    dve.tensor_scalar(xt2[par], resid[:, b + par, :], mean[:, bass.ds(b + par, 1)], rstd[:, bass.ds(b + par, 1)],
                                      ALU.subtract, ALU.mult).then_inc(xn2_ready, 1)
            dve.wait_ge(logits_ps, B)
            q = Seq(dve, route)
            q.step(dve.tensor_copy(logits, ps[0:S, 2, 0:B * EXPERTS].rearrange("p (b e) -> p b e", b=B)))
            q.step(dve.tensor_reduce(rtop, logits, AX.X, ALU.max))
            q.step(dve.tensor_tensor(rpick, logits, rtop.broadcast_to([S, B, EXPERTS]), ALU.is_equal))
            e8 = const[0:S, C_E8:C_E8 + EXPERTS].unsqueeze(1).broadcast_to([S, B, EXPERTS])
            q.step(dve.tensor_tensor(rpick, rpick, e8, ALU.mult))
            q.step(dve.tensor_reduce(rtop, rpick, AX.X, ALU.min))
            q.step(dve.tensor_tensor(chosen, rtop.broadcast_to([S, B, EXPERTS]), e8, ALU.is_equal))
            dve.tensor_copy(chosenb[:, :, :], chosen).then_inc(chosen_ready, 1)
            dve.wait_ge(counts_ps, 2)
            q.done(dve.tensor_copy(prefix, ps[0:S, 2, 0:B * EXPERTS].rearrange("p (b e) -> p b e", b=B)))
            q.step(dve.tensor_copy(total, ps[0:S, 7, 0:B * EXPERTS].rearrange("p (b e) -> p e b", b=B)))
            q.step(dve.tensor_tensor_scan(summed.rearrange("p e b -> p (e b)"), const[0:S, C_RES:C_RES + EXPERTS * B],
                                          total.rearrange("p e b -> p (e b)"), 0.0, ALU.mult, ALU.add))
            q.step(dve.tensor_tensor(etiles, summed[:, :, B - 1:B].broadcast_to([S, EXPERTS, NK128]),
                                     const[0:S, C_K128:C_K128 + NK128].unsqueeze(1).broadcast_to([S, EXPERTS, NK128]), ALU.is_gt))
            q.step(dve.tensor_reduce(ecount, etiles, AX.X, ALU.add))
            q.step(dve.tensor_tensor_scan(esum, const[0:S, C_RES8:C_RES8 + EXPERTS], ecount, 0.0, ALU.mult, ALU.add))
            q.done(dve.tensor_tensor(ebase, esum, ecount, ALU.subtract))
            q.done(dve.tensor_tensor(summed, summed, total, ALU.subtract))
            q.step(dve.tensor_tensor(tile_ge, const[0:S, C_TILE:C_TILE + ETILES].unsqueeze(2).broadcast_to([S, ETILES, EXPERTS]),
                                     esum.unsqueeze(1).broadcast_to([S, ETILES, EXPERTS]), ALU.is_ge))
            q.step(dve.tensor_reduce(tile_e, tile_ge, AX.X, ALU.add))
            q.done(dve.tensor_scalar(tile_expert[:, :], tile_e[0:1, :], float(EXPERTS - 1), None, ALU.min))
            q.step(dve.scalar_tensor_tensor(out=summed, in0=ebase.unsqueeze(2).broadcast_to([S, EXPERTS, B]), scalar=float(ETILE),
                                            in1=summed, op0=ALU.mult, op1=ALU.add))
            q.step(dve.tensor_tensor(prefix, prefix, summed.rearrange("p e b -> p b e"), ALU.add))
            q.step(dve.tensor_tensor(prefix, prefix, chosen, ALU.mult))
            q.step(dve.tensor_reduce(slotf, prefix, AX.X, ALU.add))
            dve.tensor_copy(slot[:, :], slotf).then_inc(slots_ready, 1)

        def dve_shared(dve):
            with dve.Fori(0, 4) as g:
                for m in range(HT):
                    par = m % 2
                    dve.wait_ge(sgate_ready, g * HT + m + 1)
                    dve.wait_ge(sup_ps, g * HT + m + 1)
                    dve.tensor_tensor(s_hT[:, m, :], ps[:, 4 + 2 * par, 0:4 * S], s_gate[:, par, :], ALU.mult).then_inc(sh_ready, 1)
                for pair in range(2):
                    dve.wait_ge(sdown_ps, 2 * g + pair + 1)
                    r = resid[:, bass.ds(4 * g + 2 * pair, 2), :]
                    dve.tensor_tensor(r, ps[0:S, pair, :].rearrange("p (b d) -> p b d", b=2), r, ALU.add).then_inc(sresid_ready, 1)

        def dve_experts(dve):
            def hidden(j, par):
                dve.wait_ge(egate_ready, j + 1)
                dve.wait_ge(eup_ps, j + 1)
                dve.tensor_tensor(e_h[par], ps[:, 2 + 2 * par, :], e_gate[par], ALU.mult).then_inc(eh_ready, 1)

            def answer(j, par):
                dve.wait_ge(ey_ps, j + 1)
                dve.tensor_copy(e_y[par], ps[:, 6, 0:D]).then_inc(ey_ready, 1)

            hidden(0, 0)
            hidden(1, 1)
            answer(0, 0)
            hidden(2, 0)
            answer(1, 1)
            with dve.Fori(1, (ETILES - 2) // 2) as i:
                j = 2 * i
                for par in range(2):
                    hidden(j + par + 1, 1 - par)
                    dve.wait_ge(ey_out[par], 8 * j)
                    answer(j + par, par)
            hidden(ETILES - 1, 1)
            dve.wait_ge(ey_out[0], 8 * (ETILES - 2))
            answer(ETILES - 2, 0)
            dve.wait_ge(ey_out[1], 8 * (ETILES - 2))
            answer(ETILES - 1, 1)
            for b in range(B):
                dve.wait_ge(gathered[b % 2], 16 * (b // 2 + 1))
                dve.tensor_tensor(resid[:, b, :], resid[:, b, :], back[b % 2], ALU.add).then_inc(resid2_ready, 1)

        def dve_weights(dve):
            dve.wait_ge(ffn_in, 5 * 16)
            q = Seq(dve, wq_step)
            raws = ((raw_g, FP, FT, D, raw_q[:, 0]), (raw_u, FP, FT, D, raw_q[:, 1]), (raw_d, P, KT, FFN, raw_dq))
            for n, (raw, parts, rows, width, _) in enumerate(raws):
                q.done(dve.tensor_reduce(wscale[0:parts, n, 0:rows], raw, AX.X, ALU.max, apply_absolute_value=True))
            q.wait()
            for n, (raw, parts, rows, width, _) in enumerate(raws):
                w = wscale[0:parts, n, 0:rows]
                q.step(dve.tensor_scalar(w, w, 1.0 / QMAX, None, ALU.mult))
                q.step(dve.reciprocal(winv[0:parts, n, 0:rows], w))
                q.step(dve.tensor_tensor(raw, raw, winv[0:parts, n, 0:rows].unsqueeze(2).broadcast_to([parts, rows, width]), ALU.mult))
            for raw, parts, rows, width, dst in raws:
                dve.tensor_scalar(dst, raw, ROUND, ROUND, ALU.add, ALU.subtract).then_inc(wq_ready, 1)
            dve.wait_ge(clip_exp, 1)
            q.step(dve.tensor_scalar(clip_sig[:, :], clip_sig[:, :], 1.0, QMAX, ALU.add, ALU.mult))
            q.step(dve.reciprocal(clip_sig[:, :], clip_sig[:, :]))

        def dve_ffn(dve):
            dve.wait_ge(stats_done, 4 * B)
            dve_layernorm(dve, 3)
            with dve.Fori(0, B) as b:
                dve.tensor_scalar(xn2[:, b, :], resid[:, b, :], mean[:, bass.ds(b, 1)], rstd[:, bass.ds(b, 1)],
                                  ALU.subtract, ALU.mult).then_inc(xn4_ready, 1)
            dve.wait_ge(xn4_ready, B)
            q = Seq(dve, f_step)

            def scales(turn, source, parts, dst):
                dve.tensor_reduce(amax[0:parts, :], source, AX.X, ALU.max, apply_absolute_value=True).then_inc(amax_ready, 1)
                dve.wait_ge(amaxT_ps, turn + 1)
                q.step(dve.tensor_reduce(amax1[:, 0:1], ps[0:1, 7, 0:parts], AX.X, ALU.max))
                q.step(dve.tensor_scalar(amax1[:, 1:2], amax1[:, 0:1], clip_sig[0:1, turn:turn + 1], None, ALU.mult))
                dve.reciprocal(amax1[:, 2:3], amax1[:, 1:2]).then_inc(scale_ready, 1)
                dve.wait_ge(scale_ps, turn + 1)
                q.step(dve.tensor_copy(dst, ps[:, 7, 0:2]))

            scales(0, xn2[:, :, :].rearrange("p b d -> p (b d)"), S, xscale)
            q.done(dve.tensor_scalar(gscale, wscale[0:FP, 0, :], xscale[0:FP, 0:1], None, ALU.mult))
            q.done(dve.tensor_scalar(uscale, wscale[0:FP, 1, :], xscale[0:FP, 0:1], None, ALU.mult))
            q.wait()
            x = Seq(dve, xq_step)
            for g in range(FG):
                src = xn2[:, 4 * g:4 * g + 4, :]
                if g > 0:
                    dve.wait_ge(xq_ready, g)
                x.step(dve.tensor_scalar(xqf, src, xscale[0:S, 1:2], ROUND, ALU.mult, ALU.add))
                x.step(dve.tensor_scalar(xqf, xqf, ROUND, QMAX, ALU.subtract, ALU.min))
                if g >= 2:
                    dve.wait_ge(xqT_ps, KT * (g - 1))
                dve.tensor_scalar(xqb[g % 2], xqf, -QMAX - 1.0, None, ALU.max).then_inc(xq_ready, 1)
            dve.sem_inc(hid_ready, 2)
            with dve.Fori(0, FG) as g:
                for m in range(FT):
                    par = m % 2
                    dve.wait_ge(fgate_ready, g * FT + m + 1)
                    dve.wait_ge(fup_ps, g * FT + m + 1)
                    h = hid[:, m, bass.ds(g * 4 * S, 4 * S)]
                    dve.scalar_tensor_tensor(out=h, in0=ps[0:FP, 3 + 2 * par, 0:4 * S], scalar=uscale[:, m:m + 1], in1=f_gate[par],
                                             op0=ALU.mult, op1=ALU.mult).then_inc(hid_ready, 1)
                    dve.wait_ge(hid_ready, g * FT + m + 3)
                    dve.tensor_reduce(fmax[:, bass.ds(g * FT + m, 1)], h, AX.X, ALU.max, apply_absolute_value=True).then_inc(hmax_ready, 1)
            dve.wait_ge(hmax_ready, FG * FT)
            scales(1, fmax, FP, hscale)
            q.step(dve.tensor_scalar(dcol, wscale[:, 2, 0:KT], hscale[:, 0:1], None, ALU.mult))
            for k in range(KT):
                dve.tensor_scalar(diag_d[:, k, :], ident, dcol[:, k:k + 1], None, ALU.mult).then_inc(dscale_ready, 1)
            dve.wait_ge(dscaleT_ps, 1)
            q.step(dve.tensor_copy(dscale, ps[:, 6, 0:D]))
            hs = Seq(dve, hq_step)
            for g in range(FG):
                cols = slice(g * 4 * S, (g + 1) * 4 * S)
                h = hid[:, :, cols]
                hs.step(dve.tensor_scalar(h, h, hscale[0:FP, 1:2], ROUND, ALU.mult, ALU.add))
                hs.step(dve.tensor_scalar(h, h, ROUND, QMAX, ALU.subtract, ALU.min))
                dve.tensor_scalar(hq[:, :, cols], h, -QMAX - 1.0, None, ALU.max).then_inc(hq_ready, 1)
            for b in range(B):
                dve.wait_ge(fdown_ps, b + 1)
                if b >= 2:
                    dve.wait_ge(final_ready, b - 1)
                dve.tensor_tensor(answer_f[b % 2], ps[0:S, b % 4, 0:D], dscale[0:S, :], ALU.mult).then_inc(fy_ready, 1)

        def dve_ssm(dve):
            for b in range(B):
                dve.wait_ge(resid2_ready, b + 1)
                dve.bn_stats(stats[:, b, :], resid[:, b, :]).then_inc(stats_done, 1)
            dve.wait_ge(stats_done, 3 * B)
            dve_layernorm(dve, 2)
            dve.wait_ge(ssm_in, 16 * 15)
            dve.wait_ge(ey_ps, ETILES)
            dve.wait_ge(aneg_done, 1)
            dve.tensor_scalar(a_neg, a_neg, -1.0, None, ALU.mult).then_inc(aneg_done, 1)
            for m in range(KT):
                for t in range(TAPS):
                    dve.tensor_scalar(conv_diag[:, m, t, :], ident, conv_w[:, m, t:t + 1], None, ALU.mult).then_inc(diag_done, 1)
                dve.tensor_scalar(d_diag[:, m, :], ident, d_par[:, m:m + 1], None, ALU.mult).then_inc(diag_done, 1)
            dve.tensor_copy(pick, const[0:96, C_REP:C_REP + 32].unsqueeze(2).broadcast_to([96, 32, P])).then_inc(pick_done, 1)
            for counted in (state_ready, read_ready, read_used, c_ready, drive_ready):
                dve.sem_inc(counted, 2)
            dve.sem_inc(yT_ready, 1)

            def normalise(g):
                for r in range(GB):
                    b = GB * g + r
                    dve.tensor_scalar(xn3[r], resid[:, b, :], mean[:, bass.ds(b, 1)], rstd[:, bass.ds(b, 1)],
                                      ALU.subtract, ALU.mult).then_inc(xn3_ready, 1)

            def steps(g, par):
                dve.wait_ge(softplus_ready, g + 1)
                dve.wait_ge(xc_ready, KT * g + KT)
                dve.tensor_tensor(delta[par], sp_relu, sp_abs, ALU.add).then_inc(delta_ready, 1)
                dve.wait_ge(delta_ready, g + 1)
                dve.tensor_tensor(dx[par], delta[par], xc[par], ALU.mult).then_inc(dx_ready, 1)

            def chunk(g, c, par):
                k, kp = g * CHUNKS + c, c % 2
                dve.wait_ge(b_ps, k + 1)
                if c == 0:
                    dve.wait_ge(dx_ready, g + 1)
                dve.tensor_tensor(drive[kp], dx[par].unsqueeze(1).broadcast_to([P, 2, KT, N]),
                                  ps[:, 2 + kp, 0:2 * N].rearrange("p (n s) -> p n s", n=2).unsqueeze(2).broadcast_to([P, 2, KT, N]),
                                  ALU.mult).then_inc(drive_ready, 1)
                dve.wait_ge(drive_ready, k + 3)
                dve.wait_ge(decay_ready, 2 * k + 2)
                dve.wait_ge(read_ready, k + 1)
                dve.tensor_tensor_scan(state[kp].rearrange("p n k s -> p (n k s)"), decay[kp].rearrange("p n q s -> p (n q s)"),
                                       drive[kp].rearrange("p n k s -> p (n k s)"), 0.0, ALU.mult, ALU.add).then_inc(state_ready, 1)

            def gate(g, par):
                dve.wait_ge(y_ps, g + 1)
                dve.wait_ge(res_ready, KT * g + KT)
                dve.tensor_tensor(yT, ps[:, 6, 0:KT * N].rearrange("p (k s) -> p k s", k=KT), silu_res[par], ALU.mult).then_inc(yT_ready, 1)

            def add_resid(g):
                dve.wait_ge(ssm_ps, g + 1)
                r = resid[:, bass.ds(GB * g, GB), :]
                dve.tensor_tensor(r, ps[0:S, 7, :].rearrange("p (b d) -> p b d", b=GB), r, ALU.add).then_inc(resid3_ready, 1)
                dve.wait_ge(resid3_ready, g + 1)
                for q in range(GB):
                    dve.bn_stats(stats[:, GB * g + q, :], resid[:, GB * g + q, :]).then_inc(stats_done, 1)

            def step(g, par, more=True, before=True):
                for c in range(CHUNKS):
                    if more and c == 0:
                        normalise(g + 1)
                    chunk(g, c, par)
                    if before and c == 1:
                        gate(g - 1, 1 - par)
                    if before and c == 2:
                        add_resid(g - 1)
                    if more and c == 5:
                        steps(g + 1, 1 - par)

            normalise(0)
            steps(0, 0)
            step(0, 0, before=False)
            with dve.Fori(0, (GROUPS - 2) // 2) as i:
                for half in range(2):
                    step(2 * i + 1 + half, 1 - half)
            step(GROUPS - 1, 1, more=False)
            gate(GROUPS - 1, 1)
            add_resid(GROUPS - 1)

        @block.vector
        def _(dve):
            dve_tokens(dve)
            dve_layernorm(dve, 0)
            dve_weights(dve)
            dve.memset(rsum, 1.0).then_inc(resid1_ready, 1)
            dve_attention(dve)
            dve_router(dve)
            dve_shared(dve)
            dve_experts(dve)
            dve_ssm(dve)
            dve_ffn(dve)

        def pe_tokens(pe):
            pe.wait_ge(tok_in, 64)
            h = B // 2 * IMG
            for m in range(KT):
                for c in range(2):
                    for k in range(PK):
                        last = pe.matmul(ps[:, 2 * m + c, 0:h], tok_w[:, k, m * P:(m + 1) * P], patches[:, k, c * h:(c + 1) * h],
                                         start=k == 0, stop=k == PK - 1)
                    last.then_inc(tok_ps, 1)
            pe.wait_ge(tokT_ready, 4)
            pe.wait_ge(const_in, 16)
            for pair in range(B // 2):
                bank = 4 + pair % 4
                if pair >= 4:
                    pe.wait_ge(img_ready, pair - 3)
                for r in range(2):
                    for m in range(KT):
                        b = 2 * pair + r
                        last = pe.transpose(ps[0:IMG, bank, r * D + m * P:r * D + (m + 1) * P], tokT[:, m, b * IMG:(b + 1) * IMG], ident)
                last.then_inc(tokback_ps, 1)

        def pe_attention(pe):
            def turn_x(b, after_v=True):
                pe.wait_ge(xn_ready, b + 1)
                if after_v:
                    pe.wait_ge(v_ready, b)
                for k in range(KT):
                    last = pe.transpose(ps[:, 0, k * S:(k + 1) * S], xn[:, k * P:(k + 1) * P], ident[0:S, 0:S])
                last.then_inc(xnT_ps, 1)

            def qkv(b):
                pe.wait_ge(xT_ready, b + 1)
                for t in range(2 * QUADS):
                    for k in range(KT):
                        last = pe.matmul(ps[:, 1 + t // QUADS, t % QUADS * S:(t % QUADS + 1) * S], qk_w[:, k, t, :], xT[:, k, :],
                                         start=k == 0, stop=k == KT - 1)
                last.then_inc(qk_ps, 1)
                for k in range(KT):
                    pe.matmul(ps[0:S, 0, 0:D], xT[:, k, :], v_w[:, k, :], start=k == 0, stop=False)
                pe.matmul(ps[0:S, 0, 0:D], ones[:, 0:S], v_b, start=False, stop=True).then_inc(v_ps, 1)

            def scores(b, half):
                if half == 0:
                    pe.wait_ge(qk_ready, 2 * b + 2)
                product(mask_q, qT, kT, half).then_inc(score_ps, 1)

            def product(mask, left, right, half):
                rows = (2 * half, 2 * half + 1)
                for j in range(QUADS):
                    for r in rows:
                        g = slice(32 * r, 32 * r + 32)
                        pe.matmul(ps[0:S, 3 + r, j * S:(j + 1) * S], left[g, j, :], right[g, j, :], start=j == 0,
                                  stop=False, tile_position=(32 * r, 0), skip_group_check=True)
                for r in rows:
                    last = pe.matmul(ps[0:S, 3 + r, 0:QUADS * S], identb[0:S, 0:S], mask[:, :].unsqueeze(1).broadcast_to([S, 4, S]), start=False, stop=True, skip_group_check=True)
                return last

            def turn_max(b):
                pe.wait_ge(negmax_ready, 4 * b + 4)
                for j in range(QUADS):
                    last = pe.transpose(ps[:, 1, j * S:(j + 1) * S], negmax[:, j].rearrange("p h e -> p (h e)"), ident[0:S, 0:S])
                last.then_inc(nmT_ps, 1)

            def scores_t(b, half):
                if half == 0:
                    pe.wait_ge(qm_ready, b + 1)
                product(mask_k, kT, qmT, half).then_inc(scoreT_ps, 1)

            def weighted(b, r):
                if r == 0:
                    pe.wait_ge(resid1_ready, b + 1)
                    pe.wait_ge(v_ready, b + 1)
                pe.wait_ge(probs_ready, 4 * b + r + 1)
                for j in range(QUADS):
                    g = 4 * j + r
                    last = pe.matmul(ps[0:S, 7, g * (HD + 1):(g + 1) * (HD + 1)], probs[:, r % 2, j, :], vh[:, g, :],
                                     start=True, stop=True, skip_group_check=True)
                last.then_inc(av_ps, 1)

            def turn_attn(b):
                pe.wait_ge(attn_ready, b + 1)
                for k in range(KT):
                    last = pe.transpose(ps[:, 7, k * S:(k + 1) * S], attn[:, 8 * k:8 * k + 8, :].rearrange("p h e -> p (h e)"), ident[0:S, 0:S])
                last.then_inc(attnT_ps, 1)

            def project(b):
                pe.wait_ge(attnT_ready, b + 1)
                for k in range(KT):
                    pe.matmul(ps[0:S, 7, 0:D], attnT[:, k, :], o_w[:, k, :], start=k == 0, stop=False)
                pe.matmul(ps[0:S, 7, 0:D], ones[:, 0:S], o_b, start=False, stop=True).then_inc(oproj_ps, 1)

            pe.wait_ge(attn_in, 6 * 16)
            pe.wait_ge(wqT_ready, 6)
            pe.wait_ge(pool_set, 4)
            pe.wait_ge(img_ready, B // 2)
            turn_x(0, after_v=False)
            qkv(0)
            scores(0, 0)
            scores(0, 1)
            turn_max(0)

            def step(b, more=True):
                scores_t(b, 0)
                scores_t(b, 1)
                if more:
                    turn_x(b + 1)
                weighted(b, 0)
                weighted(b, 1)
                weighted(b, 2)
                weighted(b, 3)
                if more:
                    qkv(b + 1)
                turn_attn(b)
                if more:
                    scores(b + 1, 0)
                project(b)
                if more:
                    scores(b + 1, 1)
                    turn_max(b + 1)

            with pe.Fori(0, B - 1) as b:
                step(b)
            step(B - 1, more=False)

        def pe_router(pe):
            pe.wait_ge(moe_in, 32)

            def score(b, par):
                for k in range(KT):
                    last = pe.matmul(ps[0:S, 2, bass.ds(b * EXPERTS, EXPERTS)], xtT2[par][:, k, :], router_w[:, k, :],
                                     start=k == 0, stop=k == KT - 1, skip_group_check=True)
                last.then_inc(logits_ps, 1)

            with pe.Fori(0, B // 2) as i:
                b = 2 * i
                for par in range(2):
                    pe.wait_ge(xn2_ready, b + par + 1)
                    for k in range(KT):
                        last = pe.transpose(ps[:, par, k * S:(k + 1) * S], xt2[par][:, k * P:(k + 1) * P], ident[0:S, 0:S])
                    last.then_inc(xn2T_ps, 1)
                for par in range(2):
                    pe.wait_ge(xT2_ready, b + par + 1)
                    score(b + par, par)
            pe.wait_ge(chosen_ready, 1)
            flat = chosenb[:, :, :].rearrange("p b e -> p (b e)")
            pe.matmul(ps[0:S, 2, 0:B * EXPERTS], upperb[:, :], flat, start=True, stop=True).then_inc(counts_ps, 1)
            pe.matmul(ps[0:S, 7, 0:B * EXPERTS], onesb[:, :], flat, start=True, stop=True).then_inc(counts_ps, 1)

        def pe_shared(pe):
            pe.wait_ge(xT2_kept, B + 2)
            with pe.Fori(0, 4) as g:
                for m in range(HT):
                    par = m % 2
                    pe.wait_ge(sh_ready, g * HT + m + 1)
                    for bank, at, done in ((3 + 2 * par, GATE, sgate_ps), (4 + 2 * par, UP, sup_ps)):
                        for k in range(KT):
                            last = pe.matmul(ps[:, bank, 0:4 * S], sh_w[:, at + k * HID + m * P:at + k * HID + (m + 1) * P],
                                             xT2[:, k, bass.ds(g * 4 * S, 4 * S)], start=k == 0, stop=k == KT - 1)
                        last.then_inc(done, 1)
                pe.wait_ge(sh_ready, g * HT + HT + 2)
                for pair in range(2):
                    pe.wait_ge(sresid_ready, 2 * g + pair + 1)
                    for r in range(2):
                        for m in range(HT):
                            b = 2 * pair + r
                            last = pe.matmul(ps[0:S, pair, r * D:(r + 1) * D], s_hT[:, m, b * S:(b + 1) * S],
                                             sh_w[:, DOWN + m * D:DOWN + (m + 1) * D], start=m == 0, stop=m == HT - 1,
                                             skip_group_check=True)
                    last.then_inc(sdown_ps, 1)

        def pe_experts(pe):
            def turn(j, par, half):
                pe.wait_ge(xg_in[par], half)
                for k in range(KT):
                    last = pe.transpose(ps[:, 0, k * ETILE:(k + 1) * ETILE], xg[par][:, k * P:(k + 1) * P], ident)
                last.then_inc(xgT_ps, 1)

            def up_gate(j, par):
                e = pe.value_load(tile_expert[0:1, bass.ds(j, 1)], min_val=0, max_val=EXPERTS - 1)
                pe.wait_ge(xgT_ready, j + 1)
                for bank, at, done in ((1 + 2 * par, GATE, egate_ps), (2 + 2 * par, UP, eup_ps)):
                    for k in range(KT):
                        last = pe.matmul(ps[:, bank, :], xgT[par][:, k, :], arena[:, bass.ds(e * EW + at + k * HID, HID)],
                                         start=k == 0, stop=k == KT - 1)
                    last.then_inc(done, 1)
                return e

            def down(j, e):
                pe.wait_ge(ehT_ready, j + 1)
                pe.wait_ge(ey_ready, j + 1)
                for m in range(HT):
                    last = pe.matmul(ps[:, 6, 0:D], e_hT[:, m, :], arena[:, bass.ds(e * EW + DOWN + m * D, D)],
                                     start=m == 0, stop=m == HT - 1)
                last.then_inc(ey_ps, 1)

            def turn_hidden(j, par):
                pe.wait_ge(eh_ready, j + 1)
                for m in range(HT):
                    last = pe.transpose(ps[:, 5, m * P:(m + 1) * P], e_h[par][:, m * P:(m + 1) * P], ident)
                last.then_inc(ehT_ps, 1)

            def expert(j):
                return pe.value_load(tile_expert[0:1, bass.ds(j, 1)], min_val=0, max_val=EXPERTS - 1)

            pe.wait_ge(experts_in, 16 * EXPERTS)
            pe.wait_ge(slots_ready, 1)
            pe.wait_ge(sresid_ready, 8 + 2)
            turn(0, 0, 16)
            pe.wait_ge(xgT_ready, 1)
            turn(1, 1, 16)
            up_gate(0, 0)
            with pe.Fori(0, (ETILES - 2) // 2) as i:
                j = 2 * i
                for par in range(2):
                    up_gate(j + par + 1, 1 - par)
                    turn_hidden(j + par, par)
                    turn(j + par + 2, par, 8 * j + 32)
                    down(j + par, expert(j + par))
            up_gate(ETILES - 1, 1)
            turn_hidden(ETILES - 2, 0)
            down(ETILES - 2, expert(ETILES - 2))
            turn_hidden(ETILES - 1, 1)
            down(ETILES - 1, expert(ETILES - 1))

        def pe_weights(pe):
            pe.wait_ge(cast_done, 5)
            pe.wait_ge(img_ready, B // 2)
            pe.wait_ge(wq_ready, 3)
            for n in range(2):
                for k in range(KT):
                    for t in range(FT):
                        last = pe.transpose(psb(2 * n + k)[:, t * FP:(t + 1) * FP], raw_q[:, n, t, k * P:(k + 1) * P], identb[0:FP, 0:FP])
                    last.then_inc(wqT_ps, 1)
            for q in range(2):
                for m in range(4 * q, 4 * q + 4):
                    for k in range(KT):
                        at = (m % 4) * D + k * P
                        last = pe.transpose(psb(4 + q)[0:FP, at:at + P], raw_dq[:, k, m * FP:(m + 1) * FP], identb[:, :])
                last.then_inc(wqT_ps, 1)

        def pe_ffn(pe):
            def scales(turn, parts):
                pe.wait_ge(amax_ready, turn + 1)
                pe.transpose(ps[0:1, 7, 0:parts], amax[0:parts, :], ident[0:parts, 0:parts]).then_inc(amaxT_ps, 1)
                pe.wait_ge(scale_ready, turn + 1)
                pe.matmul(ps[:, 7, 0:2], ones, amax1[:, 1:3], start=True, stop=True).then_inc(scale_ps, 1)

            scales(0, S)
            for g in range(FG):
                pe.wait_ge(xq_ready, g + 1)
                for k in range(KT):
                    if g > 0:
                        pe.wait_ge(xqT_ready, KT * (g - 1) + k + 1)
                    for r in range(4):
                        last = pe.transpose(psb(k)[:, r * S4:r * S4 + S], xqb[g % 2][:, r, k * P:(k + 1) * P], identb[0:S, 0:S])
                    last.then_inc(xqT_ps, 1)
            pe.wait_ge(xqT_ready, KT * FG)
            with pe.Fori(0, FG) as g:
                for m in range(FT):
                    par = m % 2
                    pe.wait_ge(hid_ready, g * FT + m + 1)
                    for bank, w, done in ((2 + 2 * par, gq, fgate_ps), (3 + 2 * par, uq, fup_ps)):
                        for k in range(KT):
                            last = pe.matmul(ps[0:FP, bank, 0:4 * S], w[:, k, m * FP:(m + 1) * FP], xqT[:, k, bass.ds(g * 4 * S, 4 * S)],
                                             start=k == 0, stop=k == KT - 1)
                        last.then_inc(done, 1)
            scales(1, FP)
            pe.wait_ge(dscale_ready, KT)
            for k in range(KT):
                last = pe.matmul(ps[:, 6, k * P:(k + 1) * P], onesf[:, :], diag_d[:, k, :], start=True, stop=True, skip_group_check=True)
            last.then_inc(dscaleT_ps, 1)
            for b in range(B):
                pe.wait_ge(hq_ready, b // 4 + 1)
                if b >= 4:
                    pe.wait_ge(fy_ready, b - 3)
                for m in range(FT):
                    last = pe.matmul(ps[0:S, b % 4, 0:D], hq[:, m, b * S:(b + 1) * S], dq[:, m, :], start=m == 0, stop=m == FT - 1)
                last.then_inc(fdown_ps, 1)

        def pe_ssm(pe):
            def turn(g):
                pe.wait_ge(xn3_ready, GB * g + GB)
                for k in range(KT):
                    for r in range(GB):
                        last = pe.transpose(ps[:, 0, k * N + r * S:k * N + (r + 1) * S], xn3[r][:, k * P:(k + 1) * P], ident[0:S, 0:S])
                last.then_inc(x3T_ps, 1)

            def project_in(g, par):
                pe.wait_ge(x3T_ready, g + 1)
                for m in range(2 * KT):
                    for k in range(KT):
                        last = pe.matmul(ps[:, 1 - m // KT, m % KT * N:(m % KT + 1) * N], in_w[:, k, m * P:(m + 1) * P], x3T[par][:, k, :],
                                         start=k == 0, stop=k == KT - 1, skip_group_check=True)
                    if m % KT == KT - 1:
                        last.then_inc((xin_ps, res_ps)[m // KT], 1)

            def convolve(g):
                pe.wait_ge(xpad_ready, KT * g + KT)
                for m in range(KT):
                    for t in range(TAPS):
                        last = pe.matmul(ps[:, 1, m * N:(m + 1) * N], conv_diag[:, m, t, :], xpad[:, m, :, t:t + S],
                                         start=t == 0, stop=t == TAPS - 1, skip_group_check=True)
                last.then_inc(conv_ps, 1)

            def project_x(g, par):
                pe.wait_ge(xc_ready, KT * g + KT)
                pe.wait_ge(res_ready, KT * g + KT)
                for w, rows, at in ((rank_w, RANK, 0), (bc_w, 96, N)):
                    for k in range(KT):
                        last = pe.matmul(ps[0:rows, 0, at:at + N], w[:, k, :], xc[par][:, k, :], start=k == 0, stop=k == KT - 1,
                                         skip_group_check=True)
                last.then_inc(proj_ps, 1)

            def project_dt(g):
                pe.wait_ge(proj_ready, 4 * g + 1)
                for m in range(KT):
                    last = pe.matmul(ps[:, 1, m * N:(m + 1) * N], dt_w[:, m * P:(m + 1) * P], rankT, start=True, stop=True, skip_group_check=True)
                last.then_inc(dt_ps, 1)

            def spread(g, c, par):
                k, kp = g * CHUNKS + c, c % 2
                if c == 0:
                    pe.wait_ge(bc3_ready, 2 * g + 2)
                    pe.wait_ge(proj_ready, 4 * g + 4)
                pe.wait_ge(drive_ready, k + 1)
                for n in range(2):
                    last = pe.matmul(ps[:, 2 + kp, n * N:(n + 1) * N], pick[:, 2 * c + n, :], bc3[par], start=True, stop=True, skip_group_check=True)
                last.then_inc(b_ps, 1)
                pe.wait_ge(c_ready, k + 1)
                for n in range(2):
                    last = pe.matmul(ps[:, 4 + kp, n * N:(n + 1) * N], pick[:, STATES + 2 * c + n, :], bc3[par], start=True, stop=True,
                                     skip_group_check=True)
                last.then_inc(c_ps, 1)

            def reduce(g, c, par):
                k, kp = g * CHUNKS + c, c % 2
                if c == 0:
                    pe.wait_ge(yT_ready, g + 1)
                pe.wait_ge(read_ready, k + 3)
                for n in range(2):
                    last = pe.matmul(ps[:, 6, 0:KT * N], ident, read[kp][:, n].rearrange("p k s -> p (k s)"), start=c == 0 and n == 0,
                                     stop=False, skip_group_check=True)
                last.then_inc(read_used, 1)
                if c == CHUNKS - 1:
                    for m in range(KT):
                        last = pe.matmul(ps[:, 6, m * N:(m + 1) * N], d_diag[:, m, :], xc[par][:, m, :], start=False, stop=True,
                                         skip_group_check=True)
                    last.then_inc(y_ps, 1)

            def skip(g, par):
                for r in range(GB):
                    for k in range(KT):
                        pe.matmul(ps[0:S, 7, r * D:(r + 1) * D], x3T[par][:, k, r * S:(r + 1) * S], skip_w[:, k, :], start=r == 0 and k == 0,
                                  stop=False, skip_group_check=True)
                    pe.matmul(ps[0:S, 7, r * D:(r + 1) * D], ones2[:, 0:S], outskip_b, start=False, stop=False, skip_group_check=True)

            def project_out(g):
                pe.wait_ge(yT_ready, g + 2)
                for r in range(GB):
                    for k in range(KT):
                        last = pe.matmul(ps[0:S, 7, r * D:(r + 1) * D], yT[:, k, r * S:(r + 1) * S], out_w[:, k, :], start=False,
                                         stop=k == KT - 1, skip_group_check=True)
                last.then_inc(ssm_ps, 1)

            def step(g, par, more=True, before=True):
                for c in range(CHUNKS):
                    if c < CHUNKS - 1:
                        spread(g, c + 1, par)
                    elif more:
                        spread(g + 1, 0, 1 - par)
                    if more:
                        if c == 0:
                            turn(g + 1)
                        if c == 1:
                            project_in(g + 1, 1 - par)
                        if c == 2:
                            convolve(g + 1)
                        if c == 3:
                            project_x(g + 1, 1 - par)
                        if c == 4:
                            project_dt(g + 1)
                    if c > 0:
                        reduce(g, c - 1, par)
                    elif before:
                        reduce(g - 1, CHUNKS - 1, 1 - par)
                    if before and c == 1:
                        project_out(g - 1)
                    if c == CHUNKS - 1:
                        if before:
                            pe.wait_ge(resid3_ready, g)
                        skip(g, par)

            pe.wait_ge(diag_done, KT * (TAPS + 1))
            pe.wait_ge(pick_done, 1)
            turn(0)
            project_in(0, 0)
            convolve(0)
            project_x(0, 0)
            project_dt(0)
            spread(0, 0, 0)
            step(0, 0, before=False)
            with pe.Fori(0, (GROUPS - 2) // 2) as i:
                for half in range(2):
                    step(2 * i + 1 + half, 1 - half)
            step(GROUPS - 1, 1, more=False)
            reduce(GROUPS - 1, CHUNKS - 1, 1)
            project_out(GROUPS - 1)

        @block.tensor
        def _(pe):
            pe_tokens(pe)
            pe_weights(pe)
            pe_attention(pe)
            pe_router(pe)
            pe_shared(pe)
            pe_experts(pe)
            pe_ssm(pe)
            pe_ffn(pe)


def _constants():
    c = np.zeros((P, NCONST), np.float32)
    c[:, C_ID:C_ID + P] = np.eye(P)
    q, k = np.arange(S)[:, None], np.arange(S)[None, :]
    c[:S, C_MQ:C_MQ + S] = np.where(k > q, NEG, 0.0)
    c[:S, C_MK:C_MK + S] = np.where(k < q, NEG, 0.0)
    c[:S, C_UP:C_UP + S] = k > q
    c[:, C_REP:C_REP + 32] = np.tile(np.eye(32), (4, 1))
    c[:, C_E8:C_E8 + EXPERTS] = np.arange(EXPERTS) - EXPERTS
    c[:, C_K128:C_K128 + NK128] = ETILE * np.arange(NK128)
    c[:, C_TILE:C_TILE + ETILES] = np.arange(ETILES)
    c[:, C_RES:C_RES + EXPERTS * B] = np.arange(EXPERTS * B) % B > 0
    c[:, C_RES8:C_RES8 + EXPERTS] = 1.0
    return c


def _tiles(w, parts=P):
    return np.ascontiguousarray(w.reshape(-1, parts, w.shape[-1]).transpose(1, 0, 2))


def _layout(x, n):
    a = {}
    img = np.asarray(x["x"])
    a["patches"] = _tiles(np.ascontiguousarray(img.reshape(B, 6, 16, 6, 16, 3).transpose(2, 4, 5, 0, 1, 3)).reshape(PATCH, B * IMG))
    a["tok_w"] = _tiles(n["L0_tok_W_proj"].T)
    a["tok_b"] = n["L0_tok_b_proj"].reshape(KT, P).T
    a["pos"] = _tiles(n["L0_tok_pos_emb"].T)
    a["txt"] = n["txt"]
    qkv, qkv_b = n["L0_attn_qkv_w"], n["L0_attn_qkv_b"]
    qk = np.zeros((D, 2 * QUADS, 4, 32), np.float32)
    qk[..., :HD] = qkv[:, :2 * D].reshape(D, 2 * QUADS, 4, HD)
    a["qk_w"] = _tiles(qk.reshape(D, -1)).reshape(P, KT, 2 * QUADS, P)
    qb = np.zeros((2 * QUADS, 4, 32), np.float32)
    qb[..., :HD] = qkv_b[:2 * D].reshape(2 * QUADS, 4, HD)
    qb[QUADS:, :, HD] = 1.0
    a["qk_b"] = qb.reshape(2 * QUADS, P).T
    a["v_w"], a["v_b"] = _tiles(qkv[:, 2 * D:]), qkv_b[None, 2 * D:]
    a["o_w"], a["o_b"] = _tiles(n["L0_attn_out_w"]), n["L0_attn_out_b"][None]
    a["router_w"] = _tiles(n["L0_ffn_router"].T)

    def expert(gate, up, down):
        return np.concatenate([_tiles(w.T).reshape(P, -1) for w in (up, gate, down)], axis=1)

    a["sh_w"] = expert(n["L0_ffn_w_gate_s"], n["L0_ffn_w_up_s"], n["L0_ffn_w_down_s"])
    a["ex_w"] = np.stack([expert(n["L0_ffn_gate"][e], n["L0_ffn_up"][e], n["L0_ffn_down"][e]) for e in range(EXPERTS)])
    m = {k: n["L1_attn_" + k] for k in ("in_proj_w", "in_proj_b", "conv_w", "conv_b", "x_proj_w", "x_proj_b", "dt_proj_w",
                                        "dt_proj_b", "A_log", "D_param", "out_proj_w", "out_proj_b", "skip_proj_w", "skip_proj_b")}
    a["in_w"], a["in_b"] = _tiles(m["in_proj_w"].T), m["in_proj_b"].reshape(2 * KT, P).T
    a["conv_w"] = m["conv_w"].reshape(KT, P, TAPS).transpose(1, 0, 2)
    a["conv_b"] = m["conv_b"].reshape(KT, P).T
    a["rank_w"], a["rank_b"] = _tiles(m["x_proj_w"][:RANK].T), m["x_proj_b"][:RANK, None]
    a["bc_w"] = _tiles(np.tile(m["x_proj_w"][RANK:], (3, 1)).T)
    a["bc_b"] = np.tile(m["x_proj_b"][RANK:], 3)[:, None]
    a["dt_w"], a["dt_b"] = m["dt_proj_w"].T, m["dt_proj_b"].reshape(KT, P).T
    a["a_log"], a["d_par"] = m["A_log"], m["D_param"].reshape(KT, P).T
    a["out_w"], a["skip_w"] = _tiles(m["out_proj_w"].T), _tiles(m["skip_proj_w"].T)
    a["outskip_b"] = np.stack([m["out_proj_b"], m["skip_proj_b"]])
    a["f_gate"] = n["L1_ffn_w_gate"].reshape(FT, FP, D).transpose(1, 0, 2)
    a["f_up"] = n["L1_ffn_w_up"].reshape(FT, FP, D).transpose(1, 0, 2)
    a["f_down"] = _tiles(n["L1_ffn_w_down"])
    a["clip_x"], a["clip_h"] = n["L1_ffn_clip_x"][None], n["L1_ffn_clip_down"][None]
    a["const"] = _constants()
    return {k: np.ascontiguousarray(v) for k, v in a.items()}


def kernel(**inputs):
    import concourse.bacc as bacc
    from concourse.bass_utils import run_bass_kernel_spmd

    given = {k: np.asarray(v) for k, v in inputs.items()}
    arrays = _layout(given, given)
    nc = bacc.Bacc("TRN2", target_bir_lowering=False, num_devices=1)
    a = {k: nc.dram_tensor("in_" + k, v.shape, mybir.dt.from_np(v.dtype), kind="ExternalInput").ap() for k, v in arrays.items()}
    out = nc.dram_tensor("out", (B, S, D), F32, kind="ExternalOutput").ap()
    build(nc, a, out)
    result = run_bass_kernel_spmd(nc, [{"in_" + k: v for k, v in arrays.items()}], core_ids=[0])
    return result.results[0]["out"]
```

```python
from contextlib import ExitStack

import numpy as np
import concourse.bass as bass
from concourse import mybir

F32 = mybir.dt.float32
BF16 = mybir.dt.bfloat16
I32 = mybir.dt.int32
ALU = mybir.AluOpType
ACT = mybir.ActivationFunctionType
AX = mybir.AxisListType

P = 128
B, IMG, TXT, D = 16, 36, 77, 256
S = IMG + TXT
T = B * S
KT = D // P
PATCH = 768
PK = PATCH // P
HEADS, HD = 16, 16
QUADS = HEADS // 4
HT8 = P // HD
EXPERTS, HID = 8, 512
HT = HID // P
EPS = 1e-5
LN_OPS, LN_VAR = 11, 7
WORK = 9472
NEG = -1e30
UP, GATE, DOWN, EW = 0, KT * HID, 2 * KT * HID, 2 * KT * HID + HT * D
STATES, TAPS, RANK = 16, 4, 64
GB = 2
GROUPS = B // GB
N = GB * S
CHUNKS = STATES // 2
FFN, FT, FP = 704, 8, 88
QMAX = 127.0
ROUND = 1.5 * 2.0 ** 23
S4 = S + S % 2
DT_CHUNK = 6
FIRST_SEQS, OTHER_SEQS = slice(0, 2 * GB), slice(2 * GB, B)
EARLY_SEQS, LAST_SEQS = slice(0, B - GB), slice(B - GB, B)
FG = 4
ETILE = 128
ETILES = (T + EXPERTS * (ETILE - 1)) // ETILE
SLOTS = ETILES * ETILE

C_ID, C_MQ, C_MK, C_UP = 0, 128, 128 + S, 128 + 2 * S
C_REP = C_UP + S
C_E8 = C_REP + 32
C_K128 = C_E8 + EXPERTS
NK128 = (T + ETILE - 1) // ETILE
C_TILE = C_K128 + NK128
C_RES = C_TILE + ETILES
C_RES8 = C_RES + EXPERTS * B
NCONST = C_RES8 + EXPERTS


class Seq:

    def __init__(self, eng, sem, base=0):
        self.eng, self.sem, self.base, self.n = eng, sem, base, 0

    def done(self, instruction):
        instruction.then_inc(self.sem, 1)
        self.n += 1

    def wait(self):
        self.eng.wait_ge(self.sem, self.base + self.n)

    def step(self, instruction):
        self.done(instruction)
        self.wait()


def build(nc, a, out):
    ctx = ExitStack()
    with ctx:
        def sb(name, shape, dt=F32):
            return ctx.enter_context(nc.sbuf_tensor(name, shape, dt))

        def sem(name):
            return ctx.enter_context(nc.semaphore(name))

        ps = ctx.enter_context(nc.psum_tensor("ps", [P, 8, 512], F32))

        resid = sb("resid", [S, B, D])
        const = sb("const", [P, NCONST])
        identb = sb("identb", [P, P], BF16)
        mask_q = sb("mask_q", [S, S], BF16)
        mask_k = sb("mask_k", [S, S], BF16)
        ones2 = sb("ones2", [2, P])
        ones = ones2[0:1, :]
        onesf = sb("onesf", [P, P])
        round_at = sb("round_at", [P, 2])
        stats = sb("stats", [S, B, 6])
        lnt = sb("lnt", [S, 6, B])
        mean = sb("mean", [S, B])
        rstd = sb("rstd", [S, B])
        arena = sb("arena", [P, EXPERTS * EW])
        work = sb("work", [P, WORK])
        ident = const[:, C_ID:C_ID + P]

        def psb(bank):
            return ps[:, bank, :].bitcast(BF16)

        def view(store, at, shape, parts=P):
            n = int(np.prod(shape))
            v = store[0:parts, at:at + n]
            if len(shape) > 1:
                names = "abcd"[:len(shape)]
                v = v.rearrange(f"p ({' '.join(names)}) -> p {' '.join(names)}", **{k: s for k, s in zip(names[1:], shape[1:])})
            return v

        class Place:
            def __init__(self, store, at=0):
                self.store, self.at = store, at

            def take(self, shape, parts=P):
                v = view(self.store, self.at, shape, parts)
                self.at += int(np.prod(shape))
                assert self.at <= self.store.shape[1], self.at
                return v

        pl = Place(arena)
        patches = pl.take((PK, B * IMG))
        tok_w = pl.take((PK, D))
        tok_bias = pl.take((KT,))
        pos = pl.take((KT, IMG))
        tokT = pl.take((KT, B * IMG))
        pl = Place(work)
        qk_w = pl.take((KT, 2 * KT, P))
        qk_b = pl.take((2 * KT,))
        v_w = pl.take((KT, D))
        v_b = pl.take((D,), S)
        o_w = pl.take((QUADS, D))
        o_b = pl.take((D,), S)
        head_mask = pl.take((HT8,))
        sum_pick = pl.take((P,))
        max_pick = pl.take((HEADS * P // 2,), 96).bitcast(BF16).rearrange("p (h m) -> p h m", h=HEADS)
        xn = pl.take((D,), S)
        xT = pl.take((KT, S))
        qkT = pl.take((2 * KT, S))
        negmax = pl.take((3, 32), S)
        nm_rest = pl.take((S,), 96)
        nm_hi = pl.take((S4 // 2,), 96).bitcast(BF16)[:, 0:S]
        nm_mid = pl.take((S4 // 2,), 96).bitcast(BF16)[:, 0:S]
        nm3 = pl.take((S4 // 2,), 96).bitcast(BF16)[:, 0:S]
        vh = pl.take((HEADS, 32), S)
        raw_dq_at = pl.at
        probs = pl.take((QUADS, 4, S), S)
        attn = pl.take((QUADS, S))
        rsum = pl.take((QUADS, S))
        assert pl.at <= WORK - D
        zero = view(work, WORK - D, (D,))

        sh_w = sb("sh_w", [P, EW])
        xn2 = sb("xn2", [S, B, D])
        xT2_flat = sb("xT2", [P, KT * T])
        xT2 = xT2_flat[:, :].rearrange("p (k t) -> p k t", k=KT)
        qz = view(xT2_flat, 0, (HEADS, S))
        kz = view(xT2_flat, HEADS * S, (HEADS, S))
        pl = Place(work)
        router_w = sb("router_w", [P, KT, EXPERTS])
        xt2 = [pl.take((D,), S) for _ in range(2)]
        xtT2 = [pl.take((KT, S)) for _ in range(2)]
        logits = pl.take((B, EXPERTS), S)
        rtop = pl.take((B, 1), S)
        rpick = pl.take((B, EXPERTS), S)
        chosen = pl.take((B, EXPERTS), S)
        prefix = pl.take((B, EXPERTS), S)
        total = pl.take((EXPERTS, B), S)
        summed = pl.take((EXPERTS, B), S)
        etiles = pl.take((EXPERTS, NK128), S)
        ecount = pl.take((EXPERTS,), S)
        esum = pl.take((EXPERTS,), S)
        ebase = pl.take((EXPERTS,), S)
        tile_ge = pl.take((ETILES, EXPERTS), S)
        tile_e = pl.take((ETILES,), S)
        slotf = pl.take((B,), S)
        s_gate = pl.take((2, 4 * S))
        s_hT = pl.take((HT, 4 * S))
        chosenb = sb("chosenb", [S, B, EXPERTS], BF16)
        upperb = sb("upperb", [S, S], BF16)
        onesb = sb("onesb", [S, S], BF16)
        slot = sb("slot", [S, B], I32)
        tile_expert = sb("tile_expert", [1, ETILES], I32)
        xg = [pl.take((D,)) for _ in range(2)]
        xgT = [pl.take((KT, ETILE)) for _ in range(2)]
        e_gate = [pl.take((HID,)) for _ in range(2)]
        e_h = [pl.take((HID,)) for _ in range(2)]
        e_hT = pl.take((HT, ETILE))
        e_y = [pl.take((D,)) for _ in range(2)]
        slots_in = nc.dram_tensor("slots_in", (SLOTS, D), F32).ap()
        slots_out = nc.dram_tensor("slots_out", (SLOTS, D), F32).ap()

        pl = Place(sh_w)
        in_w = pl.take((KT, 2 * D))
        in_b = pl.take((2 * KT,))
        conv_w = pl.take((KT, TAPS))
        conv_b = pl.take((KT,))
        rank_w = pl.take((KT, RANK))
        rank_b = pl.take((1,), RANK)
        bc_w = pl.take((KT, 96))
        bc_b = pl.take((1,), 96)
        dt_w = pl.take((D,), RANK)
        dt_b = pl.take((KT,))
        a_neg = pl.take((STATES,))
        d_par = pl.take((KT,))
        out_w = pl.take((KT, D))
        skip_w = pl.take((KT, D))
        outskip_b = pl.take((D,), 2)
        pl = Place(xT2_flat)
        conv_diag = pl.take((KT, TAPS, P))
        d_diag = pl.take((KT, P))
        pick = pl.take((32 * P // 2,), 96).bitcast(BF16).rearrange("p (j m) -> p j m", j=32)
        pl = Place(arena)
        xn3 = [pl.take((D,), S) for _ in range(GB)]
        x3T = [pl.take((KT, N)) for _ in range(2)]
        xpad = pl.take((KT, GB, TAPS - 1 + S))
        silu_res = [pl.take((KT, N)) for _ in range(2)]
        xc = [pl.take((KT, N)) for _ in range(2)]
        rankT = pl.take((N,), RANK)
        bc = pl.take((N,), 96)
        bc_rest = pl.take((N,), 96)
        bc_hi = pl.take((N // 2,), 96).bitcast(BF16)
        bc_mid = pl.take((N // 2,), 96).bitcast(BF16)
        bc3 = [pl.take((N // 2,), 96).bitcast(BF16) for _ in range(2)]
        sp_abs = pl.take((KT, N))
        sp_relu = pl.take((KT, N))
        delta = [pl.take((KT, N)) for _ in range(2)]
        dx = [pl.take((KT, N)) for _ in range(2)]
        decay = [pl.take((2, KT * GB, S)) for _ in range(2)]
        drive = [pl.take((2, KT, N)) for _ in range(2)]
        state = [pl.take((2, KT, N)) for _ in range(2)]
        c_sb = [pl.take((2, N)) for _ in range(2)]
        read = [pl.take((2, KT, N)) for _ in range(2)]
        yT = pl.take((KT, N))

        gq = sb("gq", [P, KT, FFN], BF16)
        uq = sb("uq", [P, KT, FFN], BF16)
        dq = sb("dq", [FP, FT, D], BF16)
        wscale = sb("wscale", [P, 4, FT])
        winv = sb("winv", [P, 3, FT])
        clips = sb("clips", [P, 2])
        clip_sig = sb("clip_sig", [P, 2])
        raw_g = xn2[0:FP, 0:8, :]
        raw_u = xn2[0:FP, 8:16, :]
        raw_d = xT2_flat[:, 0:KT * FFN].rearrange("p (k i) -> p k i", k=KT)
        pl = Place(arena)
        hid = pl.take((FT, T), FP)
        f_gate = [pl.take((FG * S,), FP) for _ in range(2)]
        fmax = pl.take((FT * FG,), FP)
        amax = pl.take((1,))
        amax1 = pl.take((4,), 1)
        xscale = pl.take((2,))
        hscale = pl.take((2,))
        gscale = pl.take((FT,), FP)
        uscale = pl.take((FT,), FP)
        dscale = pl.take((D,))
        dcol = pl.take((KT,))
        diag_d = pl.take((KT, P))
        answer_f = [pl.take((D,), S) for _ in range(2)]
        xqf = [pl.take((4, D), S) for _ in range(2)]
        xqb = [pl.take((4 * D // 2,), S).bitcast(BF16).rearrange("p (b d) -> p b d", b=4) for _ in range(2)]
        xqT = pl.take((KT * T // 2,)).bitcast(BF16).rearrange("p (k t) -> p k t", k=KT)
        pl4 = Place(work)
        hq = pl4.take((FT * T // 2,), FP).bitcast(BF16).rearrange("p (m t) -> p m t", m=FT)
        raw_q = view(xT2_flat, KT * FFN, (FT * D,), FP).bitcast(BF16).rearrange("p (w t d) -> p w t d", w=2, t=FT)
        raw_dq = view(work, raw_dq_at, (KT * FFN // 2,)).bitcast(BF16).rearrange("p (k i) -> p k i", k=KT)

        const_in, tok_in, txt_in, attn_in = sem("const_in"), sem("tok_in"), sem("txt_in"), sem("attn_in")
        cast_done, posb_done, pool_set = sem("cast_done"), sem("posb_done"), sem("pool_set")
        tok_ps, tokT_ready, tokback_ps, img_ready = sem("tok_ps"), sem("tokT_ready"), sem("tokback_ps"), sem("img_ready")
        stats_done, dve_ln, act_ln = sem("stats_done"), sem("dve_ln"), sem("act_ln")
        xn_ready, xnT_ps, xT_ready = sem("xn_ready"), sem("xnT_ps"), sem("xT_ready")
        qk_ps, qk_ready, v_ps, v_ready = sem("qk_ps"), sem("qk_ready"), sem("v_ps"), sem("v_ready")
        score_ps, negmax_ready, nmT_ps = sem("score_ps"), sem("negmax_ready"), sem("nmT_ps")
        scoreT_ps, probs_ready, av_ps = sem("scoreT_ps"), sem("probs_ready"), sem("av_ps")
        attn_copied, sums_ps, rsum_ready, attn_ready = sem("attn_copied"), sem("sums_ps"), sem("rsum_ready"), sem("attn_ready")
        oproj_ps, resid1_ready, bias_added, negmax3_ready = sem("oproj_ps"), sem("resid1_ready"), sem("bias_added"), sem("negmax3_ready")
        kz_ready, qz_ready, nm_hi_ready, nm_step, nm3_ready, pick2_done = (sem("kz_ready"), sem("qz_ready"), sem("nm_hi_ready"),
                                                                         sem("nm_step"), sem("nm3_ready"), sem("pick2_done"))
        out_done = sem("out_done")
        moe_in, experts_in, zero_set, slots_zeroed = sem("moe_in"), sem("experts_in"), sem("zero_set"), sem("slots_zeroed")
        xn2_ready, xn2T_ps, xT2_ready, xn2_kept, xT2_kept = (sem("xn2_ready"), sem("xn2T_ps"), sem("xT2_ready"),
                                                            sem("xn2_kept"), sem("xT2_kept"))
        logits_ps, route, chosen_ready, counts_ps, slots_ready = (sem("logits_ps"), sem("route"), sem("chosen_ready"),
                                                                 sem("counts_ps"), sem("slots_ready"))
        sgate_ps, sup_ps, sgate_ready, sh_ready = sem("sgate_ps"), sem("sup_ps"), sem("sgate_ready"), sem("sh_ready")
        sdown_ps, sresid_ready = sem("sdown_ps"), sem("sresid_ready")
        scattered, xg_in, xgT_ps, xgT_ready = sem("scattered"), [sem("xg_in0"), sem("xg_in1")], sem("xgT_ps"), sem("xgT_ready")
        egate_ps, eup_ps, egate_ready, eh_ready = sem("egate_ps"), sem("eup_ps"), sem("egate_ready"), sem("eh_ready")
        ehT_ps, ehT_ready, ey_ps, ey_ready, ey_out = (sem("ehT_ps"), sem("ehT_ready"), sem("ey_ps"), sem("ey_ready"),
                                                     [sem("ey_out0"), sem("ey_out1")])
        ssm_in, aneg_done, diag_done, pick_done, pads_zero = (sem("ssm_in"), sem("aneg_done"), sem("diag_done"), sem("pick_done"),
                                                             sem("pads_zero"))
        xn3_ready, x3T_ps, x3T_ready, xin_ps, res_ps = sem("xn3_ready"), sem("x3T_ps"), sem("x3T_ready"), sem("xin_ps"), sem("res_ps")
        xpad_ready, res_ready, conv_ps, xc_ready = sem("xpad_ready"), sem("res_ready"), sem("conv_ps"), sem("xc_ready")
        proj_ps, proj_ready, dt_ps, softplus_ready = sem("proj_ps"), sem("proj_ready"), sem("dt_ps"), sem("softplus_ready")
        sp_step, bc_step, bc3_ready, delta_ready, dx_ready = (sem("sp_step"), sem("bc_step"), sem("bc3_ready"), sem("delta_ready"),
                                                              sem("dx_ready"))
        b_ps, c_ps, decay_ready, c_ready = sem("b_ps"), sem("c_ps"), sem("decay_ready"), sem("c_ready")
        drive_ready, state_ready, read_ready, read_used = sem("drive_ready"), sem("state_ready"), sem("read_ready"), sem("read_used")
        y_ps, yT_ready, ssm_ps, resid3_ready = sem("y_ps"), sem("yT_ready"), sem("ssm_ps"), sem("resid3_ready")
        ffn_in, wq_step, wq_ready, wqT_ps, wqT_ready = sem("ffn_in"), sem("wq_step"), sem("wq_ready"), sem("wqT_ps"), sem("wqT_ready")
        f_step, xn4_ready, amax_ready, amaxT_ps, scale_ready, scale_ps = (sem("f_step"), sem("xn4_ready"), sem("amax_ready"),
                                                                      sem("amaxT_ps"), sem("scale_ready"), sem("scale_ps"))
        dscale_ready, dscaleT_ps, clip_exp = sem("dscale_ready"), sem("dscaleT_ps"), sem("clip_exp")
        xq_ready, xqT_ps, xqT_ready = sem("xq_ready"), sem("xqT_ps"), sem("xqT_ready")
        fgate_ps, fup_ps, fgate_ready, hid_ready = sem("fgate_ps"), sem("fup_ps"), sem("fgate_ready"), sem("hid_ready")
        hmax_ready, hq_even, hq_odd, fdown_ps, fy_ready, final_ready = (sem("hmax_ready"), sem("hq_even"), sem("hq_odd"),
                                                                     sem("fdown_ps"), sem("fy_ready"), sem("final_ready"))
        xscale_ready, gscale_ready, hscale_ready = sem("xscale_ready"), sem("gscale_ready"), sem("hscale_ready")
        xmax_ready, xround, xclip, hround, hclip = sem("xmax_ready"), sem("xround"), sem("xclip"), sem("hround"), sem("hclip")
        gathered, resid2_ready = [sem(f"gathered{n}") for n in range(B // 2)], sem("resid2_ready")

        block = ctx.enter_context(nc.Block())

        @block.sync
        def _(sp):
            sp.dma_start(tok_w, a["tok_w"]).then_inc(tok_in, 16)
            sp.dma_start(patches, a["patches"]).then_inc(tok_in, 16)
            sp.dma_start(tok_bias, a["tok_b"]).then_inc(tok_in, 16)
            sp.dma_start(pos, a["pos"]).then_inc(tok_in, 16)
            sp.dma_start(const[:, :], a["const"]).then_inc(const_in, 16)
            sp.dma_start(resid[IMG:S, :, :], a["txt"].rearrange("b s d -> s b d")).then_inc(txt_in, 16)
            for dst, name in ((qk_w, "qk_w"), (qk_b, "qk_b"), (v_w, "v_w"), (o_w, "o_w"), (sum_pick, "sum_pick"), (head_mask, "head_mask")):
                sp.dma_start(dst, a[name]).then_inc(attn_in, 16)
            for dst, name in ((v_b, "v_b"), (o_b, "o_b")):
                sp.dma_start(dst, a[name].broadcast_to([S, D])).then_inc(attn_in, 16)
            for dst, name in ((raw_g, "f_gate"), (raw_u, "f_up"), (raw_d, "f_down")):
                sp.dma_start(dst, a[name]).then_inc(ffn_in, 16)
            for c, name in enumerate(("clip_x", "clip_h")):
                sp.dma_start(clips[:, c:c + 1], a[name].broadcast_to([P, 1])).then_inc(ffn_in, 16)
            for dst, name in ((router_w[:, :, :], "router_w"), (sh_w[:, :], "sh_w")):
                sp.dma_start(dst, a[name]).then_inc(moe_in, 16)
            sp.wait_ge(zero_set, 1)
            sp.dma_start(slots_in.rearrange("(t p) d -> p t d", p=P),
                         zero.unsqueeze(1).broadcast_to([P, ETILES, D])).then_inc(slots_zeroed, 16)
            sp.wait_ge(tokback_ps, B // 2)
            for e in range(EXPERTS):
                sp.dma_start(arena[:, e * EW:(e + 1) * EW], a["ex_w"][e]).then_inc(experts_in, 16)
            sp.wait_ge(scattered, 16 * B)

            def load_tile(j, par, first):
                if not first:
                    sp.wait_ge(xgT_ps, j - 1)
                sp.dma_start(xg[par], slots_in[bass.ds(j * ETILE, ETILE), :]).then_inc(xg_in[par], 16)

            def store_tile(j, par):
                sp.wait_ge(ey_ready, j + 2)
                sp.dma_start(slots_out[bass.ds(j * ETILE, ETILE), :], e_y[par]).then_inc(ey_out[par], 16)

            load_tile(0, 0, True)
            load_tile(1, 1, True)
            sp.wait_ge(sdown_ps, 8)
            for dst, name in ((in_w, "in_w"), (in_b, "in_b"), (conv_w, "conv_w"), (conv_b, "conv_b"), (rank_w, "rank_w"),
                              (rank_b, "rank_b"), (bc_w, "bc_w"), (bc_b, "bc_b"), (dt_w, "dt_w"), (dt_b, "dt_b"),
                              (d_par, "d_par"), (out_w, "out_w"), (skip_w, "skip_w"), (outskip_b, "outskip_b")):
                sp.dma_start(dst, a[name]).then_inc(ssm_in, 16)
            sp.dma_start(a_neg, a["a_log"].broadcast_to([P, STATES])).then_inc(ssm_in, 16)
            with sp.Fori(0, (ETILES - 2) // 2) as i:
                j = 2 * i
                for par in range(2):
                    load_tile(j + par + 2, par, False)
                    store_tile(j + par, par)
            for j in (ETILES - 2, ETILES - 1):
                store_tile(j, j % 2)
            for n in range(B // 2):
                sp.wait_ge(final_ready, 2 * n + 2)
                sp.dma_start(out[2 * n:2 * n + 2].rearrange("b s d -> s b d"), resid[:, 2 * n:2 * n + 2, :]).then_inc(out_done, 16)
            sp.wait_ge(out_done, 16 * B // 2)
        def pool_attention(pool):
            def spread_queries(b):
                for t in range(KT):
                    pool.wait_ge(qk_ready, 4 * b + 2 * t + 2)
                    pool.tensor_tensor(qz[:, t * HT8:(t + 1) * HT8, :], qkT[:, t, :].unsqueeze(1).broadcast_to([P, HT8, S]),
                                       head_mask.unsqueeze(2).broadcast_to([P, HT8, S]), ALU.mult).then_inc(qz_ready, 1)

            def add_bias(b):
                pool.wait_ge(xn_ready, b + 1)
                pool.wait_ge(qz_ready, 2 * b + 2)
                pool.tensor_tensor(resid[:, b, :], resid[:, b, :], o_b, ALU.add).then_inc(bias_added, 1)
                pool.wait_ge(bias_added, b + 1)

            pool.wait_ge(attn_in, 8 * 16)
            pool.wait_ge(pool_set, 6)
            with pool.Fori(0, B) as b:
                spread_queries(b)
                add_bias(b)

        def pool_ffn(pool):
            for b in range(B):
                pool.wait_ge(fy_ready, b + 1)
                pool.tensor_tensor(resid[:, b, :], resid[:, b, :], answer_f[b % 2], ALU.add).then_inc(final_ready, 1)

        def pool_ssm(pool):
            def split(g, par):
                pool.wait_ge(proj_ready, 4 * g + 4)
                mid, low = slice(32, 64), slice(64, 96)
                pool.tensor_tensor(bc_rest[low, :], bc[low, :], bc_hi[low, :], ALU.subtract).then_inc(bc_step, 1)
                pool.tensor_tensor(bc_mid[low, :], bc[low, :], bc_hi[low, :], ALU.subtract).then_inc(bc_step, 1)
                pool.tensor_tensor(bc3[par][mid, :], bc[mid, :], bc_hi[mid, :], ALU.subtract).then_inc(bc3_ready, 1)
                pool.wait_ge(bc_step, 2 * g + 2)
                pool.tensor_tensor(bc3[par][low, :], bc_rest[low, :], bc_mid[low, :], ALU.subtract).then_inc(bc3_ready, 1)

            def step(g, par, more=True):
                for c in range(CHUNKS):
                    k = g * CHUNKS + c
                    kp = c % 2
                    if more and c == 5:
                        pool.wait_ge(read_ready, k + 2)
                        split(g + 1, 1 - par)
                        pool.wait_ge(bc3_ready, 2 * g + 4)
                    pool.wait_ge(c_ready, k + 3)
                    pool.wait_ge(state_ready, k + 3)
                    pool.wait_ge(read_used, k + 1)
                    pool.tensor_tensor(read[kp], state[kp], c_sb[kp].unsqueeze(2).broadcast_to([P, 2, KT, N]), ALU.mult)\
                        .then_inc(read_ready, 1)

            pool.wait_ge(pads_zero, 3)
            for done in gathered:
                pool.wait_ge(done, 32)
            split(0, 0)
            pool.wait_ge(bc3_ready, 2)
            step(0, 0)
            with pool.Fori(0, (GROUPS - 2) // 2) as i:
                for half in range(2):
                    step(2 * i + 1 + half, 1 - half)
            step(GROUPS - 1, 1, more=False)

        @block.gpsimd
        def _(pool):
            pool.memset(zero, 0.0).then_inc(zero_set, 1)
            pool.memset(onesf[:, :], 1.0).then_inc(pool_set, 1)
            pool.memset(round_at[:, 0:1], ROUND).then_inc(pool_set, 1)
            pool.memset(round_at[:, 1:2], -ROUND).then_inc(pool_set, 1)
            pool.memset(ones2[:, :], 1.0).then_inc(pool_set, 1)
            pool.memset(negmax, 0.0).then_inc(pool_set, 1)
            pool.memset(vh, 1.0).then_inc(pool_set, 1)

            pool_attention(pool)
            with pool.Fori(0, B // 2) as i:
                b = 2 * i
                for par in range(2):
                    pool.wait_ge(xn2_ready, b + par + 1)
                    pool.tensor_copy(xn2[:, b + par, :], xt2[par]).then_inc(xn2_kept, 1)
                    pool.wait_ge(xT2_ready, b + par + 1)
                    pool.tensor_copy(xT2[:, :, bass.ds((b + par) * S, S)], xtT2[par]).then_inc(xT2_kept, 1)
            pool.wait_ge(slots_zeroed, 16)
            pool.wait_ge(slots_ready, 1)
            pool.wait_ge(xn2_kept, B)
            for b in range(B):
                pool.indirect_dma_start(slots_in, bass.IndirectOffsetOnAxis(ap=slot[:, b:b + 1], axis=0), xn2[:, b, :], None).then_inc(scattered, 16)
            pool.wait_ge(scattered, 16 * B)
            for par in range(2):
                pool.wait_ge(ey_out[par], 16 * (ETILES // 2))
            pool.wait_ge(ey_ps, ETILES)
            pool.memset(xpad, 0.0).then_inc(pads_zero, 1)
            for d in decay:
                pool.memset(d[:, :, :, 0:1], 0.0).then_inc(pads_zero, 1)
            for b in range(B):
                pool.indirect_dma_start(xn2[:, b, :], None, slots_out,
                                        bass.IndirectOffsetOnAxis(ap=slot[:, b:b + 1], axis=0)).then_inc(gathered[b // 2], 16)
            pool_ssm(pool)
            pool_ffn(pool)

        def act_rstd(act, turn, seqs=slice(0, B)):
            act.preload_act_table_set("natural_log_exp_and_others")
            act.wait_ge(dve_ln, LN_OPS * turn + LN_VAR)
            act.activation(lnt[:, 3, seqs], lnt[:, 2, seqs], ACT.Ln).then_inc(act_ln, 1)
            act.wait_ge(act_ln, 2 * turn + 1)
            act.activation(lnt[:, 3, seqs], lnt[:, 3, seqs], ACT.Exp, scale=-0.5).then_inc(act_ln, 1)

        def act_attention(act):
            def turn_x(b):
                act.wait_ge(xnT_ps, b + 1)
                act.activation(xT, ps[:, 0, 0:KT * S].rearrange("p (k s) -> p k s", k=KT), ACT.Copy).then_inc(xT_ready, 1)

            def queries_keys(b):
                act.wait_ge(qk_ps, b + 1)
                for t in (2, 0, 3, 1):
                    act.activation(qkT[:, t, :], ps[:, 1, t * S:(t + 1) * S], ACT.Identity, bias=qk_b[:, t:t + 1]).then_inc(qk_ready, 1)

            def high_parts(b):
                act.wait_ge(nmT_ps, b + 1)
                for dst, rows in ((nm_hi, 96), (nm3, 32)):
                    act.activation(dst[0:rows, :], ps[0:rows, 7, 0:S], ACT.Copy).then_inc(nm_hi_ready, 1)

            def exps(b):
                for r in range(QUADS):
                    act.wait_ge(scoreT_ps, QUADS * b + r + 1)
                    act.activation(probs[:, r], ps[0:S, 3 + r, 0:4 * S].rearrange("p (j s) -> p j s", j=4),
                                   ACT.Exp, scale=1.0 / float(HD) ** 0.5).then_inc(probs_ready, 1)

            def outputs(b):
                act.wait_ge(av_ps, b + 1)
                act.activation(attn, ps[:, 7, 0:QUADS * S].rearrange("p (r s) -> p r s", r=QUADS), ACT.Copy).then_inc(attn_copied, 1)

            def step(b, more=True):
                high_parts(b)
                if more:
                    turn_x(b + 1)
                exps(b)
                if more:
                    queries_keys(b + 1)
                outputs(b)

            act.wait_ge(attn_in, 8 * 16)
            turn_x(0)
            queries_keys(0)
            with act.Fori(0, B - 1) as b:
                step(b)
            step(B - 1, more=False)

        def act_tokens(act):
            for pair in range(B // 2):
                act.wait_ge(tokback_ps, pair + 1)
                act.activation(resid[0:IMG, 2 * pair:2 * pair + 2, :],
                               ps[0:IMG, 4 + pair % 4, :].rearrange("p (b d) -> p b d", b=2), ACT.Copy).then_inc(img_ready, 1)

        def act_router(act):
            with act.Fori(0, B // 2) as i:
                b = 2 * i
                for par in range(2):
                    act.wait_ge(xn2T_ps, b + par + 1)
                    act.wait_ge(xT2_kept, b + par + 1)
                    act.activation(xtT2[par], ps[:, par, 0:KT * S].rearrange("p (k s) -> p k s", k=KT), ACT.Copy).then_inc(xT2_ready, 1)

        def act_shared(act):
            with act.Fori(0, (4 * HT) // 2) as i:
                n = 2 * i
                for par in range(2):
                    act.wait_ge(sgate_ps, n + par + 1)
                    act.wait_ge(sh_ready, n + par + 1)
                    act.activation(s_gate[:, par, :], ps[:, 3 + 2 * par, 0:4 * S], ACT.Silu).then_inc(sgate_ready, 1)

        def act_experts(act):
            def turn(j, par):
                act.wait_ge(xgT_ps, j + 1)
                act.activation(xgT[par], ps[:, 0, 0:KT * ETILE].rearrange("p (k s) -> p k s", k=KT), ACT.Copy).then_inc(xgT_ready, 1)

            def gate(j, par):
                act.wait_ge(egate_ps, j + 1)
                act.activation(e_gate[par], ps[:, 1 + 2 * par, :], ACT.Silu).then_inc(egate_ready, 1)

            def hidden(j):
                act.wait_ge(ehT_ps, j + 1)
                act.activation(e_hT, ps[:, 5, :].rearrange("p (m s) -> p m s", m=HT), ACT.Copy).then_inc(ehT_ready, 1)

            act.wait_ge(xgT_ps, 1)
            act.activation(xgT[0], ps[:, 0, 0:KT * ETILE].rearrange("p (k s) -> p k s", k=KT), ACT.Copy).then_inc(xgT_ready, 1)
            act.wait_ge(xgT_ps, 2)
            act.activation(xgT[1], ps[:, 0, 0:KT * ETILE].rearrange("p (k s) -> p k s", k=KT), ACT.Copy).then_inc(xgT_ready, 1)
            gate(0, 0)
            act.wait_ge(ssm_in, 16 * 15)
            act.activation(a_neg, a_neg, ACT.Exp).then_inc(aneg_done, 1)
            with act.Fori(0, (ETILES - 2) // 2) as i:
                j = 2 * i
                for par in range(2):
                    gate(j + par + 1, 1 - par)
                    hidden(j + par)
                    turn(j + par + 2, par)
            gate(ETILES - 1, 1)
            hidden(ETILES - 2)
            hidden(ETILES - 1)

        def act_weights(act):
            act.wait_ge(ffn_in, 5 * 16)
            act.activation(clip_sig[:, :], clips[:, :], ACT.Exp, scale=-1.0).then_inc(clip_exp, 1)
            for n, dst in enumerate((gq, uq)):
                for k in range(KT):
                    act.wait_ge(wqT_ps, 2 * n + k + 1)
                    act.activation(dst[:, k, :], psb(2 * n + k)[:, 0:FFN], ACT.Copy).then_inc(wqT_ready, 1)
            for q in range(2):
                act.wait_ge(wqT_ps, 5 + q)
                act.activation(dq[:, 4 * q:4 * q + 4, :], psb(4 + q)[0:FP, :].rearrange("p (m d) -> p m d", m=4), ACT.Copy).then_inc(wqT_ready, 1)

        def act_ffn(act):
            act.wait_ge(xscale_ready, 1)
            act.wait_ge(xn4_ready, B)
            def round_x(g):
                if g >= 2:
                    act.wait_ge(xq_ready, g - 1)
                act.activation(xqf[g % 2], xn2[:, 4 * g:4 * g + 4, :], ACT.Identity, scale=xscale[0:S, 1:2], bias=round_at[0:S, 0:1]).then_inc(xround, 1)

            def turn_x(g):
                for k in range(KT):
                    act.wait_ge(xqT_ps, KT * g + k + 1)
                    act.activation(xqT[:, k, g * 4 * S:(g + 1) * 4 * S].rearrange("p (b s) -> p b s", b=4),
                                   psb(2 * (g % 2) + k)[:, 0:4 * S4].rearrange("p (b s) -> p b s", b=4)[:, :, 0:S], ACT.Copy).then_inc(xqT_ready, 1)

            round_x(0)
            round_x(1)
            for g in range(FG):
                if g + 2 < FG:
                    round_x(g + 2)
                turn_x(g)
            act.wait_ge(gscale_ready, 1)
            with act.Fori(0, FG) as g:
                for m in range(FT):
                    par = m % 2
                    act.wait_ge(fgate_ps, g * FT + m + 1)
                    act.wait_ge(hid_ready, g * FT + m + 1)
                    act.activation(f_gate[par], ps[0:FP, 2 + 2 * par, 0:4 * S], ACT.Silu, scale=gscale[:, m:m + 1]).then_inc(fgate_ready, 1)
            act.wait_ge(hscale_ready, 1)

            def round_hid(piece):
                h = hid[:, :, 2 * piece * S:(2 * piece + 2) * S]
                act.activation(h, h, ACT.Identity, scale=hscale[0:FP, 1:2], bias=round_at[0:FP, 0:1]).then_inc(hround, 1)

            round_hid(0)
            for piece in range(B // 2):
                if piece + 1 < B // 2:
                    round_hid(piece + 1)
                if piece % 2 == 1:
                    act.wait_ge(hclip, piece + 1)
                    cols = slice(2 * piece * S, (2 * piece + 2) * S)
                    act.activation(hq[:, :, cols], hid[:, :, cols], ACT.Identity, bias=round_at[0:FP, 1:2]).then_inc(hq_odd, 1)

        def act_ssm(act):
            def turn(g, par):
                act.wait_ge(x3T_ps, g + 1)
                act.activation(x3T[par], ps[:, 0, 0:KT * N].rearrange("p (k s) -> p k s", k=KT), ACT.Copy).then_inc(x3T_ready, 1)

            def pad(g):
                act.wait_ge(xin_ps, g + 1)
                for m in range(KT):
                    act.activation(xpad[:, m, :, TAPS - 1:], ps[:, 1, m * N:(m + 1) * N].rearrange("p (b s) -> p b s", b=GB),
                                   ACT.Identity, bias=in_b[:, m:m + 1]).then_inc(xpad_ready, 1)

            def silus(g, par, first=False):
                act.wait_ge(res_ps, g + 1)
                act.wait_ge(conv_ps, g + 1)
                if not first:
                    act.wait_ge(yT_ready, g)
                for m in range(KT):
                    act.activation(silu_res[par][:, m, :], ps[:, 0, m * N:(m + 1) * N], ACT.Silu, bias=in_b[:, KT + m:KT + m + 1])\
                        .then_inc(res_ready, 1)
                for m in range(KT):
                    act.activation(xc[par][:, m, :], ps[:, 1, m * N:(m + 1) * N], ACT.Silu, bias=conv_b[:, m:m + 1])\
                        .then_inc(xc_ready, 1)
                act.preload_act_table_set("natural_log_exp_and_others")

            def projections(g, par):
                act.wait_ge(proj_ps, g + 1)
                act.activation(rankT, ps[0:RANK, 0, 0:N], ACT.Identity, bias=rank_b).then_inc(proj_ready, 1)
                for dst, rows in ((bc, 96), (bc_hi, 96), (bc3[par], 32)):
                    act.activation(dst[0:rows, :], ps[0:rows, 0, N:2 * N], ACT.Identity, bias=bc_b[0:rows, :]).then_inc(proj_ready, 1)

            def softplus(g):
                q = Seq(act, sp_step, 5 * g)
                act.wait_ge(dt_ps, g + 1)
                for m in range(KT):
                    q.done(act.activation(sp_abs[:, m, :], ps[:, 1, m * N:(m + 1) * N], ACT.Abs, bias=dt_b[:, m:m + 1]))
                for m in range(KT):
                    q.done(act.activation(sp_relu[:, m, :], ps[:, 1, m * N:(m + 1) * N], ACT.Relu, bias=dt_b[:, m:m + 1]))
                q.wait()
                q.step(act.activation(sp_abs, sp_abs, ACT.Exp, scale=-1.0))
                act.activation(sp_abs, sp_abs, ACT.Ln, bias=1.0).then_inc(softplus_ready, 1)

            def decays(g, c, par, first=False):
                k = g * CHUNKS + c
                if c == 0:
                    act.wait_ge(delta_ready, g + 1)
                if not first:
                    act.wait_ge(state_ready, k + 1)
                for n in range(2):
                    act.activation(decay[c % 2][:, n, :, 1:], delta[par].rearrange("p k (b s) -> p (k b) s", b=GB)[:, :, 1:],
                                   ACT.Exp, scale=a_neg[:, 2 * c + n:2 * c + n + 1]).then_inc(decay_ready, 1)

            def step(g, par, more=True, turn_next=True):
                for c in range(CHUNKS):
                    k = g * CHUNKS + c
                    kp = c % 2
                    if c < CHUNKS - 1:
                        decays(g, c + 1, par)
                    elif more:
                        decays(g + 1, 0, 1 - par)
                    act.wait_ge(c_ps, k + 1)
                    act.wait_ge(read_ready, k + 1)
                    act.activation(c_sb[kp], ps[:, 4 + kp, 0:2 * N].rearrange("p (n s) -> p n s", n=2), ACT.Copy).then_inc(c_ready, 1)
                    if turn_next and c == CHUNKS - 1:
                        turn(g + 2, par)
                    if more:
                        if c == 1:
                            pad(g + 1)
                        if c == 3:
                            silus(g + 1, 1 - par)
                        if c == 4:
                            projections(g + 1, 1 - par)
                        if c == 5:
                            softplus(g + 1)
                    elif c == 3:
                        act_rstd(act, 4, EARLY_SEQS)

            act.wait_ge(pads_zero, 3)
            turn(0, 0)
            pad(0)
            silus(0, 0, first=True)
            projections(0, 0)
            act_rstd(act, 3, OTHER_SEQS)
            softplus(0)
            turn(1, 1)
            act.wait_ge(aneg_done, 2)
            decays(0, 0, 0, first=True)
            step(0, 0)
            with act.Fori(0, (GROUPS - 4) // 2) as i:
                for half in range(2):
                    step(2 * i + 1 + half, 1 - half)
            step(GROUPS - 3, 1)
            step(GROUPS - 2, 0, turn_next=False)
            step(GROUPS - 1, 1, more=False, turn_next=False)

        @block.scalar
        def _(act):
            act_tokens(act)
            act_rstd(act, 0)
            act_weights(act)
            act_attention(act)
            act_rstd(act, 1)
            act_router(act)
            act_shared(act)
            act_experts(act)
            act_rstd(act, 2, FIRST_SEQS)
            act_ssm(act)
            act_rstd(act, 5, LAST_SEQS)
            act_ffn(act)


        def dve_layernorm(dve, turn, seqs=slice(0, B)):
            q = Seq(dve, dve_ln, LN_OPS * turn)
            me, qe, mo, qo = (stats[:, seqs, k] for k in (1, 2, 4, 5))
            q.done(dve.tensor_tensor(lnt[:, 0, seqs], me, mo, ALU.add))
            q.done(dve.tensor_tensor(lnt[:, 1, seqs], me, mo, ALU.subtract))
            q.done(dve.tensor_tensor(lnt[:, 2, seqs], qe, qo, ALU.add))
            q.wait()
            q.done(dve.tensor_scalar(mean[:, seqs], lnt[:, 0, seqs], 0.5, None, ALU.mult))
            q.done(dve.tensor_scalar(lnt[:, 2, seqs], lnt[:, 2, seqs], 1.0 / D, EPS, ALU.mult, ALU.add))
            q.step(dve.tensor_tensor(lnt[:, 1, seqs], lnt[:, 1, seqs], lnt[:, 1, seqs], ALU.mult))
            q.step(dve.scalar_tensor_tensor(out=lnt[:, 2, seqs], in0=lnt[:, 1, seqs], scalar=0.25, in1=lnt[:, 2, seqs], op0=ALU.mult, op1=ALU.add))
            assert q.n == LN_VAR
            dve.wait_ge(act_ln, 2 * turn + 2)
            y, v, t = lnt[:, 3, seqs], lnt[:, 2, seqs], lnt[:, 4, seqs]
            q.step(dve.tensor_tensor(t, y, y, ALU.mult))
            q.step(dve.tensor_tensor(t, t, v, ALU.mult))
            q.step(dve.tensor_scalar(t, t, -0.5, 1.5, ALU.mult, ALU.add))
            q.step(dve.tensor_tensor(rstd[:, seqs], y, t, ALU.mult))
            assert q.n == LN_OPS

        def dve_tokens(dve):
            dve.wait_ge(const_in, 16)
            dve.tensor_copy(identb[:, :], ident).then_inc(cast_done, 1)
            for m, c in ((mask_q, C_MQ), (mask_k, C_MK)):
                dve.tensor_copy(m[:, :], const[0:S, c:c + S]).then_inc(cast_done, 1)
            dve.tensor_copy(upperb[:, :], const[0:S, C_UP:C_UP + S]).then_inc(cast_done, 1)
            dve.memset(onesb[:, :], 1.0).then_inc(cast_done, 1)
            dve.wait_ge(tok_in, 64)
            for m in range(KT):
                dve.tensor_scalar(pos[:, m, :], pos[:, m, :], tok_bias[:, m:m + 1], None, ALU.add).then_inc(posb_done, 1)
            dve.wait_ge(posb_done, KT)
            for m in range(KT):
                for c in range(2):
                    dve.wait_ge(tok_ps, 2 * m + c + 1)
                    h = B // 2 * IMG
                    dve.tensor_tensor(tokT[:, m, c * h:(c + 1) * h].rearrange("p (b n) -> p b n", n=IMG),
                                      ps[:, 2 * m + c, 0:h].rearrange("p (b n) -> p b n", n=IMG),
                                      pos[:, m, :].unsqueeze(1).broadcast_to([P, B // 2, IMG]), ALU.add).then_inc(tokT_ready, 1)
            dve.wait_ge(txt_in, 16)
            dve.wait_ge(img_ready, B // 2)
            with dve.Fori(0, B) as b:
                dve.bn_stats(stats[:, b, :], resid[:, b, :]).then_inc(stats_done, 1)
            dve.wait_ge(stats_done, B)

        def dve_attention(dve):
            def normalise(b):
                dve.tensor_scalar(xn, resid[:, b, :], mean[:, bass.ds(b, 1)], rstd[:, bass.ds(b, 1)], ALU.subtract, ALU.mult).then_inc(xn_ready, 1)

            def spread_keys(b):
                for t in range(KT):
                    dve.wait_ge(qk_ready, 4 * b + 2 * t + 1)
                    dve.tensor_tensor(kz[:, t * HT8:(t + 1) * HT8, :], qkT[:, KT + t, :].unsqueeze(1).broadcast_to([P, HT8, S]),
                                      head_mask.unsqueeze(2).broadcast_to([P, HT8, S]), ALU.mult).then_inc(kz_ready, 1)

            def values(b):
                dve.wait_ge(v_ps, b + 1)
                dve.tensor_tensor(vh[:, :, 0:HD], ps[0:S, 0, 0:D].rearrange("p (h e) -> p h e", h=HEADS),
                                  v_b.rearrange("p (h e) -> p h e", h=HEADS), ALU.add).then_inc(v_ready, 1)

            def maxima(b):
                for r in range(QUADS):
                    dve.wait_ge(score_ps, QUADS * b + r + 1)
                    dve.tensor_reduce(negmax[:, 0, 4 * r:4 * r + 4].unsqueeze(2), ps[0:S, 3 + r, 0:4 * S].rearrange("p (j s) -> p j s", j=4),
                                      AX.X, ALU.max, negate=True).then_inc(negmax_ready, 1)
                dve.wait_ge(negmax_ready, QUADS * b + QUADS)
                dve.tensor_copy(negmax[:, 1:3, 0:HEADS], negmax[:, 0, 0:HEADS].unsqueeze(1).broadcast_to([S, 2, HEADS])).then_inc(negmax3_ready, 1)

            def split(b):
                mid, low = slice(32, 64), slice(64, 96)
                q = Seq(dve, nm_step, 2 * b)
                dve.wait_ge(nm_hi_ready, 2 * b + 2)
                q.step(dve.tensor_tensor(nm_rest, ps[0:96, 7, 0:S], nm_hi, ALU.subtract))
                dve.tensor_copy(nm3[mid, :], nm_rest[mid, :]).then_inc(nm3_ready, 1)
                q.step(dve.tensor_copy(nm_mid[low, :], nm_rest[low, :]))
                dve.tensor_tensor(nm3[low, :], nm_rest[low, :], nm_mid[low, :], ALU.subtract).then_inc(nm3_ready, 1)

            def weigh(b):
                dve.wait_ge(sums_ps, b + 1)
                dve.reciprocal(rsum, ps[:, 2, 0:QUADS * S].rearrange("p (r s) -> p r s", r=QUADS)).then_inc(rsum_ready, 1)
                dve.wait_ge(rsum_ready, b + 1)
                dve.tensor_tensor(attn, attn, rsum, ALU.mult).then_inc(attn_ready, 1)

            def add_resid(b):
                dve.wait_ge(oproj_ps, b + 1)
                dve.wait_ge(bias_added, b + 1)
                dve.tensor_tensor(resid[:, b, :], ps[0:S, 2, 0:D], resid[:, b, :], ALU.add).then_inc(resid1_ready, 1)
                dve.wait_ge(resid1_ready, b + 1)
                dve.bn_stats(stats[:, b, :], resid[:, b, :]).then_inc(stats_done, 1)

            def step(b, first=False, last=False):
                maxima(b)
                if not last:
                    normalise(b + 1)
                split(b)
                if not first:
                    weigh(b - 1)
                if not last:
                    spread_keys(b + 1)
                if not first:
                    add_resid(b - 1)
                if not last:
                    values(b + 1)

            dve.wait_ge(attn_in, 8 * 16)
            normalise(0)
            dve.tensor_copy(max_pick, const[0:96, C_REP:C_REP + HEADS].unsqueeze(2).broadcast_to([96, HEADS, P])).then_inc(pick2_done, 1)
            spread_keys(0)
            values(0)
            step(0, first=True)
            with dve.Fori(0, B - 2) as i:
                step(i + 1)
            step(B - 1, last=True)
            weigh(B - 1)
            add_resid(B - 1)

        def dve_router(dve):
            dve.wait_ge(stats_done, 2 * B)
            dve_layernorm(dve, 1)
            for n, counted in enumerate((xT2_kept, xT2_kept, sh_ready, sh_ready, sresid_ready, sresid_ready, ey_ready)):
                dve.memset(lnt[:, 5, n:n + 1], 0.0).then_inc(counted, 1)
            with dve.Fori(0, B // 2) as i:
                b = 2 * i
                for par in range(2):
                    dve.wait_ge(xT2_kept, b + par + 1)
                    dve.tensor_scalar(xt2[par], resid[:, b + par, :], mean[:, bass.ds(b + par, 1)], rstd[:, bass.ds(b + par, 1)],
                                      ALU.subtract, ALU.mult).then_inc(xn2_ready, 1)
            dve.wait_ge(logits_ps, B)
            q = Seq(dve, route)
            q.step(dve.tensor_copy(logits, ps[0:S, 2, 0:B * EXPERTS].rearrange("p (b e) -> p b e", b=B)))
            q.step(dve.tensor_reduce(rtop, logits, AX.X, ALU.max))
            q.step(dve.tensor_tensor(rpick, logits, rtop.broadcast_to([S, B, EXPERTS]), ALU.is_equal))
            e8 = const[0:S, C_E8:C_E8 + EXPERTS].unsqueeze(1).broadcast_to([S, B, EXPERTS])
            q.step(dve.tensor_tensor(rpick, rpick, e8, ALU.mult))
            q.step(dve.tensor_reduce(rtop, rpick, AX.X, ALU.min))
            q.step(dve.tensor_tensor(chosen, rtop.broadcast_to([S, B, EXPERTS]), e8, ALU.is_equal))
            dve.tensor_copy(chosenb[:, :, :], chosen).then_inc(chosen_ready, 1)
            dve.wait_ge(counts_ps, 2)
            q.done(dve.tensor_copy(prefix, ps[0:S, 2, 0:B * EXPERTS].rearrange("p (b e) -> p b e", b=B)))
            q.step(dve.tensor_copy(total, ps[0:S, 7, 0:B * EXPERTS].rearrange("p (b e) -> p e b", b=B)))
            q.step(dve.tensor_tensor_scan(summed.rearrange("p e b -> p (e b)"), const[0:S, C_RES:C_RES + EXPERTS * B],
                                          total.rearrange("p e b -> p (e b)"), 0.0, ALU.mult, ALU.add))
            q.step(dve.tensor_tensor(etiles, summed[:, :, B - 1:B].broadcast_to([S, EXPERTS, NK128]),
                                     const[0:S, C_K128:C_K128 + NK128].unsqueeze(1).broadcast_to([S, EXPERTS, NK128]), ALU.is_gt))
            q.step(dve.tensor_reduce(ecount, etiles, AX.X, ALU.add))
            q.step(dve.tensor_tensor_scan(esum, const[0:S, C_RES8:C_RES8 + EXPERTS], ecount, 0.0, ALU.mult, ALU.add))
            q.done(dve.tensor_tensor(ebase, esum, ecount, ALU.subtract))
            q.done(dve.tensor_tensor(summed, summed, total, ALU.subtract))
            q.step(dve.tensor_tensor(tile_ge, const[0:S, C_TILE:C_TILE + ETILES].unsqueeze(2).broadcast_to([S, ETILES, EXPERTS]),
                                     esum.unsqueeze(1).broadcast_to([S, ETILES, EXPERTS]), ALU.is_ge))
            q.step(dve.tensor_reduce(tile_e, tile_ge, AX.X, ALU.add))
            q.done(dve.tensor_scalar(tile_expert[:, :], tile_e[0:1, :], float(EXPERTS - 1), None, ALU.min))
            q.step(dve.scalar_tensor_tensor(out=summed, in0=ebase.unsqueeze(2).broadcast_to([S, EXPERTS, B]), scalar=float(ETILE),
                                            in1=summed, op0=ALU.mult, op1=ALU.add))
            q.step(dve.tensor_tensor(prefix, prefix, summed.rearrange("p e b -> p b e"), ALU.add))
            q.step(dve.tensor_tensor(prefix, prefix, chosen, ALU.mult))
            q.step(dve.tensor_reduce(slotf, prefix, AX.X, ALU.add))
            dve.tensor_copy(slot[:, :], slotf).then_inc(slots_ready, 1)

        def dve_shared(dve):
            with dve.Fori(0, 4) as g:
                for m in range(HT):
                    par = m % 2
                    dve.wait_ge(sgate_ready, g * HT + m + 1)
                    dve.wait_ge(sup_ps, g * HT + m + 1)
                    dve.tensor_tensor(s_hT[:, m, :], ps[:, 4 + 2 * par, 0:4 * S], s_gate[:, par, :], ALU.mult).then_inc(sh_ready, 1)
                for pair in range(2):
                    dve.wait_ge(sdown_ps, 2 * g + pair + 1)
                    r = resid[:, bass.ds(4 * g + 2 * pair, 2), :]
                    dve.tensor_tensor(r, ps[0:S, pair, :].rearrange("p (b d) -> p b d", b=2), r, ALU.add).then_inc(sresid_ready, 1)

        def dve_experts(dve):
            def hidden(j, par):
                dve.wait_ge(egate_ready, j + 1)
                dve.wait_ge(eup_ps, j + 1)
                dve.tensor_tensor(e_h[par], ps[:, 2 + 2 * par, :], e_gate[par], ALU.mult).then_inc(eh_ready, 1)

            def answer(j, par):
                dve.wait_ge(ey_ps, j + 1)
                dve.tensor_copy(e_y[par], ps[:, 6, 0:D]).then_inc(ey_ready, 1)

            hidden(0, 0)
            hidden(1, 1)
            answer(0, 0)
            hidden(2, 0)
            answer(1, 1)
            dve_ssm_tables(dve)
            with dve.Fori(1, (ETILES - 2) // 2) as i:
                j = 2 * i
                for par in range(2):
                    hidden(j + par + 1, 1 - par)
                    dve.wait_ge(ey_out[par], 8 * j)
                    answer(j + par, par)
            hidden(ETILES - 1, 1)
            dve.wait_ge(ey_out[0], 8 * (ETILES - 2))
            answer(ETILES - 2, 0)
            dve.wait_ge(ey_out[1], 8 * (ETILES - 2))
            answer(ETILES - 1, 1)

        def dve_weights(dve):
            dve.wait_ge(ffn_in, 5 * 16)
            q = Seq(dve, wq_step)
            raws = ((raw_g, FP, FT, D, raw_q[:, 0]), (raw_u, FP, FT, D, raw_q[:, 1]), (raw_d, P, KT, FFN, raw_dq))
            for n, (raw, parts, rows, width, _) in enumerate(raws):
                q.done(dve.tensor_reduce(wscale[0:parts, n, 0:rows], raw, AX.X, ALU.max, apply_absolute_value=True))
            q.wait()
            for n, (raw, parts, rows, width, _) in enumerate(raws):
                w = wscale[0:parts, n, 0:rows]
                q.step(dve.tensor_scalar(w, w, 1.0 / QMAX, None, ALU.mult))
                q.step(dve.reciprocal(winv[0:parts, n, 0:rows], w))
                q.step(dve.tensor_tensor(raw, raw, winv[0:parts, n, 0:rows].unsqueeze(2).broadcast_to([parts, rows, width]), ALU.mult))
            for raw, parts, rows, width, dst in raws:
                dve.tensor_scalar(dst, raw, ROUND, ROUND, ALU.add, ALU.subtract).then_inc(wq_ready, 1)
            dve.wait_ge(clip_exp, 1)
            q.step(dve.tensor_scalar(clip_sig[:, :], clip_sig[:, :], 1.0, QMAX, ALU.add, ALU.mult))
            q.step(dve.reciprocal(clip_sig[:, :], clip_sig[:, :]))

        def dve_xn4(dve, b):
            dve.tensor_scalar(xn2[:, b, :], resid[:, b, :], mean[:, b:b + 1], rstd[:, b:b + 1],
                              ALU.subtract, ALU.mult).then_inc(xn4_ready, 1)
            dve.wait_ge(xn4_ready, b + 1)
            dve.tensor_reduce(lnt[:, 5, b:b + 1], xn2[:, b, :], AX.X, ALU.max, apply_absolute_value=True).then_inc(xmax_ready, 1)

        def dve_ffn(dve):
            dve.wait_ge(stats_done, 4 * B)
            dve_layernorm(dve, 5, LAST_SEQS)
            for b in range(LAST_SEQS.start, B):
                dve_xn4(dve, b)
            dve.wait_ge(xmax_ready, B)
            q = Seq(dve, f_step)

            def scales(turn, source, parts, dst):
                dve.tensor_reduce(amax[0:parts, :], source, AX.X, ALU.max, apply_absolute_value=True).then_inc(amax_ready, 1)
                dve.wait_ge(amaxT_ps, turn + 1)
                q.step(dve.tensor_reduce(amax1[:, 0:1], ps[0:1, 7, 0:parts], AX.X, ALU.max))
                q.step(dve.tensor_scalar(amax1[:, 1:2], amax1[:, 0:1], clip_sig[0:1, turn:turn + 1], None, ALU.mult))
                dve.reciprocal(amax1[:, 2:3], amax1[:, 1:2]).then_inc(scale_ready, 1)
                dve.wait_ge(scale_ps, turn + 1)
                q.step(dve.tensor_copy(dst, ps[:, 7, 0:2]))

            scales(0, lnt[:, 5, :], S, xscale)
            dve.sem_inc(xscale_ready, 1)
            q.done(dve.tensor_scalar(gscale, wscale[0:FP, 0, :], xscale[0:FP, 0:1], None, ALU.mult))
            q.done(dve.tensor_scalar(uscale, wscale[0:FP, 1, :], xscale[0:FP, 0:1], None, ALU.mult))
            q.wait()
            dve.sem_inc(gscale_ready, 1)
            for g in range(FG):
                dve.wait_ge(xround, g + 1)
                dve.tensor_scalar(xqf[g % 2], xqf[g % 2], ROUND - QMAX - 1.0, ROUND + QMAX, ALU.max, ALU.min).then_inc(xclip, 1)
                dve.wait_ge(xclip, g + 1)
                if g >= 2:
                    dve.wait_ge(xqT_ps, KT * (g - 1))
                dve.tensor_scalar(xqb[g % 2], xqf[g % 2], ROUND, None, ALU.subtract).then_inc(xq_ready, 1)
            dve.sem_inc(hid_ready, 2)
            with dve.Fori(0, FG) as g:
                for m in range(FT):
                    par = m % 2
                    dve.wait_ge(fgate_ready, g * FT + m + 1)
                    dve.wait_ge(fup_ps, g * FT + m + 1)
                    h = hid[:, m, bass.ds(g * 4 * S, 4 * S)]
                    dve.scalar_tensor_tensor(out=h, in0=ps[0:FP, 3 + 2 * par, 0:4 * S], scalar=uscale[:, m:m + 1], in1=f_gate[par],
                                             op0=ALU.mult, op1=ALU.mult).then_inc(hid_ready, 1)
                    dve.wait_ge(hid_ready, g * FT + m + 3)
                    dve.tensor_reduce(fmax[:, bass.ds(g * FT + m, 1)], h, AX.X, ALU.max, apply_absolute_value=True).then_inc(hmax_ready, 1)
            dve.wait_ge(hmax_ready, FG * FT)
            scales(1, fmax, FP, hscale)
            dve.sem_inc(hscale_ready, 1)
            q.step(dve.tensor_scalar(dcol, wscale[:, 2, 0:KT], hscale[:, 0:1], None, ALU.mult))
            for k in range(KT):
                dve.tensor_scalar(diag_d[:, k, :], ident, dcol[:, k:k + 1], None, ALU.mult).then_inc(dscale_ready, 1)
            dve.wait_ge(dscaleT_ps, 1)
            q.step(dve.tensor_copy(dscale, ps[:, 6, 0:D]))

            def answers(piece):
                for b in range(2 * piece, 2 * piece + 2):
                    dve.wait_ge(fdown_ps, b + 1)
                    if b >= 2:
                        dve.wait_ge(final_ready, b - 1)
                    dve.tensor_tensor(answer_f[b % 2], ps[0:S, b % 4, 0:D], dscale[0:S, :], ALU.mult).then_inc(fy_ready, 1)

            for piece in range(B // 2):
                h = hid[:, :, 2 * piece * S:(2 * piece + 2) * S]
                dve.wait_ge(hround, piece + 1)
                dve.tensor_scalar(h, h, ROUND - QMAX - 1.0, ROUND + QMAX, ALU.max, ALU.min).then_inc(hclip, 1)
                if piece % 2 == 0:
                    dve.wait_ge(hclip, piece + 1)
                    dve.tensor_scalar(hq[:, :, 2 * piece * S:(2 * piece + 2) * S], h, ROUND, None, ALU.subtract).then_inc(hq_even, 1)
                if piece >= 2:
                    answers(piece - 2)
            answers(B // 2 - 2)
            answers(B // 2 - 1)

        def dve_ssm_tables(dve):
            dve.wait_ge(ssm_in, 16 * 15)
            dve.wait_ge(aneg_done, 1)
            dve.tensor_scalar(a_neg, a_neg, -1.0, None, ALU.mult).then_inc(aneg_done, 1)
            for m in range(KT):
                for t in range(TAPS):
                    dve.tensor_scalar(conv_diag[:, m, t, :], ident, conv_w[:, m, t:t + 1], None, ALU.mult).then_inc(diag_done, 1)
                dve.tensor_scalar(d_diag[:, m, :], ident, d_par[:, m:m + 1], None, ALU.mult).then_inc(diag_done, 1)
            dve.tensor_copy(pick, const[0:96, C_REP:C_REP + 32].unsqueeze(2).broadcast_to([96, 32, P])).then_inc(pick_done, 1)

        def dve_ssm(dve):
            def add_answers(seqs):
                for b in range(seqs.start, seqs.stop):
                    dve.wait_ge(gathered[b // 2], 32)
                    dve.tensor_tensor(resid[:, b, :], resid[:, b, :], xn2[:, b, :], ALU.add).then_inc(resid2_ready, 1)
                    dve.wait_ge(resid2_ready, b + 1)
                    dve.bn_stats(stats[:, b, :], resid[:, b, :]).then_inc(stats_done, 1)
                dve.wait_ge(stats_done, 2 * B + seqs.stop)

            add_answers(FIRST_SEQS)
            dve_layernorm(dve, 2, FIRST_SEQS)
            for counted in (state_ready, read_ready, read_used, c_ready, drive_ready):
                dve.sem_inc(counted, 2)
            dve.sem_inc(yT_ready, 1)

            def normalise(g):
                for r in range(GB):
                    b = GB * g + r
                    dve.tensor_scalar(xn3[r], resid[:, b, :], mean[:, bass.ds(b, 1)], rstd[:, bass.ds(b, 1)],
                                      ALU.subtract, ALU.mult).then_inc(xn3_ready, 1)

            def steps(g, par):
                dve.wait_ge(softplus_ready, g + 1)
                dve.wait_ge(xc_ready, KT * g + KT)
                dve.tensor_tensor(delta[par], sp_relu, sp_abs, ALU.add).then_inc(delta_ready, 1)
                dve.wait_ge(delta_ready, g + 1)
                dve.tensor_tensor(dx[par], delta[par], xc[par], ALU.mult).then_inc(dx_ready, 1)

            def chunk(g, c, par):
                k, kp = g * CHUNKS + c, c % 2
                dve.wait_ge(b_ps, k + 1)
                if c == 0:
                    dve.wait_ge(dx_ready, g + 1)
                dve.tensor_tensor(drive[kp], dx[par].unsqueeze(1).broadcast_to([P, 2, KT, N]),
                                  ps[:, 2 + kp, 0:2 * N].rearrange("p (n s) -> p n s", n=2).unsqueeze(2).broadcast_to([P, 2, KT, N]),
                                  ALU.mult).then_inc(drive_ready, 1)
                dve.wait_ge(drive_ready, k + 3)
                dve.wait_ge(decay_ready, 2 * k + 2)
                dve.wait_ge(read_ready, k + 1)
                dve.tensor_tensor_scan(state[kp].rearrange("p n k s -> p (n k s)"), decay[kp].rearrange("p n q s -> p (n q s)"),
                                       drive[kp].rearrange("p n k s -> p (n k s)"), 0.0, ALU.mult, ALU.add).then_inc(state_ready, 1)

            def gate(g, par):
                dve.wait_ge(y_ps, g + 1)
                dve.wait_ge(res_ready, KT * g + KT)
                dve.tensor_tensor(yT, ps[:, 6, 0:KT * N].rearrange("p (k s) -> p k s", k=KT), silu_res[par], ALU.mult).then_inc(yT_ready, 1)

            def add_resid(g):
                dve.wait_ge(ssm_ps, g + 1)
                r = resid[:, bass.ds(GB * g, GB), :]
                dve.tensor_tensor(r, ps[0:S, 7, :].rearrange("p (b d) -> p b d", b=GB), r, ALU.add).then_inc(resid3_ready, 1)
                dve.wait_ge(resid3_ready, g + 1)
                for q in range(GB):
                    dve.bn_stats(stats[:, GB * g + q, :], resid[:, GB * g + q, :]).then_inc(stats_done, 1)

            def step(g, par, more=True, before=True, turn_next=True):
                for c in range(CHUNKS):
                    if turn_next and c == CHUNKS - 2:
                        normalise(g + 2)
                    chunk(g, c, par)
                    if before and c == 1:
                        gate(g - 1, 1 - par)
                    if before and c == 2:
                        add_resid(g - 1)
                    if more and c == DT_CHUNK:
                        steps(g + 1, 1 - par)
                    if not more:
                        if c == 3:
                            dve.wait_ge(stats_done, 3 * B + EARLY_SEQS.stop)
                            dve_layernorm(dve, 4, EARLY_SEQS)
                        if c >= 4:
                            for b in range(4 * (c - 4), min(4 * (c - 4) + 4, EARLY_SEQS.stop)):
                                dve_xn4(dve, b)

            dve.wait_ge(ey_ps, ETILES)
            normalise(0)
            add_answers(OTHER_SEQS)
            dve_layernorm(dve, 3, OTHER_SEQS)
            steps(0, 0)
            normalise(1)
            step(0, 0, before=False)
            with dve.Fori(0, (GROUPS - 4) // 2) as i:
                for half in range(2):
                    step(2 * i + 1 + half, 1 - half)
            step(GROUPS - 3, 1)
            step(GROUPS - 2, 0, turn_next=False)
            step(GROUPS - 1, 1, more=False, turn_next=False)
            gate(GROUPS - 1, 1)
            add_resid(GROUPS - 1)

        @block.vector
        def _(dve):
            dve_tokens(dve)
            dve_layernorm(dve, 0)
            dve_weights(dve)
            dve_attention(dve)
            dve_router(dve)
            dve_shared(dve)
            dve_experts(dve)
            dve_ssm(dve)
            dve_ffn(dve)

        def pe_tokens(pe):
            pe.wait_ge(tok_in, 64)
            h = B // 2 * IMG
            for m in range(KT):
                for c in range(2):
                    for k in range(PK):
                        last = pe.matmul(ps[:, 2 * m + c, 0:h], tok_w[:, k, m * P:(m + 1) * P], patches[:, k, c * h:(c + 1) * h],
                                         start=k == 0, stop=k == PK - 1)
                    last.then_inc(tok_ps, 1)
            pe.wait_ge(tokT_ready, 4)
            pe.wait_ge(const_in, 16)
            for pair in range(B // 2):
                bank = 4 + pair % 4
                if pair >= 4:
                    pe.wait_ge(img_ready, pair - 3)
                for r in range(2):
                    for m in range(KT):
                        b = 2 * pair + r
                        last = pe.transpose(ps[0:IMG, bank, r * D + m * P:r * D + (m + 1) * P], tokT[:, m, b * IMG:(b + 1) * IMG], ident)
                last.then_inc(tokback_ps, 1)

        def pe_attention(pe):
            def turn_x(b, after_v=True):
                pe.wait_ge(xn_ready, b + 1)
                if after_v:
                    pe.wait_ge(v_ready, b)
                for k in range(KT):
                    last = pe.transpose(ps[:, 0, k * S:(k + 1) * S], xn[:, k * P:(k + 1) * P], ident[0:S, 0:S])
                last.then_inc(xnT_ps, 1)

            def queries_keys(b):
                pe.wait_ge(xT_ready, b + 1)
                for t in range(2 * KT):
                    for k in range(KT):
                        last = pe.matmul(ps[:, 1, t * S:(t + 1) * S], qk_w[:, k, t, :], xT[:, k, :],
                                         start=k == 0, stop=k == KT - 1, skip_group_check=True)
                last.then_inc(qk_ps, 1)

            def values(b):
                for k in range(KT):
                    last = pe.matmul(ps[0:S, 0, 0:D], xT[:, k, :], v_w[:, k, :], start=k == 0, stop=k == KT - 1, skip_group_check=True)
                last.then_inc(v_ps, 1)

            def scores(b, r):
                pe.wait_ge(qk_ready, 4 * b + r // 2 * 2 + 2)
                pe.wait_ge(kz_ready, 2 * b + r // 2 + 1)
                pe.matmul(ps[0:S, 3 + r, 0:4 * S], qkT[:, r // 2, :], kz[:, 4 * r:4 * r + 4, :], start=True, stop=False, skip_group_check=True)
                mask(r, mask_q, stop=True).then_inc(score_ps, 1)

            def scores_t(b, r):
                pe.wait_ge(qz_ready, 2 * b + r // 2 + 1)
                pe.wait_ge(negmax_ready, 4 * b + r + 1)
                pe.matmul(ps[0:S, 3 + r, 0:4 * S], qkT[:, KT + r // 2, :], qz[:, 4 * r:4 * r + 4, :], start=True, stop=False, skip_group_check=True)
                mask(r, mask_k, stop=False)

            def mask(r, m, stop):
                return pe.matmul(ps[0:S, 3 + r, 0:4 * S], identb[0:S, 0:S], m[:, :].unsqueeze(1).broadcast_to([S, 4, S]),
                                 start=False, stop=stop, skip_group_check=True)

            def turn_max(b):
                pe.wait_ge(negmax3_ready, b + 1)
                pe.transpose(ps[0:96, 7, 0:S], negmax.rearrange("p n h -> p (n h)"), ident[0:S, 0:S]).then_inc(nmT_ps, 1)

            def less_max(b):
                pe.wait_ge(nm_hi_ready, 2 * b + 2)
                pe.wait_ge(nm3_ready, 2 * b + 2)
                for r in range(QUADS):
                    for j in range(4):
                        last = pe.matmul(ps[0:S, 3 + r, j * S:(j + 1) * S], max_pick[:, 4 * r + j, 0:S], nm3, start=False, stop=True, skip_group_check=True)
                    last.then_inc(scoreT_ps, 1)

            def weighted(b):
                pe.wait_ge(v_ready, b + 1)
                for r in range(QUADS):
                    pe.wait_ge(probs_ready, QUADS * b + r + 1)
                    for j in range(4):
                        c = slice(32 * j, 32 * j + 32)
                        last = pe.matmul(ps[c, 7, r * S:(r + 1) * S], vh[:, 4 * r + j, :], probs[:, r, j, :],
                                         start=True, stop=True, tile_position=(0, 32 * j), skip_group_check=True)
                last.then_inc(av_ps, 1)

            def spread_sums(b, first=False):
                pe.wait_ge(attn_copied, b + 1)
                if not first:
                    pe.wait_ge(resid1_ready, b)
                pe.matmul(ps[:, 2, 0:QUADS * S], sum_pick, attn.rearrange("p r s -> p (r s)"), start=True, stop=True).then_inc(sums_ps, 1)

            def project(b):
                pe.wait_ge(attn_ready, b + 1)
                for r in range(QUADS):
                    last = pe.matmul(ps[0:S, 2, 0:D], attn[:, r, :], o_w[:, r, :], start=r == 0, stop=r == QUADS - 1)
                last.then_inc(oproj_ps, 1)

            def step(b, back=True, more=True, first_spread=False):
                scores(b, 0)
                scores(b, 1)
                if back:
                    spread_sums(b - 1, first_spread)
                scores(b, 2)
                scores(b, 3)
                scores_t(b, 0)
                scores_t(b, 1)
                turn_max(b)
                scores_t(b, 2)
                scores_t(b, 3)
                if more:
                    turn_x(b + 1)
                less_max(b)
                if more:
                    queries_keys(b + 1)
                if back:
                    project(b - 1)
                weighted(b)
                if more:
                    values(b + 1)

            pe.wait_ge(attn_in, 8 * 16)
            pe.wait_ge(wqT_ready, 6)
            pe.wait_ge(pool_set, 6)
            pe.wait_ge(img_ready, B // 2)
            turn_x(0, after_v=False)
            queries_keys(0)
            values(0)
            pe.wait_ge(pick2_done, 1)
            step(0, back=False)
            step(1, first_spread=True)
            with pe.Fori(0, B - 3) as i:
                step(i + 2)
            step(B - 1, more=False)
            spread_sums(B - 1)
            project(B - 1)

        def pe_router(pe):
            pe.wait_ge(moe_in, 32)

            def score(b, par):
                for k in range(KT):
                    last = pe.matmul(ps[0:S, 2, bass.ds(b * EXPERTS, EXPERTS)], xtT2[par][:, k, :], router_w[:, k, :],
                                     start=k == 0, stop=k == KT - 1, skip_group_check=True)
                last.then_inc(logits_ps, 1)

            with pe.Fori(0, B // 2) as i:
                b = 2 * i
                for par in range(2):
                    pe.wait_ge(xn2_ready, b + par + 1)
                    for k in range(KT):
                        last = pe.transpose(ps[:, par, k * S:(k + 1) * S], xt2[par][:, k * P:(k + 1) * P], ident[0:S, 0:S])
                    last.then_inc(xn2T_ps, 1)
                for par in range(2):
                    pe.wait_ge(xT2_ready, b + par + 1)
                    score(b + par, par)
            pe.wait_ge(chosen_ready, 1)
            flat = chosenb[:, :, :].rearrange("p b e -> p (b e)")
            pe.matmul(ps[0:S, 2, 0:B * EXPERTS], upperb[:, :], flat, start=True, stop=True).then_inc(counts_ps, 1)
            pe.matmul(ps[0:S, 7, 0:B * EXPERTS], onesb[:, :], flat, start=True, stop=True).then_inc(counts_ps, 1)

        def pe_shared(pe):
            pe.wait_ge(xT2_kept, B + 2)
            with pe.Fori(0, 4) as g:
                for m in range(HT):
                    par = m % 2
                    pe.wait_ge(sh_ready, g * HT + m + 1)
                    for bank, at, done in ((3 + 2 * par, GATE, sgate_ps), (4 + 2 * par, UP, sup_ps)):
                        for k in range(KT):
                            last = pe.matmul(ps[:, bank, 0:4 * S], sh_w[:, at + k * HID + m * P:at + k * HID + (m + 1) * P],
                                             xT2[:, k, bass.ds(g * 4 * S, 4 * S)], start=k == 0, stop=k == KT - 1)
                        last.then_inc(done, 1)
                pe.wait_ge(sh_ready, g * HT + HT + 2)
                for pair in range(2):
                    pe.wait_ge(sresid_ready, 2 * g + pair + 1)
                    for r in range(2):
                        for m in range(HT):
                            b = 2 * pair + r
                            last = pe.matmul(ps[0:S, pair, r * D:(r + 1) * D], s_hT[:, m, b * S:(b + 1) * S],
                                             sh_w[:, DOWN + m * D:DOWN + (m + 1) * D], start=m == 0, stop=m == HT - 1,
                                             skip_group_check=True)
                    last.then_inc(sdown_ps, 1)

        def pe_experts(pe):
            def turn(j, par, half):
                pe.wait_ge(xg_in[par], half)
                for k in range(KT):
                    last = pe.transpose(ps[:, 0, k * ETILE:(k + 1) * ETILE], xg[par][:, k * P:(k + 1) * P], ident)
                last.then_inc(xgT_ps, 1)

            def up_gate(j, par):
                e = pe.value_load(tile_expert[0:1, bass.ds(j, 1)], min_val=0, max_val=EXPERTS - 1)
                pe.wait_ge(xgT_ready, j + 1)
                for bank, at, done in ((1 + 2 * par, GATE, egate_ps), (2 + 2 * par, UP, eup_ps)):
                    for k in range(KT):
                        last = pe.matmul(ps[:, bank, :], xgT[par][:, k, :], arena[:, bass.ds(e * EW + at + k * HID, HID)],
                                         start=k == 0, stop=k == KT - 1)
                    last.then_inc(done, 1)
                return e

            def down(j, e):
                pe.wait_ge(ehT_ready, j + 1)
                pe.wait_ge(ey_ready, j + 1)
                for m in range(HT):
                    last = pe.matmul(ps[:, 6, 0:D], e_hT[:, m, :], arena[:, bass.ds(e * EW + DOWN + m * D, D)],
                                     start=m == 0, stop=m == HT - 1)
                last.then_inc(ey_ps, 1)

            def turn_hidden(j, par):
                pe.wait_ge(eh_ready, j + 1)
                for m in range(HT):
                    last = pe.transpose(ps[:, 5, m * P:(m + 1) * P], e_h[par][:, m * P:(m + 1) * P], ident)
                last.then_inc(ehT_ps, 1)

            def expert(j):
                return pe.value_load(tile_expert[0:1, bass.ds(j, 1)], min_val=0, max_val=EXPERTS - 1)

            pe.wait_ge(experts_in, 16 * EXPERTS)
            pe.wait_ge(slots_ready, 1)
            pe.wait_ge(sresid_ready, 8 + 2)
            turn(0, 0, 16)
            pe.wait_ge(xgT_ready, 1)
            turn(1, 1, 16)
            up_gate(0, 0)
            with pe.Fori(0, (ETILES - 2) // 2) as i:
                j = 2 * i
                for par in range(2):
                    up_gate(j + par + 1, 1 - par)
                    turn_hidden(j + par, par)
                    turn(j + par + 2, par, 8 * j + 32)
                    down(j + par, expert(j + par))
            up_gate(ETILES - 1, 1)
            turn_hidden(ETILES - 2, 0)
            down(ETILES - 2, expert(ETILES - 2))
            turn_hidden(ETILES - 1, 1)
            down(ETILES - 1, expert(ETILES - 1))

        def pe_weights(pe):
            pe.wait_ge(cast_done, 5)
            pe.wait_ge(img_ready, B // 2)
            pe.wait_ge(wq_ready, 3)
            for n in range(2):
                for k in range(KT):
                    for t in range(FT):
                        last = pe.transpose(psb(2 * n + k)[:, t * FP:(t + 1) * FP], raw_q[:, n, t, k * P:(k + 1) * P], identb[0:FP, 0:FP])
                    last.then_inc(wqT_ps, 1)
            for q in range(2):
                for m in range(4 * q, 4 * q + 4):
                    for k in range(KT):
                        at = (m % 4) * D + k * P
                        last = pe.transpose(psb(4 + q)[0:FP, at:at + P], raw_dq[:, k, m * FP:(m + 1) * FP], identb[:, :])
                last.then_inc(wqT_ps, 1)

        def pe_ffn(pe):
            def scales(turn, parts):
                pe.wait_ge(amax_ready, turn + 1)
                pe.transpose(ps[0:1, 7, 0:parts], amax[0:parts, :], ident[0:parts, 0:parts]).then_inc(amaxT_ps, 1)
                pe.wait_ge(scale_ready, turn + 1)
                pe.matmul(ps[:, 7, 0:2], ones, amax1[:, 1:3], start=True, stop=True).then_inc(scale_ps, 1)

            scales(0, S)
            for g in range(FG):
                pe.wait_ge(xq_ready, g + 1)
                for k in range(KT):
                    if g > 1:
                        pe.wait_ge(xqT_ready, KT * (g - 2) + k + 1)
                    for r in range(4):
                        last = pe.transpose(psb(2 * (g % 2) + k)[:, r * S4:r * S4 + S], xqb[g % 2][:, r, k * P:(k + 1) * P], identb[0:S, 0:S])
                    last.then_inc(xqT_ps, 1)
            pe.wait_ge(xqT_ready, KT * FG)
            with pe.Fori(0, FG) as g:
                for m in range(FT):
                    par = m % 2
                    pe.wait_ge(hid_ready, g * FT + m + 1)
                    for bank, w, done in ((2 + 2 * par, gq, fgate_ps), (3 + 2 * par, uq, fup_ps)):
                        for k in range(KT):
                            last = pe.matmul(ps[0:FP, bank, 0:4 * S], w[:, k, m * FP:(m + 1) * FP], xqT[:, k, bass.ds(g * 4 * S, 4 * S)],
                                             start=k == 0, stop=k == KT - 1)
                        last.then_inc(done, 1)
            scales(1, FP)
            pe.wait_ge(dscale_ready, KT)
            for k in range(KT):
                last = pe.matmul(ps[:, 6, k * P:(k + 1) * P], onesf[:, :], diag_d[:, k, :], start=True, stop=True, skip_group_check=True)
            last.then_inc(dscaleT_ps, 1)
            for b in range(B):
                pe.wait_ge((hq_even, hq_odd)[b // 2 % 2], b // 4 + 1)
                if b >= 4:
                    pe.wait_ge(fy_ready, b - 3)
                for m in range(FT):
                    last = pe.matmul(ps[0:S, b % 4, 0:D], hq[:, m, b * S:(b + 1) * S], dq[:, m, :], start=m == 0, stop=m == FT - 1)
                last.then_inc(fdown_ps, 1)

        def pe_ssm(pe):
            def turn(g):
                pe.wait_ge(xn3_ready, GB * g + GB)
                for k in range(KT):
                    for r in range(GB):
                        last = pe.transpose(ps[:, 0, k * N + r * S:k * N + (r + 1) * S], xn3[r][:, k * P:(k + 1) * P], ident[0:S, 0:S])
                last.then_inc(x3T_ps, 1)

            def project_in(g, par, half):
                pe.wait_ge(x3T_ready, g + 1)
                for m in range(half * KT, half * KT + KT):
                    for k in range(KT):
                        last = pe.matmul(ps[:, 1 - m // KT, m % KT * N:(m % KT + 1) * N], in_w[:, k, m * P:(m + 1) * P], x3T[par][:, k, :],
                                         start=k == 0, stop=k == KT - 1, skip_group_check=True)
                    if m % KT == KT - 1:
                        last.then_inc((xin_ps, res_ps)[m // KT], 1)

            def convolve(g):
                pe.wait_ge(xpad_ready, KT * g + KT)
                for m in range(KT):
                    for t in range(TAPS):
                        last = pe.matmul(ps[:, 1, m * N:(m + 1) * N], conv_diag[:, m, t, :], xpad[:, m, :, t:t + S],
                                         start=t == 0, stop=t == TAPS - 1, skip_group_check=True)
                last.then_inc(conv_ps, 1)

            def project_x(g, par):
                pe.wait_ge(xc_ready, KT * g + KT)
                pe.wait_ge(res_ready, KT * g + KT)
                for w, rows, at in ((rank_w, RANK, 0), (bc_w, 96, N)):
                    for k in range(KT):
                        last = pe.matmul(ps[0:rows, 0, at:at + N], w[:, k, :], xc[par][:, k, :], start=k == 0, stop=k == KT - 1,
                                         skip_group_check=True)
                last.then_inc(proj_ps, 1)

            def project_dt(g):
                pe.wait_ge(proj_ready, 4 * g + 1)
                for m in range(KT):
                    last = pe.matmul(ps[:, 1, m * N:(m + 1) * N], dt_w[:, m * P:(m + 1) * P], rankT, start=True, stop=True, skip_group_check=True)
                last.then_inc(dt_ps, 1)

            def spread(g, c, par):
                k, kp = g * CHUNKS + c, c % 2
                if c == 0:
                    pe.wait_ge(bc3_ready, 2 * g + 2)
                    pe.wait_ge(proj_ready, 4 * g + 4)
                pe.wait_ge(drive_ready, k + 1)
                for n in range(2):
                    last = pe.matmul(ps[:, 2 + kp, n * N:(n + 1) * N], pick[:, 2 * c + n, :], bc3[par], start=True, stop=True, skip_group_check=True)
                last.then_inc(b_ps, 1)
                pe.wait_ge(c_ready, k + 1)
                for n in range(2):
                    last = pe.matmul(ps[:, 4 + kp, n * N:(n + 1) * N], pick[:, STATES + 2 * c + n, :], bc3[par], start=True, stop=True,
                                     skip_group_check=True)
                last.then_inc(c_ps, 1)

            def reduce(g, c, par):
                k, kp = g * CHUNKS + c, c % 2
                if c == 0:
                    pe.wait_ge(yT_ready, g + 1)
                pe.wait_ge(read_ready, k + 3)
                for n in range(2):
                    last = pe.matmul(ps[:, 6, 0:KT * N], ident, read[kp][:, n].rearrange("p k s -> p (k s)"), start=c == 0 and n == 0,
                                     stop=False, skip_group_check=True)
                last.then_inc(read_used, 1)
                if c == CHUNKS - 1:
                    for m in range(KT):
                        last = pe.matmul(ps[:, 6, m * N:(m + 1) * N], d_diag[:, m, :], xc[par][:, m, :], start=False, stop=True,
                                         skip_group_check=True)
                    last.then_inc(y_ps, 1)

            def skip(g, par):
                for r in range(GB):
                    for k in range(KT):
                        pe.matmul(ps[0:S, 7, r * D:(r + 1) * D], x3T[par][:, k, r * S:(r + 1) * S], skip_w[:, k, :], start=r == 0 and k == 0,
                                  stop=False, skip_group_check=True)
                    pe.matmul(ps[0:S, 7, r * D:(r + 1) * D], ones2[:, 0:S], outskip_b, start=False, stop=False, skip_group_check=True)

            def project_out(g):
                pe.wait_ge(yT_ready, g + 2)
                for r in range(GB):
                    for k in range(KT):
                        last = pe.matmul(ps[0:S, 7, r * D:(r + 1) * D], yT[:, k, r * S:(r + 1) * S], out_w[:, k, :], start=False,
                                         stop=k == KT - 1, skip_group_check=True)
                last.then_inc(ssm_ps, 1)

            def step(g, par, more=True, before=True, turn_next=True):
                for c in range(CHUNKS):
                    if c < CHUNKS - 1:
                        spread(g, c + 1, par)
                    elif more:
                        spread(g + 1, 0, 1 - par)
                    if more:
                        if c in (0, 1):
                            project_in(g + 1, 1 - par, c)
                        if c == 2:
                            convolve(g + 1)
                        if c == 5:
                            project_dt(g + 1)
                    if turn_next and c == CHUNKS - 1:
                        turn(g + 2)
                    if c > 0:
                        reduce(g, c - 1, par)
                    elif before:
                        reduce(g - 1, CHUNKS - 1, 1 - par)
                    if before and c == 1:
                        project_out(g - 1)
                    if more and c == 4:
                        project_x(g + 1, 1 - par)
                    if c == 6:
                        if before:
                            pe.wait_ge(resid3_ready, g)
                        skip(g, par)

            pe.wait_ge(diag_done, KT * (TAPS + 1))
            pe.wait_ge(pick_done, 1)
            turn(0)
            project_in(0, 0, 0)
            project_in(0, 0, 1)
            convolve(0)
            project_x(0, 0)
            project_dt(0)
            turn(1)
            spread(0, 0, 0)
            step(0, 0, before=False)
            with pe.Fori(0, (GROUPS - 4) // 2) as i:
                for half in range(2):
                    step(2 * i + 1 + half, 1 - half)
            step(GROUPS - 3, 1)
            step(GROUPS - 2, 0, turn_next=False)
            step(GROUPS - 1, 1, more=False, turn_next=False)
            reduce(GROUPS - 1, CHUNKS - 1, 1)
            project_out(GROUPS - 1)

        @block.tensor
        def _(pe):
            pe_tokens(pe)
            pe_weights(pe)
            pe_attention(pe)
            pe_router(pe)
            pe_shared(pe)
            pe_experts(pe)
            pe_ssm(pe)
            pe_ffn(pe)


def _constants():
    c = np.zeros((P, NCONST), np.float32)
    c[:, C_ID:C_ID + P] = np.eye(P)
    q, k = np.arange(S)[:, None], np.arange(S)[None, :]
    c[:S, C_MQ:C_MQ + S] = np.where(k > q, NEG, 0.0)
    c[:S, C_MK:C_MK + S] = np.where(k < q, NEG, 0.0)
    c[:S, C_UP:C_UP + S] = k > q
    c[:, C_REP:C_REP + 32] = np.tile(np.eye(32), (4, 1))
    c[:, C_E8:C_E8 + EXPERTS] = np.arange(EXPERTS) - EXPERTS
    c[:, C_K128:C_K128 + NK128] = ETILE * np.arange(NK128)
    c[:, C_TILE:C_TILE + ETILES] = np.arange(ETILES)
    c[:, C_RES:C_RES + EXPERTS * B] = np.arange(EXPERTS * B) % B > 0
    c[:, C_RES8:C_RES8 + EXPERTS] = 1.0
    return c


def _tiles(w, parts=P):
    return np.ascontiguousarray(w.reshape(-1, parts, w.shape[-1]).transpose(1, 0, 2))


def _layout(x, n):
    a = {}
    img = np.asarray(x["x"])
    a["patches"] = _tiles(np.ascontiguousarray(img.reshape(B, 6, 16, 6, 16, 3).transpose(2, 4, 5, 0, 1, 3)).reshape(PATCH, B * IMG))
    a["tok_w"] = _tiles(n["L0_tok_W_proj"].T)
    a["tok_b"] = n["L0_tok_b_proj"].reshape(KT, P).T
    a["pos"] = _tiles(n["L0_tok_pos_emb"].T)
    a["txt"] = n["txt"]
    qkv, qkv_b = n["L0_attn_qkv_w"], n["L0_attn_qkv_b"]
    a["qk_w"] = _tiles(qkv[:, :2 * D]).reshape(P, KT, 2 * KT, P)
    a["qk_b"] = qkv_b[:2 * D].reshape(2 * KT, P).T
    a["v_w"], a["v_b"] = _tiles(qkv[:, 2 * D:]), qkv_b[None, 2 * D:]
    ow = np.zeros((4, 32, QUADS, D), np.float32)
    ow[:, :HD] = n["L0_attn_out_w"].reshape(QUADS, 4, HD, D).transpose(1, 2, 0, 3)
    a["o_w"], a["o_b"] = ow.reshape(P, QUADS, D), n["L0_attn_out_b"][None]
    row, col = np.arange(P)[:, None], np.arange(P)[None, :]
    a["sum_pick"] = (row == col // 32 * 32 + HD).astype(np.float32)
    a["head_mask"] = (row // HD == np.arange(HT8)[None, :]).astype(np.float32)
    a["router_w"] = _tiles(n["L0_ffn_router"].T)

    def expert(gate, up, down):
        return np.concatenate([_tiles(w.T).reshape(P, -1) for w in (up, gate, down)], axis=1)

    a["sh_w"] = expert(n["L0_ffn_w_gate_s"], n["L0_ffn_w_up_s"], n["L0_ffn_w_down_s"])
    a["ex_w"] = np.stack([expert(n["L0_ffn_gate"][e], n["L0_ffn_up"][e], n["L0_ffn_down"][e]) for e in range(EXPERTS)])
    m = {k: n["L1_attn_" + k] for k in ("in_proj_w", "in_proj_b", "conv_w", "conv_b", "x_proj_w", "x_proj_b", "dt_proj_w",
                                        "dt_proj_b", "A_log", "D_param", "out_proj_w", "out_proj_b", "skip_proj_w", "skip_proj_b")}
    a["in_w"], a["in_b"] = _tiles(m["in_proj_w"].T), m["in_proj_b"].reshape(2 * KT, P).T
    a["conv_w"] = m["conv_w"].reshape(KT, P, TAPS).transpose(1, 0, 2)
    a["conv_b"] = m["conv_b"].reshape(KT, P).T
    a["rank_w"], a["rank_b"] = _tiles(m["x_proj_w"][:RANK].T), m["x_proj_b"][:RANK, None]
    a["bc_w"] = _tiles(np.tile(m["x_proj_w"][RANK:], (3, 1)).T)
    a["bc_b"] = np.tile(m["x_proj_b"][RANK:], 3)[:, None]
    a["dt_w"], a["dt_b"] = m["dt_proj_w"].T, m["dt_proj_b"].reshape(KT, P).T
    a["a_log"], a["d_par"] = m["A_log"], m["D_param"].reshape(KT, P).T
    a["out_w"], a["skip_w"] = _tiles(m["out_proj_w"].T), _tiles(m["skip_proj_w"].T)
    a["outskip_b"] = np.stack([m["out_proj_b"], m["skip_proj_b"]])
    a["f_gate"] = n["L1_ffn_w_gate"].reshape(FT, FP, D).transpose(1, 0, 2)
    a["f_up"] = n["L1_ffn_w_up"].reshape(FT, FP, D).transpose(1, 0, 2)
    a["f_down"] = _tiles(n["L1_ffn_w_down"])
    a["clip_x"], a["clip_h"] = n["L1_ffn_clip_x"][None], n["L1_ffn_clip_down"][None]
    a["const"] = _constants()
    return {k: np.ascontiguousarray(v) for k, v in a.items()}


def kernel(**inputs):
    import concourse.bacc as bacc
    from concourse.bass_utils import run_bass_kernel_spmd

    given = {k: np.asarray(v) for k, v in inputs.items()}
    arrays = _layout(given, given)
    nc = bacc.Bacc("TRN2", target_bir_lowering=False, num_devices=1)
    a = {k: nc.dram_tensor("in_" + k, v.shape, mybir.dt.from_np(v.dtype), kind="ExternalInput").ap() for k, v in arrays.items()}
    out = nc.dram_tensor("out", (B, S, D), F32, kind="ExternalOutput").ap()
    build(nc, a, out)
    result = run_bass_kernel_spmd(nc, [{"in_" + k: v for k, v in arrays.items()}], core_ids=[0])
    return result.results[0]["out"]
```

```python
from contextlib import ExitStack

import numpy as np
import concourse.bass as bass
from concourse import mybir

F32 = mybir.dt.float32
BF16 = mybir.dt.bfloat16
I32 = mybir.dt.int32
ALU = mybir.AluOpType
ACT = mybir.ActivationFunctionType
AX = mybir.AxisListType

P = 128
B, IMG, TXT, D = 16, 36, 77, 256
S = IMG + TXT
T = B * S
KT = D // P
PATCH = 768
PK = PATCH // P
HEADS, HD = 16, 16
QUADS = HEADS // 4
HT8 = P // HD
EXPERTS, HID = 8, 512
HT = HID // P
EPS = 1e-5
LN_OPS, LN_VAR = 11, 7
CHOICE_OPS = 6
WORK = 9472
NEG = -1e30
UP, GATE, DOWN, EW = 0, KT * HID, 2 * KT * HID, 2 * KT * HID + HT * D
STATES, TAPS, RANK = 16, 4, 64
GB = 2
GROUPS = B // GB
N = GB * S
CHUNKS = STATES // 2
FFN, FT, FP = 704, 8, 88
QMAX = 127.0
ROUND = 1.5 * 2.0 ** 23
S4 = S + S % 2
PAIRED = (6, 7)
AT_CONV, AT_SILU, AT_RANK, AT_RANK_OUT, AT_DT, AT_SOFTPLUS, AT_STEPS = 0, 2, 2, 3, 3, 4, 5
AT_GATE, AT_OUT, AT_RESID = 0, 1, 2
AT_NORMALISE, AT_TURN, AT_IN, AT_PAD = 4, 5, 6, 7
OPENING = 1
AT_SKIP = 4
FIRST_SEQS, OTHER_SEQS = slice(0, 2 * GB), slice(2 * GB, B)
BUT_ONE_SEQS, ONE_SEQ = slice(0, B - 1), slice(B - 1, B)
ROUTER_BANKS = (0, 1, 3, 4)
TAIL_SEQS = 4
EARLY_SEQS, LAST_SEQS = slice(0, B - GB), slice(B - GB, B)
FG = 4
ETILE = 128
ETILES = (T + EXPERTS * (ETILE - 1)) // ETILE
SLOTS = ETILES * ETILE

C_ID, C_MQ, C_MK, C_UP = 0, 128, 128 + S, 128 + 2 * S
C_REP = C_UP + S
C_E8 = C_REP + 32
C_K128 = C_E8 + EXPERTS
NK128 = (T + ETILE - 1) // ETILE
C_TILE = C_K128 + NK128
C_RES = C_TILE + ETILES
C_RES8 = C_RES + EXPERTS * B
NCONST = C_RES8 + EXPERTS


class Seq:

    def __init__(self, eng, sem, base=0):
        self.eng, self.sem, self.base, self.n = eng, sem, base, 0

    def done(self, instruction):
        instruction.then_inc(self.sem, 1)
        self.n += 1

    def wait(self):
        self.eng.wait_ge(self.sem, self.base + self.n)

    def step(self, instruction):
        self.done(instruction)
        self.wait()


def build(nc, a, out):
    ctx = ExitStack()
    with ctx:
        def sb(name, shape, dt=F32):
            return ctx.enter_context(nc.sbuf_tensor(name, shape, dt))

        def sem(name):
            return ctx.enter_context(nc.semaphore(name))

        ps = ctx.enter_context(nc.psum_tensor("ps", [P, 8, 512], F32))

        resid = sb("resid", [S, B, D])
        const = sb("const", [P, NCONST])
        identb = sb("identb", [P, P], BF16)
        mask_q = sb("mask_q", [S, S], BF16)
        mask_k = sb("mask_k", [S, S], BF16)
        ones2 = sb("ones2", [2, P])
        ones = ones2[0:1, :]
        onesf = sb("onesf", [P, P])
        round_at = sb("round_at", [P, 2])
        stats = sb("stats", [S, B, 6])
        lnt = sb("lnt", [S, 6, B])
        mean = sb("mean", [S, B])
        rstd = sb("rstd", [S, B])
        arena = sb("arena", [P, EXPERTS * EW])
        work = sb("work", [P, WORK])
        ident = const[:, C_ID:C_ID + P]

        def psb(bank):
            return ps[:, bank, :].bitcast(BF16)

        def view(store, at, shape, parts=P):
            n = int(np.prod(shape))
            v = store[0:parts, at:at + n]
            if len(shape) > 1:
                names = "abcd"[:len(shape)]
                v = v.rearrange(f"p ({' '.join(names)}) -> p {' '.join(names)}", **{k: s for k, s in zip(names[1:], shape[1:])})
            return v

        class Place:
            def __init__(self, store, at=0):
                self.store, self.at = store, at

            def take(self, shape, parts=P):
                v = view(self.store, self.at, shape, parts)
                self.at += int(np.prod(shape))
                assert self.at <= self.store.shape[1], self.at
                return v

        pl = Place(arena)
        patches = pl.take((PK, B * IMG))
        tok_w = pl.take((PK, D))
        tok_bias = pl.take((KT,))
        pos = pl.take((KT, IMG))
        tokT = pl.take((KT, B * IMG))
        pl = Place(work)
        qk_w = pl.take((KT, 2 * KT, P))
        qk_b = pl.take((2 * KT,))
        v_w = pl.take((KT, D))
        v_b = pl.take((D,), S)
        o_w = pl.take((QUADS, D))
        o_b = pl.take((D,), S)
        head_mask = pl.take((HT8,))
        sum_pick = pl.take((P,))
        max_pick = pl.take((HEADS * P // 2,), 96).bitcast(BF16).rearrange("p (h m) -> p h m", h=HEADS)
        xn = pl.take((D,), S)
        xT = pl.take((KT, S))
        qkT = pl.take((2 * KT, S))
        negmax = pl.take((3, 32), S)
        nm_rest = pl.take((S,), 96)
        nm_hi = pl.take((S4 // 2,), 96).bitcast(BF16)[:, 0:S]
        nm_mid = pl.take((S4 // 2,), 96).bitcast(BF16)[:, 0:S]
        nm3 = pl.take((S4 // 2,), 96).bitcast(BF16)[:, 0:S]
        vh = pl.take((HEADS, 32), S)
        probs = pl.take((QUADS, 4, S), S)
        attn = pl.take((QUADS, S))
        rsum = pl.take((QUADS, S))
        assert pl.at <= WORK - D
        zero = view(work, WORK - D, (D,))

        sh_w = sb("sh_w", [P, EW])
        xn2 = sb("xn2", [S, B, D])
        xT2_flat = sb("xT2", [P, KT * T])
        xT2 = xT2_flat[:, :].rearrange("p (k t) -> p k t", k=KT)
        qz = view(xT2_flat, 0, (HEADS, S))
        kz = view(xT2_flat, HEADS * S, (HEADS, S))
        pl = Place(work)
        router_w = sb("router_w", [P, KT, EXPERTS])
        logits = pl.take((B, EXPERTS), S)
        rtop = pl.take((B, 1), S)
        rpick = pl.take((B, EXPERTS), S)
        chosen = pl.take((B, EXPERTS), S)
        prefix = pl.take((B, EXPERTS), S)
        total = pl.take((EXPERTS, B), S)
        summed = pl.take((EXPERTS, B), S)
        etiles = pl.take((EXPERTS, NK128), S)
        ecount = pl.take((EXPERTS,), S)
        esum = pl.take((EXPERTS,), S)
        ebase = pl.take((EXPERTS,), S)
        tile_ge = pl.take((ETILES, EXPERTS), S)
        tile_e = pl.take((ETILES,), S)
        slotf = pl.take((B,), S)
        s_gate = pl.take((2, 4 * S))
        raw_d = view(work, pl.at, (KT, FFN))
        s_hT = pl.take((HT, 4 * S))
        chosenb = sb("chosenb", [S, B, EXPERTS], BF16)
        upperb = sb("upperb", [S, S], BF16)
        onesb = sb("onesb", [S, S], BF16)
        slot = sb("slot", [S, B], I32)
        tile_expert = sb("tile_expert", [1, ETILES], I32)
        xg = [pl.take((D,)) for _ in range(2)]
        xgT = [pl.take((KT, ETILE)) for _ in range(2)]
        e_gate = [pl.take((HID,)) for _ in range(2)]
        e_h = [pl.take((HID,)) for _ in range(2)]
        e_hT = pl.take((HT, ETILE))
        e_y = [pl.take((D,)) for _ in range(2)]
        w_int = [pl.take((D // 2,), 88).bitcast(BF16) for _ in range(2)]
        slots_in = nc.dram_tensor("slots_in", (SLOTS, D), F32).ap()
        slots_out = nc.dram_tensor("slots_out", (SLOTS, D), F32).ap()

        pl = Place(sh_w)
        in_w = pl.take((KT, 2 * D))
        in_b = pl.take((2 * KT,))
        conv_w = pl.take((KT, TAPS))
        conv_b = pl.take((KT,))
        rank_w = pl.take((KT, RANK))
        rank_b = pl.take((1,), RANK)
        bc_w = pl.take((KT, 96))
        bc_b = pl.take((1,), 96)
        dt_w = pl.take((D,), RANK)
        dt_b = pl.take((KT,))
        a_neg = pl.take((STATES,))
        d_par = pl.take((KT,))
        out_w = pl.take((KT, D))
        skip_w = pl.take((KT, D))
        outskip_b = pl.take((D,), 2)
        pl = Place(xT2_flat)
        conv_diag = pl.take((KT, TAPS, P))
        d_diag = pl.take((KT, P))
        pick = pl.take((32 * P // 2,), 96).bitcast(BF16).rearrange("p (j m) -> p j m", j=32)
        pl = Place(arena)
        xn3 = [pl.take((D,), S) for _ in range(GB)]
        x3T = [pl.take((KT, N)) for _ in range(2)]
        xpad = pl.take((KT, GB, TAPS - 1 + S))
        silu_res = [pl.take((KT, N)) for _ in range(2)]
        xc = [pl.take((KT, N)) for _ in range(2)]
        rankT = pl.take((N,), RANK)
        bc = pl.take((N,), 96)
        bc_rest = pl.take((N,), 96)
        bc_hi = pl.take((N // 2,), 96).bitcast(BF16)
        bc_mid = pl.take((N // 2,), 96).bitcast(BF16)
        bc3 = [pl.take((N // 2,), 96).bitcast(BF16) for _ in range(2)]
        sp_abs = pl.take((KT, N))
        sp_relu = pl.take((KT, N))
        delta = [pl.take((KT, N)) for _ in range(2)]
        dx = [pl.take((KT, N)) for _ in range(2)]
        decay = [pl.take((2, KT * GB, S)) for _ in range(2)]
        drive = [pl.take((2, KT, N)) for _ in range(2)]
        state = [pl.take((2, KT, N)) for _ in range(2)]
        c_sb = [pl.take((2, N)) for _ in range(2)]
        read = [pl.take((2, KT, N)) for _ in range(2)]
        yT = pl.take((KT, N))

        guq = sb("guq", [P, KT, 2 * FFN], BF16)
        gq, uq = guq[:, :, 0:FFN], guq[:, :, FFN:2 * FFN]
        dq = sb("dq", [FP, FT, D], BF16)
        wscale = sb("wscale", [P, 3, FT])
        winv = sb("winv", [P, 2 * FT])
        clips = sb("clips", [P, 2])
        clip_sig = sb("clip_sig", [P, 2])
        raw_gu = xn2[0:FP, :, :]
        pl = Place(arena)
        hid = pl.take((FT, T), FP)
        f_gate = [pl.take((FG * S,), FP) for _ in range(4)]
        f_up = [pl.take((FG * S,), FP) for _ in range(2)]
        fmax = pl.take((FT * FG,), FP)
        amax = pl.take((1,))
        amax1 = pl.take((4,), 1)
        xscale = pl.take((2,))
        hscale = pl.take((2,))
        gscale = pl.take((FT,), FP)
        uscale = pl.take((FT,), FP)
        dscale = pl.take((D,))
        dcol = pl.take((KT,))
        diag_d = pl.take((KT, P))
        answer_f = [pl.take((D,), S) for _ in range(2)]
        xqf = [pl.take((4, D), S) for _ in range(2)]
        xqb = [pl.take((4 * D // 2,), S).bitcast(BF16).rearrange("p (b d) -> p b d", b=4) for _ in range(2)]
        xqT = pl.take((KT * T // 2,)).bitcast(BF16).rearrange("p (k t) -> p k t", k=KT)
        pl4 = Place(work)
        hq = pl4.take((FT * T // 2,), FP).bitcast(BF16).rearrange("p (m t) -> p m t", m=FT)

        const_in, tok_in, txt_in, attn_in = sem("const_in"), sem("tok_in"), sem("txt_in"), sem("attn_in")
        cast_done, posb_done, pool_set = sem("cast_done"), sem("posb_done"), sem("pool_set")
        tok_ps, tokT_ready, tokback_ps, img_ready = sem("tok_ps"), sem("tokT_ready"), sem("tokback_ps"), sem("img_ready")
        stats_done, dve_ln, act_ln = sem("stats_done"), sem("dve_ln"), sem("act_ln")
        xn_ready, xnT_ps, xT_ready = sem("xn_ready"), sem("xnT_ps"), sem("xT_ready")
        qk_ps, qk_ready, v_ps, v_ready = sem("qk_ps"), sem("qk_ready"), sem("v_ps"), sem("v_ready")
        score_ps, negmax_ready, nmT_ps = sem("score_ps"), sem("negmax_ready"), sem("nmT_ps")
        scoreT_ps, probs_ready, av_ps = sem("scoreT_ps"), sem("probs_ready"), sem("av_ps")
        attn_copied, sums_ps, rsum_ready, attn_ready = sem("attn_copied"), sem("sums_ps"), sem("rsum_ready"), sem("attn_ready")
        oproj_ps, resid1_ready, bias_added, negmax3_ready = sem("oproj_ps"), sem("resid1_ready"), sem("bias_added"), sem("negmax3_ready")
        kz_ready, qz_ready, nm_hi_ready, nm_step, nm3_ready, pick2_done = (sem("kz_ready"), sem("qz_ready"), sem("nm_hi_ready"),
                                                                         sem("nm_step"), sem("nm3_ready"), sem("pick2_done"))
        out_done = sem("out_done")
        moe_in, experts_in, zero_set, slots_zeroed = sem("moe_in"), sem("experts_in"), sem("zero_set"), sem("slots_zeroed")
        xn2_ready, xn2T_ps, xT2_ready = sem("xn2_ready"), sem("xn2T_ps"), sem("xT2_ready")
        logits_ps, route, chosen_ready, counts_ps, slots_ready = (sem("logits_ps"), sem("route"), sem("chosen_ready"),
                                                                 sem("counts_ps"), sem("slots_ready"))
        sgate_ps, sup_ps, sgate_ready, sh_ready = sem("sgate_ps"), sem("sup_ps"), sem("sgate_ready"), sem("sh_ready")
        sdown_ps, sresid_ready = sem("sdown_ps"), sem("sresid_ready")
        scattered, xg_in, xgT_ps, xgT_ready = sem("scattered"), [sem("xg_in0"), sem("xg_in1")], sem("xgT_ps"), sem("xgT_ready")
        egate_ps, eup_ps, egate_ready, eh_ready = sem("egate_ps"), sem("eup_ps"), sem("egate_ready"), sem("eh_ready")
        ehT_ps, ehT_ready, ey_ps, ey_ready, ey_out = (sem("ehT_ps"), sem("ehT_ready"), sem("ey_ps"), sem("ey_ready"),
                                                     [sem("ey_out0"), sem("ey_out1")])
        ssm_in, aneg_done, diag_done, pick_done, pads_zero = (sem("ssm_in"), sem("aneg_done"), sem("diag_done"), sem("pick_done"),
                                                             sem("pads_zero"))
        xn3_ready, x3T_ps, x3T_ready, xin_ps, res_ps = sem("xn3_ready"), sem("x3T_ps"), sem("x3T_ready"), sem("xin_ps"), sem("res_ps")
        xpad_ready, res_ready, conv_ps, xc_ready = sem("xpad_ready"), sem("res_ready"), sem("conv_ps"), sem("xc_ready")
        proj_ps, proj_ready, dt_ps, softplus_ready = sem("proj_ps"), sem("proj_ready"), sem("dt_ps"), sem("softplus_ready")
        sp_step, bc_step, bc3_ready, delta_ready, dx_ready = (sem("sp_step"), sem("bc_step"), sem("bc3_ready"), sem("delta_ready"),
                                                              sem("dx_ready"))
        b_ps, c_ps, decay_ready, c_ready = sem("b_ps"), sem("c_ps"), sem("decay_ready"), sem("c_ready")
        drive_ready, state_ready, read_ready, read_used = sem("drive_ready"), sem("state_ready"), sem("read_ready"), sem("read_used")
        y_ps, yT_ready, ssm_ps, resid3_ready = sem("y_ps"), sem("yT_ready"), sem("ssm_ps"), sem("resid3_ready")
        pair_ready = sem("pair_ready")
        patch_in = [sem(f"patch_in{n}") for n in range(PK // 2)]
        clip_in, ffn_d_in = sem("clip_in"), sem("ffn_d_in")
        ffn_in, wq_step, wq_ready, wqT_ps, wqT_ready = sem("ffn_in"), sem("wq_step"), sem("wq_ready"), sem("wqT_ps"), sem("wqT_ready")
        f_step, xn4_ready, amax_ready, amaxT_ps, scale_ready, scale_ps = (sem("f_step"), sem("xn4_ready"), sem("amax_ready"),
                                                                      sem("amaxT_ps"), sem("scale_ready"), sem("scale_ps"))
        dscale_ready, dscaleT_ps, clip_exp = sem("dscale_ready"), sem("dscaleT_ps"), sem("clip_exp")
        xq_ready, xqT_ps, xqT_ready = sem("xq_ready"), sem("xqT_ps"), sem("xqT_ready")
        fgate_ps, fup_ps, fgate_ready = sem("fgate_ps"), sem("fup_ps"), sem("fgate_ready")
        hid_even, hid_odd, fup_ready = sem("hid_even"), sem("hid_odd"), sem("fup_ready")
        hmax_ready, hq_even, hq_odd, fdown_ps, fy_ready, final_ready = (sem("hmax_ready"), sem("hq_even"), sem("hq_odd"),
                                                                     sem("fdown_ps"), sem("fy_ready"), sem("final_ready"))
        fscale_ready = sem("fscale_ready")
        xmax_ready, xround, xclip, hround, hclip = sem("xmax_ready"), sem("xround"), sem("xclip"), sem("hround"), sem("hclip")
        gathered, resid2_ready = [sem(f"gathered{n}") for n in range(B // 4)], sem("resid2_ready")

        block = ctx.enter_context(nc.Block())

        @block.sync
        def _(sp):
            for part in range(PK // 2):
                k = slice(2 * part, 2 * part + 2)
                sp.dma_start(tok_w[:, k, :], a["tok_w"][:, k, :]).then_inc(patch_in[part], 16)
                sp.dma_start(patches[:, k, :], a["patches"][:, k, :]).then_inc(patch_in[part], 16)
            sp.dma_start(tok_bias, a["tok_b"]).then_inc(tok_in, 16)
            sp.dma_start(pos, a["pos"]).then_inc(tok_in, 16)
            sp.dma_start(const[:, :], a["const"]).then_inc(const_in, 16)
            sp.dma_start(resid[IMG:S, :, :], a["txt"].rearrange("b s d -> s b d")).then_inc(txt_in, 16)
            for dst, name in ((qk_w, "qk_w"), (qk_b, "qk_b"), (v_w, "v_w"), (o_w, "o_w"), (sum_pick, "sum_pick"), (head_mask, "head_mask")):
                sp.dma_start(dst, a[name]).then_inc(attn_in, 16)
            for dst, name in ((v_b, "v_b"), (o_b, "o_b")):
                sp.dma_start(dst, a[name].broadcast_to([S, D])).then_inc(attn_in, 16)
            for c, name in enumerate(("clip_x", "clip_h")):
                sp.dma_start(clips[:, c:c + 1], a[name].broadcast_to([P, 1])).then_inc(clip_in, 16)
            for dst, name in ((router_w[:, :, :], "router_w"), (sh_w[:, :], "sh_w")):
                sp.dma_start(dst, a[name]).then_inc(moe_in, 16)
            sp.wait_ge(zero_set, 1)
            sp.dma_start(slots_in.rearrange("(t p) d -> p t d", p=P),
                         zero.unsqueeze(1).broadcast_to([P, ETILES, D])).then_inc(slots_zeroed, 16)
            sp.wait_ge(tokback_ps, B // 2)
            for e in range(EXPERTS):
                sp.dma_start(arena[:, e * EW:(e + 1) * EW], a["ex_w"][e]).then_inc(experts_in, 16)
            sp.wait_ge(scattered, 16 * B)

            def load_tile(j, par, first):
                if not first:
                    sp.wait_ge(xgT_ps, j - 1)
                sp.dma_start(xg[par], slots_in[bass.ds(j * ETILE, ETILE), :]).then_inc(xg_in[par], 16)

            def store_tile(j, par):
                sp.wait_ge(ey_ready, j + 2)
                sp.dma_start(slots_out[bass.ds(j * ETILE, ETILE), :], e_y[par]).then_inc(ey_out[par], 16)

            load_tile(0, 0, True)
            load_tile(1, 1, True)
            for n, name in enumerate(("f_gate", "f_up")):
                sp.dma_start(raw_gu[:, n * FT:(n + 1) * FT, :], a[name]).then_inc(ffn_in, 16)
            sp.wait_ge(sdown_ps, 8)
            for dst, name in ((in_w, "in_w"), (in_b, "in_b"), (conv_w, "conv_w"), (conv_b, "conv_b"), (rank_w, "rank_w"),
                              (rank_b, "rank_b"), (bc_w, "bc_w"), (bc_b, "bc_b"), (dt_w, "dt_w"), (dt_b, "dt_b"),
                              (d_par, "d_par"), (out_w, "out_w"), (skip_w, "skip_w"), (outskip_b, "outskip_b")):
                sp.dma_start(dst, a[name]).then_inc(ssm_in, 16)
            sp.dma_start(raw_d, a["f_down"]).then_inc(ffn_d_in, 16)
            sp.dma_start(a_neg, a["a_log"].broadcast_to([P, STATES])).then_inc(ssm_in, 16)
            with sp.Fori(0, (ETILES - 2) // 2) as i:
                j = 2 * i
                for par in range(2):
                    load_tile(j + par + 2, par, False)
                    store_tile(j + par, par)
            for j in (ETILES - 2, ETILES - 1):
                store_tile(j, j % 2)
            for n in range(B // 2):
                sp.wait_ge(final_ready, 2 * n + 2)
                sp.dma_start(out[2 * n:2 * n + 2].rearrange("b s d -> s b d"), resid[:, 2 * n:2 * n + 2, :]).then_inc(out_done, 16)
            sp.wait_ge(out_done, 16 * B // 2)
        def pool_attention(pool):
            def spread_queries(b):
                for t in range(KT):
                    pool.wait_ge(qk_ready, 4 * b + 2 * t + 2)
                    pool.tensor_tensor(qz[:, t * HT8:(t + 1) * HT8, :], qkT[:, t, :].unsqueeze(1).broadcast_to([P, HT8, S]),
                                       head_mask.unsqueeze(2).broadcast_to([P, HT8, S]), ALU.mult).then_inc(qz_ready, 1)

            def add_bias(b):
                pool.wait_ge(xn_ready, b + 1)
                pool.wait_ge(qz_ready, 2 * b + 2)
                pool.tensor_tensor(resid[:, b, :], resid[:, b, :], o_b, ALU.add).then_inc(bias_added, 1)
                pool.wait_ge(bias_added, b + 1)

            pool.wait_ge(attn_in, 8 * 16)
            pool.wait_ge(pool_set, 6)
            with pool.Fori(0, B) as b:
                spread_queries(b)
                add_bias(b)

        def pool_ffn(pool):
            pool.sem_inc(hid_odd, 2)
            with pool.Fori(0, FG) as g:
                for m in range(1, FT, 2):
                    pool.wait_ge(fgate_ready, g * FT + m + 1)
                    pool.wait_ge(fup_ready, g * (FT // 2) + m // 2 + 3)
                    pool.tensor_tensor(hid[:, m, bass.ds(g * 4 * S, 4 * S)], f_up[m // 2 % 2], f_gate[m % 4], ALU.mult).then_inc(hid_odd, 1)
            for b in range(B):
                pool.wait_ge(fy_ready, b + 1)
                pool.tensor_tensor(resid[:, b, :], resid[:, b, :], answer_f[b % 2], ALU.add).then_inc(final_ready, 1)

        def pool_ssm(pool):
            def split(g, par):
                pool.wait_ge(proj_ready, 4 * g + 4)
                mid, low = slice(32, 64), slice(64, 96)
                pool.tensor_tensor(bc_rest[low, :], bc[low, :], bc_hi[low, :], ALU.subtract).then_inc(bc_step, 1)
                pool.tensor_tensor(bc_mid[low, :], bc[low, :], bc_hi[low, :], ALU.subtract).then_inc(bc_step, 1)
                pool.tensor_tensor(bc3[par][mid, :], bc[mid, :], bc_hi[mid, :], ALU.subtract).then_inc(bc3_ready, 1)
                pool.wait_ge(bc_step, 2 * g + 2)
                pool.tensor_tensor(bc3[par][low, :], bc_rest[low, :], bc_mid[low, :], ALU.subtract).then_inc(bc3_ready, 1)

            def step(g, par, more=True):
                for c in range(CHUNKS):
                    k = g * CHUNKS + c
                    kp = c % 2
                    if more and c == 5:
                        pool.wait_ge(read_ready, k + 2)
                        split(g + 1, 1 - par)
                        pool.wait_ge(bc3_ready, 2 * g + 4)
                    pool.wait_ge(c_ready, k + 3)
                    pool.wait_ge(state_ready, k + 3)
                    pool.wait_ge(read_used, k + 1)
                    pool.tensor_tensor(read[kp], state[kp], c_sb[kp].unsqueeze(2).broadcast_to([P, 2, KT, N]), ALU.mult)\
                        .then_inc(read_ready, 1)

            pool.wait_ge(pads_zero, 3)
            for done in gathered:
                pool.wait_ge(done, 64)
            split(0, 0)
            pool.wait_ge(bc3_ready, 2)
            step(0, 0)
            with pool.Fori(0, (GROUPS - 2) // 2) as i:
                for half in range(2):
                    step(2 * i + 1 + half, 1 - half)
            step(GROUPS - 1, 1, more=False)

        @block.gpsimd
        def _(pool):
            pool.memset(zero, 0.0).then_inc(zero_set, 1)
            pool.memset(onesf[:, :], 1.0).then_inc(pool_set, 1)
            pool.memset(round_at[:, 0:1], ROUND).then_inc(pool_set, 1)
            pool.memset(round_at[:, 1:2], -ROUND).then_inc(pool_set, 1)
            pool.memset(ones2[:, :], 1.0).then_inc(pool_set, 1)
            pool.memset(negmax, 0.0).then_inc(pool_set, 1)
            pool.memset(vh, 1.0).then_inc(pool_set, 1)

            pool_attention(pool)
            pool.wait_ge(slots_zeroed, 16)
            pool.wait_ge(slots_ready, 1)
            pool.wait_ge(xn2_ready, B)
            for b in range(B):
                pool.indirect_dma_start(slots_in, bass.IndirectOffsetOnAxis(ap=slot[:, b:b + 1], axis=0), xn2[:, b, :], None).then_inc(scattered, 16)
            pool.wait_ge(scattered, 16 * B)
            pool.wait_ge(wqT_ps, 2 * FT)
            pool.wait_ge(ey_ps, ETILES)
            pool.memset(xpad, 0.0).then_inc(pads_zero, 1)
            for d in decay:
                pool.memset(d[:, :, :, 0:1], 0.0).then_inc(pads_zero, 1)
            for par in range(2):
                pool.wait_ge(ey_out[par], 16 * (ETILES // 2))
            for b in range(B):
                pool.indirect_dma_start(xn2[:, b, :], None, slots_out,
                                        bass.IndirectOffsetOnAxis(ap=slot[:, b:b + 1], axis=0)).then_inc(gathered[b // 4], 16)
            pool_ssm(pool)
            pool_ffn(pool)

        def act_rstd(act, turn, seqs=slice(0, B), load=True):
            if load:
                act.preload_act_table_set("natural_log_exp_and_others")
            act.wait_ge(dve_ln, LN_OPS * turn + LN_VAR)
            act.activation(lnt[:, 3, seqs], lnt[:, 2, seqs], ACT.Ln).then_inc(act_ln, 1)
            act.wait_ge(act_ln, 2 * turn + 1)
            act.activation(lnt[:, 3, seqs], lnt[:, 3, seqs], ACT.Exp, scale=-0.5).then_inc(act_ln, 1)

        def act_attention(act):
            def turn_x(b):
                act.wait_ge(xnT_ps, b + 1)
                act.activation(xT, ps[:, 0, 0:KT * S].rearrange("p (k s) -> p k s", k=KT), ACT.Copy).then_inc(xT_ready, 1)

            def queries_keys(b):
                act.wait_ge(qk_ps, b + 1)
                for t in (2, 0, 3, 1):
                    act.activation(qkT[:, t, :], ps[:, 1, t * S:(t + 1) * S], ACT.Identity, bias=qk_b[:, t:t + 1]).then_inc(qk_ready, 1)

            def high_parts(b):
                act.wait_ge(nmT_ps, b + 1)
                for dst, rows in ((nm_hi, 96), (nm3, 32)):
                    act.activation(dst[0:rows, :], ps[0:rows, 7, 0:S], ACT.Copy).then_inc(nm_hi_ready, 1)

            def exps(b):
                for r in range(QUADS):
                    act.wait_ge(scoreT_ps, QUADS * b + r + 1)
                    act.activation(probs[:, r], ps[0:S, 3 + r, 0:4 * S].rearrange("p (j s) -> p j s", j=4),
                                   ACT.Exp, scale=1.0 / float(HD) ** 0.5).then_inc(probs_ready, 1)

            def outputs(b):
                act.wait_ge(av_ps, b + 1)
                act.activation(attn, ps[:, 7, 0:QUADS * S].rearrange("p (r s) -> p r s", r=QUADS), ACT.Copy).then_inc(attn_copied, 1)

            def step(b, more=True):
                high_parts(b)
                if more:
                    turn_x(b + 1)
                exps(b)
                if more:
                    queries_keys(b + 1)
                outputs(b)

            act.wait_ge(attn_in, 8 * 16)
            turn_x(0)
            queries_keys(0)
            with act.Fori(0, B - 1) as b:
                step(b)
            step(B - 1, more=False)
            act_rstd(act, 1, BUT_ONE_SEQS)

        def act_tokens(act):
            for pair in range(B // 2):
                act.wait_ge(tokback_ps, pair + 1)
                act.activation(resid[0:IMG, 2 * pair:2 * pair + 2, :],
                               ps[0:IMG, 4 + pair % 4, :].rearrange("p (b d) -> p b d", b=2), ACT.Copy).then_inc(img_ready, 1)

        def act_router(act):
            for b in range(B):
                if b == B - 1:
                    act_rstd(act, 2, ONE_SEQ, load=False)
                act.wait_ge(xn2T_ps, b + 1)
                act.activation(xT2[:, :, b * S:(b + 1) * S], ps[:, ROUTER_BANKS[b % 4], 0:KT * S].rearrange("p (k s) -> p k s", k=KT), ACT.Copy).then_inc(xT2_ready, 1)

        def act_shared(act):
            with act.Fori(0, (4 * HT) // 2) as i:
                n = 2 * i
                for par in range(2):
                    act.wait_ge(sgate_ps, n + par + 1)
                    act.wait_ge(sh_ready, n + par + 1)
                    act.activation(s_gate[:, par, :], ps[:, 3 + 2 * par, 0:4 * S], ACT.Silu).then_inc(sgate_ready, 1)

        def act_experts(act):
            def turn(j, par):
                act.wait_ge(xgT_ps, j + 1)
                act.activation(xgT[par], ps[:, 0, 0:KT * ETILE].rearrange("p (k s) -> p k s", k=KT), ACT.Copy).then_inc(xgT_ready, 1)

            def gate(j, par):
                act.wait_ge(egate_ps, j + 1)
                act.activation(e_gate[par], ps[:, 1 + 2 * par, :], ACT.Silu).then_inc(egate_ready, 1)

            def hidden(j):
                act.wait_ge(ehT_ps, j + 1)
                act.activation(e_hT, ps[:, 5, :].rearrange("p (m s) -> p m s", m=HT), ACT.Copy).then_inc(ehT_ready, 1)

            act.wait_ge(xgT_ps, 1)
            act.activation(xgT[0], ps[:, 0, 0:KT * ETILE].rearrange("p (k s) -> p k s", k=KT), ACT.Copy).then_inc(xgT_ready, 1)
            act.wait_ge(xgT_ps, 2)
            act.activation(xgT[1], ps[:, 0, 0:KT * ETILE].rearrange("p (k s) -> p k s", k=KT), ACT.Copy).then_inc(xgT_ready, 1)
            gate(0, 0)

            def step(j, par, weights):
                gate(j + 1, 1 - par)
                hidden(j)
                turn(j + 2, par)
                if weights:
                    act_weights(act, j - 4)

            for j in range(4):
                step(j, j % 2, False)
                if j == 0:
                    act.wait_ge(ssm_in, 16 * 15)
                    act.activation(a_neg, a_neg, ACT.Exp).then_inc(aneg_done, 1)
            with act.Fori(2, 2 + FT) as i:
                for par in range(2):
                    step(2 * i + par, par, True)
            gate(ETILES - 1, 1)
            hidden(ETILES - 2)
            hidden(ETILES - 1)

        def act_weights(act, w):
            act.wait_ge(wqT_ps, w + 1)
            act.activation(guq[:, :, bass.ds(w * FP, FP)], psb(7)[:, 0:KT * FP].rearrange("p (k i) -> p k i", k=KT), ACT.Copy).then_inc(wqT_ready, 1)

        def act_weights_down(act):
            for n in range(4):
                act.wait_ge(wqT_ps, 2 * FT + n + 1)
                act.activation(dq[:, 2 * n:2 * n + 2, :], ps[0:FP, 1 + n, :].rearrange("p (m d) -> p m d", m=2), ACT.Copy).then_inc(wqT_ready, 1)

        def act_ffn(act):
            act.wait_ge(fscale_ready, 1)
            act.wait_ge(xn4_ready, B)
            def round_x(g):
                if g >= 2:
                    act.wait_ge(xq_ready, g - 1)
                act.activation(xqf[g % 2], xn2[:, 4 * g:4 * g + 4, :], ACT.Identity, scale=xscale[0:S, 1:2], bias=round_at[0:S, 0:1]).then_inc(xround, 1)

            def turn_x(g):
                for k in range(KT):
                    act.wait_ge(xqT_ps, KT * g + k + 1)
                    act.activation(xqT[:, k, g * 4 * S:(g + 1) * 4 * S].rearrange("p (b s) -> p b s", b=4),
                                   psb(2 * (g % 2) + k)[:, 0:4 * S4].rearrange("p (b s) -> p b s", b=4)[:, :, 0:S], ACT.Copy).then_inc(xqT_ready, 1)

            round_x(0)
            round_x(1)
            for g in range(FG):
                if g + 2 < FG:
                    round_x(g + 2)
                turn_x(g)
            act.wait_ge(fscale_ready, 2)
            act.sem_inc(fup_ready, 2)
            with act.Fori(0, FG // 2) as turn:
                for m2 in range(2 * FT):
                    m, pair = m2 % FT, m2 % 4
                    g = turn * 2 + m2 // FT
                    before = g * (FT // 2) + m // 2 + 1
                    act.wait_ge(fgate_ps, g * FT + m + 1)
                    act.wait_ge((hid_even, hid_odd)[m % 2], before)
                    act.activation(f_gate[pair], ps[0:FP, 2 * pair, 0:4 * S], ACT.Silu, scale=gscale[:, m:m + 1]).then_inc(fgate_ready, 1)
                    if m % 2 == 1:
                        act.wait_ge(fup_ps, g * FT + m + 1)
                        act.activation(f_up[m // 2 % 2], ps[0:FP, 2 * pair + 1, 0:4 * S], ACT.Copy, scale=uscale[:, m:m + 1]).then_inc(fup_ready, 1)
            act.wait_ge(fscale_ready, 3)

            def round_hid(piece):
                h = hid[:, :, 2 * piece * S:(2 * piece + 2) * S]
                act.activation(h, h, ACT.Identity, scale=hscale[0:FP, 1:2], bias=round_at[0:FP, 0:1]).then_inc(hround, 1)

            round_hid(0)
            for piece in range(B // 2):
                if piece + 1 < B // 2:
                    round_hid(piece + 1)
                if piece % 2 == 1:
                    act.wait_ge(hclip, piece + 1)
                    cols = slice(2 * piece * S, (2 * piece + 2) * S)
                    act.activation(hq[:, :, cols], hid[:, :, cols], ACT.Identity, bias=round_at[0:FP, 1:2]).then_inc(hq_odd, 1)

        def act_ssm(act):
            def turn(g, par):
                act.wait_ge(x3T_ps, g + 1)
                act.activation(x3T[par], ps[:, 0, 0:KT * N].rearrange("p (k s) -> p k s", k=KT), ACT.Copy).then_inc(x3T_ready, 1)

            def pad(g):
                act.wait_ge(xin_ps, g + 1)
                for m in range(KT):
                    act.activation(xpad[:, m, :, TAPS - 1:], ps[:, 1, m * N:(m + 1) * N].rearrange("p (b s) -> p b s", b=GB),
                                   ACT.Identity, bias=in_b[:, m:m + 1]).then_inc(xpad_ready, 1)

            def silus(g, par, first=False):
                act.wait_ge(res_ps, g + 1)
                act.wait_ge(conv_ps, g + 1)
                if not first:
                    act.wait_ge(yT_ready, g)
                for m in range(KT):
                    act.activation(silu_res[par][:, m, :], ps[:, 0, m * N:(m + 1) * N], ACT.Silu, bias=in_b[:, KT + m:KT + m + 1])\
                        .then_inc(res_ready, 1)
                for m in range(KT):
                    act.activation(xc[par][:, m, :], ps[:, 1, m * N:(m + 1) * N], ACT.Silu, bias=conv_b[:, m:m + 1])\
                        .then_inc(xc_ready, 1)
                act.preload_act_table_set("natural_log_exp_and_others")

            def projections(g, par):
                act.wait_ge(proj_ps, g + 1)
                act.activation(rankT, ps[0:RANK, 0, 0:N], ACT.Identity, bias=rank_b).then_inc(proj_ready, 1)
                for dst, rows in ((bc, 96), (bc_hi, 96), (bc3[par], 32)):
                    act.activation(dst[0:rows, :], ps[0:rows, 0, N:2 * N], ACT.Identity, bias=bc_b[0:rows, :]).then_inc(proj_ready, 1)

            def softplus(g):
                q = Seq(act, sp_step, 5 * g)
                act.wait_ge(dt_ps, g + 1)
                for m in range(KT):
                    q.done(act.activation(sp_abs[:, m, :], ps[:, 1, m * N:(m + 1) * N], ACT.Abs, bias=dt_b[:, m:m + 1]))
                for m in range(KT):
                    q.done(act.activation(sp_relu[:, m, :], ps[:, 1, m * N:(m + 1) * N], ACT.Relu, bias=dt_b[:, m:m + 1]))
                q.wait()
                q.step(act.activation(sp_abs, sp_abs, ACT.Exp, scale=-1.0))
                act.activation(sp_abs, sp_abs, ACT.Ln, bias=1.0).then_inc(softplus_ready, 1)

            def decays(g, c, par, first=False):
                k = g * CHUNKS + c
                if c == 0:
                    act.wait_ge(delta_ready, g + 1)
                if not first:
                    act.wait_ge(state_ready, k + 1)
                for n in range(2):
                    act.activation(decay[c % 2][:, n, :, 1:], delta[par].rearrange("p k (b s) -> p (k b) s", b=GB)[:, :, 1:],
                                   ACT.Exp, scale=a_neg[:, 2 * c + n:2 * c + n + 1]).then_inc(decay_ready, 1)

            def step(g, par, more=True, before=True, turn_next=True):
                for c in range(CHUNKS):
                    k = g * CHUNKS + c
                    kp = c % 2
                    if c < CHUNKS - 1:
                        decays(g, c + 1, par)
                    elif more:
                        decays(g + 1, 0, 1 - par)
                    act.wait_ge(c_ps, k + 1)
                    act.wait_ge(read_ready, k + 1)
                    act.activation(c_sb[kp], ps[:, 4 + kp, 0:2 * N].rearrange("p (n s) -> p n s", n=2), ACT.Copy).then_inc(c_ready, 1)
                    if not before and c == OPENING:
                        pad(1)
                    if more:
                        if c == AT_SILU:
                            silus(g + 1, 1 - par)
                        if c == AT_RANK_OUT:
                            projections(g + 1, 1 - par)
                        if c == AT_SOFTPLUS:
                            softplus(g + 1)
                    elif c == 3:
                        act_rstd(act, 5, EARLY_SEQS, load=False)
                    if turn_next:
                        if c == AT_TURN:
                            turn(g + 2, par)
                        if c == AT_PAD:
                            pad(g + 2)

            act.wait_ge(pads_zero, 3)
            turn(0, 0)
            pad(0)
            silus(0, 0, first=True)
            projections(0, 0)
            act_rstd(act, 4, OTHER_SEQS, load=False)
            softplus(0)
            turn(1, 1)
            act.wait_ge(aneg_done, 2)
            decays(0, 0, 0, first=True)
            step(0, 0, before=False)
            with act.Fori(0, (GROUPS - 4) // 2) as i:
                for half in range(2):
                    step(2 * i + 1 + half, 1 - half)
            step(GROUPS - 3, 1)
            step(GROUPS - 2, 0, turn_next=False)
            step(GROUPS - 1, 1, more=False, turn_next=False)

        @block.scalar
        def _(act):
            act_tokens(act)
            act.wait_ge(clip_in, 2 * 16)
            act.activation(clip_sig[:, :], clips[:, :], ACT.Exp, scale=-1.0).then_inc(clip_exp, 1)
            act_rstd(act, 0)
            act_attention(act)
            act_router(act)
            act_shared(act)
            act_experts(act)
            act_weights_down(act)
            act_rstd(act, 3, FIRST_SEQS)
            act_ssm(act)
            act_rstd(act, 6, LAST_SEQS, load=False)
            act_ffn(act)


        def dve_layernorm(dve, turn, seqs=slice(0, B)):
            q = Seq(dve, dve_ln, LN_OPS * turn)
            me, qe, mo, qo = (stats[:, seqs, k] for k in (1, 2, 4, 5))
            q.done(dve.tensor_tensor(lnt[:, 0, seqs], me, mo, ALU.add))
            q.done(dve.tensor_tensor(lnt[:, 1, seqs], me, mo, ALU.subtract))
            q.done(dve.tensor_tensor(lnt[:, 2, seqs], qe, qo, ALU.add))
            q.wait()
            q.done(dve.tensor_scalar(mean[:, seqs], lnt[:, 0, seqs], 0.5, None, ALU.mult))
            q.done(dve.tensor_scalar(lnt[:, 2, seqs], lnt[:, 2, seqs], 1.0 / D, EPS, ALU.mult, ALU.add))
            q.step(dve.tensor_tensor(lnt[:, 1, seqs], lnt[:, 1, seqs], lnt[:, 1, seqs], ALU.mult))
            q.step(dve.scalar_tensor_tensor(out=lnt[:, 2, seqs], in0=lnt[:, 1, seqs], scalar=0.25, in1=lnt[:, 2, seqs], op0=ALU.mult, op1=ALU.add))
            assert q.n == LN_VAR
            dve.wait_ge(act_ln, 2 * turn + 2)
            y, v, t = lnt[:, 3, seqs], lnt[:, 2, seqs], lnt[:, 4, seqs]
            q.step(dve.tensor_tensor(t, y, y, ALU.mult))
            q.step(dve.tensor_tensor(t, t, v, ALU.mult))
            q.step(dve.tensor_scalar(t, t, -0.5, 1.5, ALU.mult, ALU.add))
            q.step(dve.tensor_tensor(rstd[:, seqs], y, t, ALU.mult))
            assert q.n == LN_OPS

        def dve_tokens(dve):
            dve.wait_ge(const_in, 16)
            dve.tensor_copy(identb[:, :], ident).then_inc(cast_done, 1)
            for m, c in ((mask_q, C_MQ), (mask_k, C_MK)):
                dve.tensor_copy(m[:, :], const[0:S, c:c + S]).then_inc(cast_done, 1)
            dve.tensor_copy(upperb[:, :], const[0:S, C_UP:C_UP + S]).then_inc(cast_done, 1)
            dve.memset(onesb[:, :], 1.0).then_inc(cast_done, 1)
            dve.wait_ge(tok_in, 32)
            for m in range(KT):
                dve.tensor_scalar(pos[:, m, :], pos[:, m, :], tok_bias[:, m:m + 1], None, ALU.add).then_inc(posb_done, 1)
            dve.wait_ge(posb_done, KT)
            for m in range(KT):
                for c in range(2):
                    dve.wait_ge(tok_ps, 2 * m + c + 1)
                    h = B // 2 * IMG
                    dve.tensor_tensor(tokT[:, m, c * h:(c + 1) * h].rearrange("p (b n) -> p b n", n=IMG),
                                      ps[:, 2 * m + c, 0:h].rearrange("p (b n) -> p b n", n=IMG),
                                      pos[:, m, :].unsqueeze(1).broadcast_to([P, B // 2, IMG]), ALU.add).then_inc(tokT_ready, 1)
            dve.wait_ge(txt_in, 16)
            for b in range(B):
                dve.wait_ge(img_ready, b // 2 + 1)
                dve.bn_stats(stats[:, b, :], resid[:, b, :]).then_inc(stats_done, 1)
            dve.wait_ge(stats_done, B)

        def dve_attention(dve):
            def normalise(b):
                dve.tensor_scalar(xn, resid[:, b, :], mean[:, bass.ds(b, 1)], rstd[:, bass.ds(b, 1)], ALU.subtract, ALU.mult).then_inc(xn_ready, 1)

            def spread_keys(b):
                for t in range(KT):
                    dve.wait_ge(qk_ready, 4 * b + 2 * t + 1)
                    dve.tensor_tensor(kz[:, t * HT8:(t + 1) * HT8, :], qkT[:, KT + t, :].unsqueeze(1).broadcast_to([P, HT8, S]),
                                      head_mask.unsqueeze(2).broadcast_to([P, HT8, S]), ALU.mult).then_inc(kz_ready, 1)

            def values(b):
                dve.wait_ge(v_ps, b + 1)
                dve.tensor_tensor(vh[:, :, 0:HD], ps[0:S, 0, 0:D].rearrange("p (h e) -> p h e", h=HEADS),
                                  v_b.rearrange("p (h e) -> p h e", h=HEADS), ALU.add).then_inc(v_ready, 1)

            def maxima(b):
                for r in range(QUADS):
                    dve.wait_ge(score_ps, QUADS * b + r + 1)
                    dve.tensor_reduce(negmax[:, 0, 4 * r:4 * r + 4].unsqueeze(2), ps[0:S, 3 + r, 0:4 * S].rearrange("p (j s) -> p j s", j=4),
                                      AX.X, ALU.max, negate=True).then_inc(negmax_ready, 1)
                dve.wait_ge(negmax_ready, QUADS * b + QUADS)
                dve.tensor_copy(negmax[:, 1:3, 0:HEADS], negmax[:, 0, 0:HEADS].unsqueeze(1).broadcast_to([S, 2, HEADS])).then_inc(negmax3_ready, 1)

            def split(b):
                mid, low = slice(32, 64), slice(64, 96)
                q = Seq(dve, nm_step, 2 * b)
                dve.wait_ge(nm_hi_ready, 2 * b + 2)
                q.step(dve.tensor_tensor(nm_rest, ps[0:96, 7, 0:S], nm_hi, ALU.subtract))
                dve.tensor_copy(nm3[mid, :], nm_rest[mid, :]).then_inc(nm3_ready, 1)
                q.step(dve.tensor_copy(nm_mid[low, :], nm_rest[low, :]))
                dve.tensor_tensor(nm3[low, :], nm_rest[low, :], nm_mid[low, :], ALU.subtract).then_inc(nm3_ready, 1)

            def weigh(b):
                dve.wait_ge(sums_ps, b + 1)
                dve.reciprocal(rsum, ps[:, 2, 0:QUADS * S].rearrange("p (r s) -> p r s", r=QUADS)).then_inc(rsum_ready, 1)
                dve.wait_ge(rsum_ready, b + 1)
                dve.tensor_tensor(attn, attn, rsum, ALU.mult).then_inc(attn_ready, 1)

            def add_resid(b):
                dve.wait_ge(oproj_ps, b + 1)
                dve.wait_ge(bias_added, b + 1)
                dve.tensor_tensor(resid[:, b, :], ps[0:S, 2, 0:D], resid[:, b, :], ALU.add).then_inc(resid1_ready, 1)
                dve.wait_ge(resid1_ready, b + 1)
                dve.bn_stats(stats[:, b, :], resid[:, b, :]).then_inc(stats_done, 1)

            def step(b, first=False, last=False):
                maxima(b)
                if not last:
                    normalise(b + 1)
                split(b)
                if not first:
                    weigh(b - 1)
                if not last:
                    spread_keys(b + 1)
                if not first:
                    add_resid(b - 1)
                if not last:
                    values(b + 1)

            dve.wait_ge(attn_in, 8 * 16)
            normalise(0)
            dve.tensor_copy(max_pick, const[0:96, C_REP:C_REP + HEADS].unsqueeze(2).broadcast_to([96, HEADS, P])).then_inc(pick2_done, 1)
            spread_keys(0)
            values(0)
            step(0, first=True)
            with dve.Fori(0, B - 2) as i:
                step(i + 1)
            step(B - 1, last=True)
            dve.wait_ge(stats_done, B + B - 1)
            dve_layernorm(dve, 1, BUT_ONE_SEQS)
            for b in range(TAIL_SEQS):
                dve_xn2(dve, b)
            weigh(B - 1)
            for b in range(TAIL_SEQS, B - 1):
                dve_xn2(dve, b)
            add_resid(B - 1)
            dve.wait_ge(stats_done, 2 * B)
            dve_layernorm(dve, 2, ONE_SEQ)
            dve_xn2(dve, B - 1)

        def dve_xn2(dve, b):
            dve.tensor_scalar(xn2[:, b, :], resid[:, b, :], mean[:, b:b + 1], rstd[:, b:b + 1], ALU.subtract, ALU.mult).then_inc(xn2_ready, 1)

        def dve_router(dve):
            dve.sem_inc(sh_ready, 2)
            dve.sem_inc(sresid_ready, 2)
            dve.sem_inc(ey_ready, 1)
            dve.wait_ge(logits_ps, B)
            q = Seq(dve, route)
            q.step(dve.tensor_copy(logits, ps[0:S, 7, 0:B * EXPERTS].rearrange("p (b e) -> p b e", b=B)))
            q.step(dve.tensor_reduce(rtop, logits, AX.X, ALU.max))
            q.step(dve.tensor_tensor(rpick, logits, rtop.broadcast_to([S, B, EXPERTS]), ALU.is_equal))
            e8 = const[0:S, C_E8:C_E8 + EXPERTS].unsqueeze(1).broadcast_to([S, B, EXPERTS])
            q.step(dve.tensor_tensor(rpick, rpick, e8, ALU.mult))
            q.step(dve.tensor_reduce(rtop, rpick, AX.X, ALU.min))
            q.step(dve.tensor_tensor(chosen, rtop.broadcast_to([S, B, EXPERTS]), e8, ALU.is_equal))
            assert q.n == CHOICE_OPS
            dve.tensor_copy(chosenb[:, :, :], chosen).then_inc(chosen_ready, 1)

        def dve_slots(dve):
            q = Seq(dve, route, CHOICE_OPS)
            dve.wait_ge(counts_ps, 2)
            q.done(dve.tensor_copy(prefix, ps[0:S, 2, 0:B * EXPERTS].rearrange("p (b e) -> p b e", b=B)))
            q.step(dve.tensor_copy(total, ps[0:S, 7, 0:B * EXPERTS].rearrange("p (b e) -> p e b", b=B)))
            q.step(dve.tensor_tensor_scan(summed.rearrange("p e b -> p (e b)"), const[0:S, C_RES:C_RES + EXPERTS * B],
                                          total.rearrange("p e b -> p (e b)"), 0.0, ALU.mult, ALU.add))
            q.step(dve.tensor_tensor(etiles, summed[:, :, B - 1:B].broadcast_to([S, EXPERTS, NK128]),
                                     const[0:S, C_K128:C_K128 + NK128].unsqueeze(1).broadcast_to([S, EXPERTS, NK128]), ALU.is_gt))
            q.step(dve.tensor_reduce(ecount, etiles, AX.X, ALU.add))
            q.step(dve.tensor_tensor_scan(esum, const[0:S, C_RES8:C_RES8 + EXPERTS], ecount, 0.0, ALU.mult, ALU.add))
            q.done(dve.tensor_tensor(ebase, esum, ecount, ALU.subtract))
            q.done(dve.tensor_tensor(summed, summed, total, ALU.subtract))
            q.step(dve.tensor_tensor(tile_ge, const[0:S, C_TILE:C_TILE + ETILES].unsqueeze(2).broadcast_to([S, ETILES, EXPERTS]),
                                     esum.unsqueeze(1).broadcast_to([S, ETILES, EXPERTS]), ALU.is_ge))
            q.step(dve.tensor_reduce(tile_e, tile_ge, AX.X, ALU.add))
            q.done(dve.tensor_scalar(tile_expert[:, :], tile_e[0:1, :], float(EXPERTS - 1), None, ALU.min))
            q.step(dve.scalar_tensor_tensor(out=summed, in0=ebase.unsqueeze(2).broadcast_to([S, EXPERTS, B]), scalar=float(ETILE),
                                            in1=summed, op0=ALU.mult, op1=ALU.add))
            q.step(dve.tensor_tensor(prefix, prefix, summed.rearrange("p e b -> p b e"), ALU.add))
            q.step(dve.tensor_tensor(prefix, prefix, chosen, ALU.mult))
            q.step(dve.tensor_reduce(slotf, prefix, AX.X, ALU.add))
            dve.tensor_copy(slot[:, :], slotf).then_inc(slots_ready, 1)

        def dve_shared(dve):
            def group(g):
                for m in range(HT):
                    par = m % 2
                    dve.wait_ge(sgate_ready, g * HT + m + 1)
                    dve.wait_ge(sup_ps, g * HT + m + 1)
                    dve.tensor_tensor(s_hT[:, m, :], ps[:, 4 + 2 * par, 0:4 * S], s_gate[:, par, :], ALU.mult).then_inc(sh_ready, 1)
                for pair in range(2):
                    dve.wait_ge(sdown_ps, 2 * g + pair + 1)
                    r = resid[:, bass.ds(4 * g + 2 * pair, 2), :]
                    dve.tensor_tensor(r, ps[0:S, pair, :].rearrange("p (b d) -> p b d", b=2), r, ALU.add).then_inc(sresid_ready, 1)

            group(0)
            dve_slots(dve)
            with dve.Fori(1, 4) as g:
                group(g)

        def dve_experts(dve):
            def hidden(j, par):
                dve.wait_ge(egate_ready, j + 1)
                dve.wait_ge(eup_ps, j + 1)
                dve.tensor_tensor(e_h[par], ps[:, 2 + 2 * par, :], e_gate[par], ALU.mult).then_inc(eh_ready, 1)

            def answer(j, par):
                dve.wait_ge(ey_ps, j + 1)
                dve.tensor_copy(e_y[par], ps[:, 6, 0:D]).then_inc(ey_ready, 1)

            hidden(0, 0)
            hidden(1, 1)
            answer(0, 0)
            hidden(2, 0)
            answer(1, 1)
            dve_ssm_tables(dve)
            dve.wait_ge(ffn_in, 2 * 16)
            dve.sem_inc(wqT_ready, 2)

            def step(j, par, stored, weights):
                hidden(j + 1, 1 - par)
                dve.wait_ge(ey_out[par], stored)
                answer(j, par)
                if weights:
                    dve_weights(dve, j - 2, par)

            with dve.Fori(1, 1 + FT) as i:
                for par in range(2):
                    step(2 * i + par, par, 16 * i, True)
            for j in range(2 + 2 * FT, ETILES - 2):
                step(j, j % 2, 8 * (j - j % 2), False)
            hidden(ETILES - 1, 1)
            dve.wait_ge(ey_out[0], 8 * (ETILES - 2))
            answer(ETILES - 2, 0)
            dve.wait_ge(ey_out[1], 8 * (ETILES - 2))
            answer(ETILES - 1, 1)

        def dve_clips(dve):
            dve.wait_ge(clip_exp, 1)
            q = Seq(dve, f_step)
            q.step(dve.tensor_scalar(clip_sig[:, :], clip_sig[:, :], 1.0, QMAX, ALU.add, ALU.mult))
            q.step(dve.reciprocal(clip_sig[:, :], clip_sig[:, :]))

        def dve_weights(dve, w, par):
            raw = raw_gu[:, bass.ds(w, 1), :].rearrange("p o d -> p (o d)")
            scale = wscale[0:FP, :, :].rearrange("p n t -> p (n t)")[:, bass.ds(w, 1)]
            inverse = winv[0:FP, bass.ds(w, 1)]
            q = Seq(dve, wq_step, 4 * w)
            q.step(dve.tensor_reduce(scale, raw, AX.X, ALU.max, apply_absolute_value=True))
            q.step(dve.tensor_scalar(scale, scale, 1.0 / QMAX, None, ALU.mult))
            q.step(dve.reciprocal(inverse, scale))
            q.step(dve.tensor_scalar(raw, raw, inverse, ROUND, ALU.mult, ALU.add))
            dve.wait_ge(wqT_ready, w + 1)
            dve.tensor_scalar(w_int[par], raw, ROUND, None, ALU.subtract).then_inc(wq_ready, 1)

        def dve_weights_down(dve):
            dve.wait_ge(ffn_d_in, 16)
            q = Seq(dve, wq_step, 4 * 2 * FT)
            scale = wscale[:, 2, 0:KT]
            q.step(dve.tensor_reduce(scale, raw_d, AX.X, ALU.max, apply_absolute_value=True))
            q.step(dve.tensor_scalar(scale, scale, 1.0 / QMAX, None, ALU.mult))
            q.step(dve.reciprocal(winv[:, 0:KT], scale))
            for k in range(KT):
                q.done(dve.tensor_scalar(raw_d[:, k, :], raw_d[:, k, :], winv[:, k:k + 1], ROUND, ALU.mult, ALU.add))
            q.wait()
            dve.tensor_scalar(raw_d, raw_d, ROUND, None, ALU.subtract).then_inc(wq_ready, 1)

        def dve_xn4(dve, b):
            dve.tensor_scalar(xn2[:, b, :], resid[:, b, :], mean[:, b:b + 1], rstd[:, b:b + 1],
                              ALU.subtract, ALU.mult).then_inc(xn4_ready, 1)
            dve.wait_ge(xn4_ready, b + 1)
            dve.tensor_reduce(lnt[:, 5, b:b + 1], xn2[:, b, :], AX.X, ALU.max, apply_absolute_value=True).then_inc(xmax_ready, 1)

        def dve_ffn(dve):
            dve.wait_ge(stats_done, 4 * B)
            dve_layernorm(dve, 6, LAST_SEQS)
            for b in range(LAST_SEQS.start, B):
                dve_xn4(dve, b)
            dve.wait_ge(xmax_ready, B)
            q = Seq(dve, f_step, 2)

            def scales(turn, source, parts, dst):
                dve.tensor_reduce(amax[0:parts, :], source, AX.X, ALU.max, apply_absolute_value=True).then_inc(amax_ready, 1)
                dve.wait_ge(amaxT_ps, turn + 1)
                q.step(dve.tensor_reduce(amax1[:, 0:1], ps[0:1, 7, 0:parts], AX.X, ALU.max))
                q.step(dve.tensor_scalar(amax1[:, 1:2], amax1[:, 0:1], clip_sig[0:1, turn:turn + 1], None, ALU.mult))
                dve.reciprocal(amax1[:, 2:3], amax1[:, 1:2]).then_inc(scale_ready, 1)
                dve.wait_ge(scale_ps, turn + 1)
                q.step(dve.tensor_copy(dst, ps[:, 7, 0:2]))

            scales(0, lnt[:, 5, :], S, xscale)
            dve.sem_inc(fscale_ready, 1)
            q.done(dve.tensor_scalar(gscale, wscale[0:FP, 0, :], xscale[0:FP, 0:1], None, ALU.mult))
            q.done(dve.tensor_scalar(uscale, wscale[0:FP, 1, :], xscale[0:FP, 0:1], None, ALU.mult))
            q.wait()
            dve.sem_inc(fscale_ready, 1)
            for g in range(FG):
                dve.wait_ge(xround, g + 1)
                dve.tensor_scalar(xqf[g % 2], xqf[g % 2], ROUND - QMAX - 1.0, ROUND + QMAX, ALU.max, ALU.min).then_inc(xclip, 1)
                dve.wait_ge(xclip, g + 1)
                if g >= 2:
                    dve.wait_ge(xqT_ps, KT * (g - 1))
                dve.tensor_scalar(xqb[g % 2], xqf[g % 2], ROUND, None, ALU.subtract).then_inc(xq_ready, 1)
            dve.sem_inc(hid_even, 2)

            def product(g, m):
                dve.wait_ge(fgate_ready, g * FT + m + 1)
                dve.wait_ge(fup_ps, g * FT + m + 1)
                dve.scalar_tensor_tensor(out=hid[:, m, bass.ds(g * 4 * S, 4 * S)], in0=ps[0:FP, 2 * (m % 4) + 1, 0:4 * S],
                                         scalar=uscale[:, m:m + 1], in1=f_gate[m % 4], op0=ALU.mult, op1=ALU.mult).then_inc(hid_even, 1)

            def greatest(g, m):
                dve.wait_ge((hid_even, hid_odd)[m % 2], g * (FT // 2) + m // 2 + 3)
                dve.tensor_reduce(fmax[:, bass.ds(g * FT + m, 1)], hid[:, m, bass.ds(g * 4 * S, 4 * S)], AX.X, ALU.max,
                                  apply_absolute_value=True).then_inc(hmax_ready, 1)

            def products_and_maxima(g, last=False):
                for m in range(0, FT, 2):
                    if m + 4 < FT:
                        product(g, m + 4)
                    elif not last:
                        product(g + 1, m + 4 - FT)
                    greatest(g, m)
                    greatest(g, m + 1)

            product(0, 0)
            product(0, 2)
            with dve.Fori(0, FG - 1) as g:
                products_and_maxima(g)
            products_and_maxima(FG - 1, last=True)
            dve.wait_ge(hmax_ready, FG * FT)
            scales(1, fmax, FP, hscale)
            dve.sem_inc(fscale_ready, 1)
            q.step(dve.tensor_scalar(dcol, wscale[:, 2, 0:KT], hscale[:, 0:1], None, ALU.mult))
            for k in range(KT):
                dve.tensor_scalar(diag_d[:, k, :], ident, dcol[:, k:k + 1], None, ALU.mult).then_inc(dscale_ready, 1)
            dve.wait_ge(dscaleT_ps, 1)
            q.step(dve.tensor_copy(dscale, ps[:, 6, 0:D]))

            def answers(piece):
                for b in range(2 * piece, 2 * piece + 2):
                    dve.wait_ge(fdown_ps, b + 1)
                    if b >= 2:
                        dve.wait_ge(final_ready, b - 1)
                    dve.tensor_tensor(answer_f[b % 2], ps[0:S, b % 4, 0:D], dscale[0:S, :], ALU.mult).then_inc(fy_ready, 1)

            for piece in range(B // 2):
                h = hid[:, :, 2 * piece * S:(2 * piece + 2) * S]
                dve.wait_ge(hround, piece + 1)
                dve.tensor_scalar(h, h, ROUND - QMAX - 1.0, ROUND + QMAX, ALU.max, ALU.min).then_inc(hclip, 1)
                if piece % 2 == 0:
                    dve.wait_ge(hclip, piece + 1)
                    dve.tensor_scalar(hq[:, :, 2 * piece * S:(2 * piece + 2) * S], h, ROUND, None, ALU.subtract).then_inc(hq_even, 1)
                if piece >= 2:
                    answers(piece - 2)
            answers(B // 2 - 2)
            answers(B // 2 - 1)

        def dve_ssm_tables(dve):
            dve.wait_ge(ssm_in, 16 * 15)
            dve.wait_ge(aneg_done, 1)
            dve.tensor_scalar(a_neg, a_neg, -1.0, None, ALU.mult).then_inc(aneg_done, 1)
            for m in range(KT):
                for t in range(TAPS):
                    dve.tensor_scalar(conv_diag[:, m, t, :], ident, conv_w[:, m, t:t + 1], None, ALU.mult).then_inc(diag_done, 1)
                dve.tensor_scalar(d_diag[:, m, :], ident, d_par[:, m:m + 1], None, ALU.mult).then_inc(diag_done, 1)
            dve.tensor_copy(pick, const[0:96, C_REP:C_REP + 32].unsqueeze(2).broadcast_to([96, 32, P])).then_inc(pick_done, 1)

        def dve_ssm(dve):
            def add_answers(seqs):
                for b in range(seqs.start, seqs.stop):
                    dve.wait_ge(gathered[b // 4], 64)
                    dve.tensor_tensor(resid[:, b, :], resid[:, b, :], xn2[:, b, :], ALU.add).then_inc(resid2_ready, 1)
                    dve.wait_ge(resid2_ready, b + 1)
                    dve.bn_stats(stats[:, b, :], resid[:, b, :]).then_inc(stats_done, 1)
                dve.wait_ge(stats_done, 2 * B + seqs.stop)

            dve_weights_down(dve)
            add_answers(FIRST_SEQS)
            dve_layernorm(dve, 3, FIRST_SEQS)
            for counted in (state_ready, read_ready, read_used, c_ready, drive_ready):
                dve.sem_inc(counted, 2)
            dve.sem_inc(yT_ready, 1)

            def normalise(g):
                for r in range(GB):
                    b = GB * g + r
                    dve.tensor_scalar(xn3[r], resid[:, b, :], mean[:, bass.ds(b, 1)], rstd[:, bass.ds(b, 1)],
                                      ALU.subtract, ALU.mult).then_inc(xn3_ready, 1)

            def steps(g, par):
                dve.wait_ge(softplus_ready, g + 1)
                dve.wait_ge(xc_ready, KT * g + KT)
                dve.tensor_tensor(delta[par], sp_relu, sp_abs, ALU.add).then_inc(delta_ready, 1)
                dve.wait_ge(delta_ready, g + 1)
                dve.tensor_tensor(dx[par], delta[par], xc[par], ALU.mult).then_inc(dx_ready, 1)

            def chunk(g, c, par):
                k, kp = g * CHUNKS + c, c % 2
                dve.wait_ge(b_ps, k + 1)
                if c == 0:
                    dve.wait_ge(dx_ready, g + 1)
                dve.tensor_tensor(drive[kp], dx[par].unsqueeze(1).broadcast_to([P, 2, KT, N]),
                                  ps[:, 2 + kp, 0:2 * N].rearrange("p (n s) -> p n s", n=2).unsqueeze(2).broadcast_to([P, 2, KT, N]),
                                  ALU.mult).then_inc(drive_ready, 1)
                dve.wait_ge(drive_ready, k + 3)
                dve.wait_ge(decay_ready, 2 * k + 2)
                dve.wait_ge(read_ready, k + 1)
                dve.tensor_tensor_scan(state[kp].rearrange("p n k s -> p (n k s)"), decay[kp].rearrange("p n q s -> p (n q s)"),
                                       drive[kp].rearrange("p n k s -> p (n k s)"), 0.0, ALU.mult, ALU.add).then_inc(state_ready, 1)

            def pair(g, c):
                if c in PAIRED:
                    dve.wait_ge(read_ready, g * CHUNKS + c + 3)
                    r = read[c % 2]
                    dve.tensor_tensor(r[:, 0], r[:, 0], r[:, 1], ALU.add).then_inc(pair_ready, 1)

            def gate(g, par):
                dve.wait_ge(y_ps, g + 1)
                dve.wait_ge(res_ready, KT * g + KT)
                dve.tensor_tensor(yT, ps[:, 6, 0:KT * N].rearrange("p (k s) -> p k s", k=KT), silu_res[par], ALU.mult).then_inc(yT_ready, 1)

            def add_resid(g):
                dve.wait_ge(ssm_ps, g + 1)
                r = resid[:, bass.ds(GB * g, GB), :]
                dve.tensor_tensor(r, ps[0:S, 7, :].rearrange("p (b d) -> p b d", b=GB), r, ALU.add).then_inc(resid3_ready, 1)
                dve.wait_ge(resid3_ready, g + 1)
                for q in range(GB):
                    dve.bn_stats(stats[:, GB * g + q, :], resid[:, GB * g + q, :]).then_inc(stats_done, 1)

            def step(g, par, more=True, before=True, turn_next=True):
                for c in range(CHUNKS):
                    if turn_next and c == AT_NORMALISE:
                        normalise(g + 2)
                    chunk(g, c, par)
                    if c > 0:
                        pair(g, c - 1)
                    elif before:
                        pair(g - 1, CHUNKS - 1)
                    if before and c == AT_GATE:
                        gate(g - 1, 1 - par)
                    if before and c == AT_RESID:
                        add_resid(g - 1)
                    if more and c == AT_STEPS:
                        steps(g + 1, 1 - par)
                    if not more:
                        if c == 3:
                            dve.wait_ge(stats_done, 3 * B + EARLY_SEQS.stop)
                            dve_layernorm(dve, 5, EARLY_SEQS)
                        if c >= 4:
                            for b in range(4 * (c - 4), min(4 * (c - 4) + 4, EARLY_SEQS.stop)):
                                dve_xn4(dve, b)

            dve.wait_ge(ey_ps, ETILES)
            normalise(0)
            add_answers(OTHER_SEQS)
            dve.wait_ge(x3T_ps, 1)
            normalise(1)
            dve_layernorm(dve, 4, OTHER_SEQS)
            steps(0, 0)
            step(0, 0, before=False)
            with dve.Fori(0, (GROUPS - 4) // 2) as i:
                for half in range(2):
                    step(2 * i + 1 + half, 1 - half)
            step(GROUPS - 3, 1)
            step(GROUPS - 2, 0, turn_next=False)
            step(GROUPS - 1, 1, more=False, turn_next=False)
            pair(GROUPS - 1, CHUNKS - 1)
            gate(GROUPS - 1, 1)
            add_resid(GROUPS - 1)

        @block.vector
        def _(dve):
            dve_tokens(dve)
            dve_layernorm(dve, 0)
            dve_clips(dve)
            dve_attention(dve)
            dve_router(dve)
            dve_shared(dve)
            dve_experts(dve)
            dve_ssm(dve)
            dve_ffn(dve)

        def pe_tokens(pe):
            h = B // 2 * IMG
            for part in range(PK // 2):
                pe.wait_ge(patch_in[part], 32)
                for m in range(KT):
                    for c in range(2):
                        for k in range(2 * part, 2 * part + 2):
                            last = pe.matmul(ps[:, 2 * m + c, 0:h], tok_w[:, k, m * P:(m + 1) * P], patches[:, k, c * h:(c + 1) * h],
                                             start=k == 0, stop=k == PK - 1)
                        if part == PK // 2 - 1:
                            last.then_inc(tok_ps, 1)
            pe.wait_ge(tokT_ready, 4)
            pe.wait_ge(const_in, 16)
            for pair in range(B // 2):
                bank = 4 + pair % 4
                if pair >= 4:
                    pe.wait_ge(img_ready, pair - 3)
                for r in range(2):
                    for m in range(KT):
                        b = 2 * pair + r
                        last = pe.transpose(ps[0:IMG, bank, r * D + m * P:r * D + (m + 1) * P], tokT[:, m, b * IMG:(b + 1) * IMG], ident)
                last.then_inc(tokback_ps, 1)

        def pe_attention(pe):
            def turn_x(b, after_v=True):
                pe.wait_ge(xn_ready, b + 1)
                if after_v:
                    pe.wait_ge(v_ready, b)
                for k in range(KT):
                    last = pe.transpose(ps[:, 0, k * S:(k + 1) * S], xn[:, k * P:(k + 1) * P], ident[0:S, 0:S])
                last.then_inc(xnT_ps, 1)

            def queries_keys(b):
                pe.wait_ge(xT_ready, b + 1)
                for t in range(2 * KT):
                    for k in range(KT):
                        last = pe.matmul(ps[:, 1, t * S:(t + 1) * S], qk_w[:, k, t, :], xT[:, k, :],
                                         start=k == 0, stop=k == KT - 1, skip_group_check=True)
                last.then_inc(qk_ps, 1)

            def values(b):
                for k in range(KT):
                    last = pe.matmul(ps[0:S, 0, 0:D], xT[:, k, :], v_w[:, k, :], start=k == 0, stop=k == KT - 1, skip_group_check=True)
                last.then_inc(v_ps, 1)

            def scores(b, r):
                pe.wait_ge(qk_ready, 4 * b + r // 2 * 2 + 2)
                pe.wait_ge(kz_ready, 2 * b + r // 2 + 1)
                pe.matmul(ps[0:S, 3 + r, 0:4 * S], qkT[:, r // 2, :], kz[:, 4 * r:4 * r + 4, :], start=True, stop=False, skip_group_check=True)
                mask(r, mask_q, stop=True).then_inc(score_ps, 1)

            def scores_t(b, r):
                pe.wait_ge(qz_ready, 2 * b + r // 2 + 1)
                pe.wait_ge(negmax_ready, 4 * b + r + 1)
                pe.matmul(ps[0:S, 3 + r, 0:4 * S], qkT[:, KT + r // 2, :], qz[:, 4 * r:4 * r + 4, :], start=True, stop=False, skip_group_check=True)
                mask(r, mask_k, stop=False)

            def mask(r, m, stop):
                return pe.matmul(ps[0:S, 3 + r, 0:4 * S], identb[0:S, 0:S], m[:, :].unsqueeze(1).broadcast_to([S, 4, S]),
                                 start=False, stop=stop, skip_group_check=True)

            def turn_max(b):
                pe.wait_ge(negmax3_ready, b + 1)
                pe.transpose(ps[0:96, 7, 0:S], negmax.rearrange("p n h -> p (n h)"), ident[0:S, 0:S]).then_inc(nmT_ps, 1)

            def less_max(b):
                pe.wait_ge(nm_hi_ready, 2 * b + 2)
                pe.wait_ge(nm3_ready, 2 * b + 2)
                for r in range(QUADS):
                    for j in range(4):
                        last = pe.matmul(ps[0:S, 3 + r, j * S:(j + 1) * S], max_pick[:, 4 * r + j, 0:S], nm3, start=False, stop=True, skip_group_check=True)
                    last.then_inc(scoreT_ps, 1)

            def weighted(b):
                pe.wait_ge(v_ready, b + 1)
                for r in range(QUADS):
                    pe.wait_ge(probs_ready, QUADS * b + r + 1)
                    for j in range(4):
                        c = slice(32 * j, 32 * j + 32)
                        last = pe.matmul(ps[c, 7, r * S:(r + 1) * S], vh[:, 4 * r + j, :], probs[:, r, j, :],
                                         start=True, stop=True, tile_position=(0, 32 * j), skip_group_check=True)
                last.then_inc(av_ps, 1)

            def spread_sums(b, first=False):
                pe.wait_ge(attn_copied, b + 1)
                if not first:
                    pe.wait_ge(resid1_ready, b)
                pe.matmul(ps[:, 2, 0:QUADS * S], sum_pick, attn.rearrange("p r s -> p (r s)"), start=True, stop=True).then_inc(sums_ps, 1)

            def project(b):
                pe.wait_ge(attn_ready, b + 1)
                for r in range(QUADS):
                    last = pe.matmul(ps[0:S, 2, 0:D], attn[:, r, :], o_w[:, r, :], start=r == 0, stop=r == QUADS - 1)
                last.then_inc(oproj_ps, 1)

            def step(b, back=True, more=True, first_spread=False):
                scores(b, 0)
                scores(b, 1)
                if back:
                    spread_sums(b - 1, first_spread)
                scores(b, 2)
                scores(b, 3)
                scores_t(b, 0)
                scores_t(b, 1)
                turn_max(b)
                scores_t(b, 2)
                scores_t(b, 3)
                if more:
                    turn_x(b + 1)
                less_max(b)
                if more:
                    queries_keys(b + 1)
                if back:
                    project(b - 1)
                weighted(b)
                if more:
                    values(b + 1)

            pe.wait_ge(attn_in, 8 * 16)
            pe.wait_ge(cast_done, 5)
            pe.wait_ge(pool_set, 6)
            pe.wait_ge(img_ready, B // 2)
            turn_x(0, after_v=False)
            queries_keys(0)
            values(0)
            pe.wait_ge(pick2_done, 1)
            step(0, back=False)
            step(1, first_spread=True)
            with pe.Fori(0, B - 3) as i:
                step(i + 2)
            step(B - 1, more=False)
            spread_sums(B - 1)
            for b in range(TAIL_SEQS):
                pe_turn2(pe, b)
            pe.wait_ge(moe_in, 32)
            for b in range(TAIL_SEQS):
                pe_score(pe, b)
            project(B - 1)

        def pe_score(pe, b):
            pe.wait_ge(xT2_ready, b + 1)
            for k in range(KT):
                last = pe.matmul(ps[0:S, 7, b * EXPERTS:(b + 1) * EXPERTS], xT2[:, k, b * S:(b + 1) * S], router_w[:, k, :],
                                 start=k == 0, stop=k == KT - 1, skip_group_check=True)
            last.then_inc(logits_ps, 1)

        def pe_turn2(pe, b):
            pe.wait_ge(xn2_ready, b + 1)
            if b >= 4:
                pe.wait_ge(xT2_ready, b - 3)
            for k in range(KT):
                last = pe.transpose(ps[:, ROUTER_BANKS[b % 4], k * S:(k + 1) * S], xn2[:, b, k * P:(k + 1) * P], ident[0:S, 0:S])
            last.then_inc(xn2T_ps, 1)

        def pe_router(pe):
            for b in range(TAIL_SEQS, B):
                if b == B - 1:
                    for earlier in range(TAIL_SEQS, B - 2):
                        pe_score(pe, earlier)
                pe_turn2(pe, b)
            for b in range(B - 2, B):
                pe_score(pe, b)

        def pe_counts(pe):
            pe.wait_ge(chosen_ready, 1)
            flat = chosenb[:, :, :].rearrange("p b e -> p (b e)")
            pe.matmul(ps[0:S, 2, 0:B * EXPERTS], upperb[:, :], flat, start=True, stop=True).then_inc(counts_ps, 1)
            pe.matmul(ps[0:S, 7, 0:B * EXPERTS], onesb[:, :], flat, start=True, stop=True).then_inc(counts_ps, 1)

        def pe_shared(pe):
            pe.wait_ge(xT2_ready, B)
            def group(g):
                for m in range(HT):
                    par = m % 2
                    pe.wait_ge(sh_ready, g * HT + m + 1)
                    for bank, at, done in ((3 + 2 * par, GATE, sgate_ps), (4 + 2 * par, UP, sup_ps)):
                        for k in range(KT):
                            last = pe.matmul(ps[:, bank, 0:4 * S], sh_w[:, at + k * HID + m * P:at + k * HID + (m + 1) * P],
                                             xT2[:, k, bass.ds(g * 4 * S, 4 * S)], start=k == 0, stop=k == KT - 1)
                        last.then_inc(done, 1)
                pe.wait_ge(sh_ready, g * HT + HT + 2)
                for pair in range(2):
                    pe.wait_ge(sresid_ready, 2 * g + pair + 1)
                    for r in range(2):
                        for m in range(HT):
                            b = 2 * pair + r
                            last = pe.matmul(ps[0:S, pair, r * D:(r + 1) * D], s_hT[:, m, b * S:(b + 1) * S],
                                             sh_w[:, DOWN + m * D:DOWN + (m + 1) * D], start=m == 0, stop=m == HT - 1,
                                             skip_group_check=True)
                    last.then_inc(sdown_ps, 1)

            group(0)
            pe_counts(pe)
            with pe.Fori(1, 4) as g:
                group(g)

        def pe_experts(pe):
            def turn(j, par, half):
                pe.wait_ge(xg_in[par], half)
                for k in range(KT):
                    last = pe.transpose(ps[:, 0, k * ETILE:(k + 1) * ETILE], xg[par][:, k * P:(k + 1) * P], ident)
                last.then_inc(xgT_ps, 1)

            def gate_up(j, par, j_before=None):
                e = expert(j)
                pe.wait_ge(xgT_ready, j + 1)
                for bank, at, done in ((1 + 2 * par, GATE, egate_ps), (2 + 2 * par, UP, eup_ps)):
                    for k in range(KT):
                        last = pe.matmul(ps[:, bank, :], xgT[par][:, k, :], arena[:, bass.ds(e * EW + at + k * HID, HID)],
                                         start=k == 0, stop=k == KT - 1)
                    last.then_inc(done, 1)
                    if at == GATE and j_before is not None:
                        e_before = expert(j_before)
                        turn_hidden(j_before, 1 - par)
                return e_before if j_before is not None else None

            def down(j, e):
                pe.wait_ge(ehT_ready, j + 1)
                pe.wait_ge(ey_ready, j + 1)
                for m in range(HT):
                    last = pe.matmul(ps[:, 6, 0:D], e_hT[:, m, :], arena[:, bass.ds(e * EW + DOWN + m * D, D)],
                                     start=m == 0, stop=m == HT - 1)
                last.then_inc(ey_ps, 1)

            def turn_hidden(j, par):
                pe.wait_ge(eh_ready, j + 1)
                for m in range(HT):
                    last = pe.transpose(ps[:, 5, m * P:(m + 1) * P], e_h[par][:, m * P:(m + 1) * P], ident)
                last.then_inc(ehT_ps, 1)

            def expert(j):
                return pe.value_load(tile_expert[0:1, bass.ds(j, 1)], min_val=0, max_val=EXPERTS - 1)

            pe.wait_ge(experts_in, 16 * EXPERTS)
            pe.wait_ge(slots_ready, 1)
            pe.wait_ge(sresid_ready, 8 + 2)
            turn(0, 0, 16)
            pe.wait_ge(xgT_ready, 1)
            turn(1, 1, 16)
            gate_up(0, 0)

            def step(j, par, loaded, weights):
                e_down = gate_up(j + 1, 1 - par, j)
                turn(j + 2, par, loaded)
                down(j, e_down)
                if weights:
                    pe_weights(pe, j - 4, par)

            for j in range(4):
                step(j, j % 2, 8 * (j - j % 2) + 32, False)
            with pe.Fori(2, 2 + FT) as i:
                for par in range(2):
                    step(2 * i + par, par, 16 * i + 32, True)
            assert 4 + 2 * FT == ETILES - 2
            down(ETILES - 2, gate_up(ETILES - 1, 1, ETILES - 2))
            turn_hidden(ETILES - 1, 1)
            down(ETILES - 1, expert(ETILES - 1))

        def pe_weights(pe, w, par):
            pe.wait_ge(wq_ready, w + 1)
            pe.wait_ge(wqT_ready, w + 2)
            for k in range(KT):
                last = pe.transpose(psb(7)[:, k * FP:(k + 1) * FP], w_int[par][:, k * P:(k + 1) * P], identb[0:FP, 0:FP])
            last.then_inc(wqT_ps, 1)

        def pe_weights_down(pe):
            pe.wait_ge(wq_ready, 2 * FT + 1)
            pe.wait_ge(eh_ready, ETILES)
            for n in range(4):
                for m in range(2 * n, 2 * n + 2):
                    for k in range(KT):
                        at = m % 2 * D + k * P
                        last = pe.transpose(ps[0:FP, 1 + n, at:at + P], raw_d[:, k, m * FP:(m + 1) * FP], ident)
                last.then_inc(wqT_ps, 1)

        def pe_ffn(pe):
            def scales(turn, parts):
                pe.wait_ge(amax_ready, turn + 1)
                pe.transpose(ps[0:1, 7, 0:parts], amax[0:parts, :], ident[0:parts, 0:parts]).then_inc(amaxT_ps, 1)
                pe.wait_ge(scale_ready, turn + 1)
                pe.matmul(ps[:, 7, 0:2], ones, amax1[:, 1:3], start=True, stop=True).then_inc(scale_ps, 1)

            scales(0, S)
            for g in range(FG):
                pe.wait_ge(xq_ready, g + 1)
                for k in range(KT):
                    if g > 1:
                        pe.wait_ge(xqT_ready, KT * (g - 2) + k + 1)
                    for r in range(4):
                        last = pe.transpose(psb(2 * (g % 2) + k)[:, r * S4:r * S4 + S], xqb[g % 2][:, r, k * P:(k + 1) * P], identb[0:S, 0:S])
                    last.then_inc(xqT_ps, 1)
            pe.wait_ge(xqT_ready, KT * FG)
            with pe.Fori(0, FG) as g:
                for m in range(FT):
                    pair = m % 4
                    pe.wait_ge((hid_even, fup_ready)[m % 2], g * (FT // 2) + m // 2 + 1)
                    for bank, w, done in ((2 * pair, gq, fgate_ps), (2 * pair + 1, uq, fup_ps)):
                        for k in range(KT):
                            last = pe.matmul(ps[0:FP, bank, 0:4 * S], w[:, k, m * FP:(m + 1) * FP], xqT[:, k, bass.ds(g * 4 * S, 4 * S)],
                                             start=k == 0, stop=k == KT - 1)
                        last.then_inc(done, 1)
            scales(1, FP)
            pe.wait_ge(dscale_ready, KT)
            for k in range(KT):
                last = pe.matmul(ps[:, 6, k * P:(k + 1) * P], onesf[:, :], diag_d[:, k, :], start=True, stop=True, skip_group_check=True)
            last.then_inc(dscaleT_ps, 1)
            for b in range(B):
                pe.wait_ge((hq_even, hq_odd)[b // 2 % 2], b // 4 + 1)
                if b >= 4:
                    pe.wait_ge(fy_ready, b - 3)
                for m in range(FT):
                    last = pe.matmul(ps[0:S, b % 4, 0:D], hq[:, m, b * S:(b + 1) * S], dq[:, m, :], start=m == 0, stop=m == FT - 1)
                last.then_inc(fdown_ps, 1)

        def pe_ssm(pe):
            def turn(g, first=False):
                pe.wait_ge(xn3_ready, GB * g + GB)
                if not first:
                    pe.wait_ge(proj_ready, 4 * g)
                for k in range(KT):
                    for r in range(GB):
                        last = pe.transpose(ps[:, 0, k * N + r * S:k * N + (r + 1) * S], xn3[r][:, k * P:(k + 1) * P], ident[0:S, 0:S])
                last.then_inc(x3T_ps, 1)

            def project_in(g, par, half, first=False):
                pe.wait_ge(x3T_ready, g + 1)
                if not first:
                    pe.wait_ge(softplus_ready, g)
                for m in range(half * KT, half * KT + KT):
                    for k in range(KT):
                        last = pe.matmul(ps[:, 1 - m // KT, m % KT * N:(m % KT + 1) * N], in_w[:, k, m * P:(m + 1) * P], x3T[par][:, k, :],
                                         start=k == 0, stop=k == KT - 1, skip_group_check=True)
                    if m % KT == KT - 1:
                        last.then_inc((xin_ps, res_ps)[m // KT], 1)

            def convolve(g):
                pe.wait_ge(xpad_ready, KT * g + KT)
                for m in range(KT):
                    for t in range(TAPS):
                        last = pe.matmul(ps[:, 1, m * N:(m + 1) * N], conv_diag[:, m, t, :], xpad[:, m, :, t:t + S],
                                         start=t == 0, stop=t == TAPS - 1, skip_group_check=True)
                last.then_inc(conv_ps, 1)

            def project_x(g, par):
                pe.wait_ge(xc_ready, KT * g + KT)
                pe.wait_ge(res_ready, KT * g + KT)
                for w, rows, at in ((rank_w, RANK, 0), (bc_w, 96, N)):
                    for k in range(KT):
                        last = pe.matmul(ps[0:rows, 0, at:at + N], w[:, k, :], xc[par][:, k, :], start=k == 0, stop=k == KT - 1,
                                         skip_group_check=True)
                last.then_inc(proj_ps, 1)

            def project_dt(g):
                pe.wait_ge(proj_ready, 4 * g + 1)
                for m in range(KT):
                    last = pe.matmul(ps[:, 1, m * N:(m + 1) * N], dt_w[:, m * P:(m + 1) * P], rankT, start=True, stop=True, skip_group_check=True)
                last.then_inc(dt_ps, 1)

            def spread(g, c, par):
                k, kp = g * CHUNKS + c, c % 2
                if c == 0:
                    pe.wait_ge(bc3_ready, 2 * g + 2)
                    pe.wait_ge(proj_ready, 4 * g + 4)
                pe.wait_ge(drive_ready, k + 1)
                for n in range(2):
                    last = pe.matmul(ps[:, 2 + kp, n * N:(n + 1) * N], pick[:, 2 * c + n, :], bc3[par], start=True, stop=True, skip_group_check=True)
                last.then_inc(b_ps, 1)
                pe.wait_ge(c_ready, k + 1)
                for n in range(2):
                    last = pe.matmul(ps[:, 4 + kp, n * N:(n + 1) * N], pick[:, STATES + 2 * c + n, :], bc3[par], start=True, stop=True,
                                     skip_group_check=True)
                last.then_inc(c_ps, 1)

            def reduce(g, c, par):
                k, kp = g * CHUNKS + c, c % 2
                if c == 0:
                    pe.wait_ge(yT_ready, g + 1)
                pe.wait_ge(read_ready, k + 3)
                if c in PAIRED:
                    pe.wait_ge(pair_ready, len(PAIRED) * g + PAIRED.index(c) + 1)
                for n in range(1 if c in PAIRED else 2):
                    last = pe.matmul(ps[:, 6, 0:KT * N], ident, read[kp][:, n].rearrange("p k s -> p (k s)"), start=c == 0 and n == 0,
                                     stop=False, skip_group_check=True)
                last.then_inc(read_used, 1)
                if c == CHUNKS - 1:
                    for m in range(KT):
                        last = pe.matmul(ps[:, 6, m * N:(m + 1) * N], d_diag[:, m, :], xc[par][:, m, :], start=False, stop=True,
                                         skip_group_check=True)
                    last.then_inc(y_ps, 1)

            def skip(g, par):
                for r in range(GB):
                    for k in range(KT):
                        pe.matmul(ps[0:S, 7, r * D:(r + 1) * D], x3T[par][:, k, r * S:(r + 1) * S], skip_w[:, k, :], start=r == 0 and k == 0,
                                  stop=False, skip_group_check=True)
                    pe.matmul(ps[0:S, 7, r * D:(r + 1) * D], ones2[:, 0:S], outskip_b, start=False, stop=False, skip_group_check=True)

            def project_out(g):
                pe.wait_ge(yT_ready, g + 2)
                for r in range(GB):
                    for k in range(KT):
                        last = pe.matmul(ps[0:S, 7, r * D:(r + 1) * D], yT[:, k, r * S:(r + 1) * S], out_w[:, k, :], start=False,
                                         stop=k == KT - 1, skip_group_check=True)
                last.then_inc(ssm_ps, 1)

            def step(g, par, more=True, before=True, turn_next=True):
                for c in range(CHUNKS):
                    if c < CHUNKS - 1:
                        spread(g, c + 1, par)
                    elif more:
                        spread(g + 1, 0, 1 - par)
                    if not before and c <= OPENING:
                        project_in(1, 1, c)
                    if c == 0 and before:
                        reduce(g - 1, CHUNKS - 1, 1 - par)
                    if more:
                        if c == (AT_CONV if before else OPENING):
                            convolve(g + 1)
                        if c == AT_DT:
                            project_dt(g + 1)
                    if turn_next:
                        if c == AT_TURN:
                            turn(g + 2)
                        if c >= AT_IN:
                            project_in(g + 2, par, c - AT_IN)
                    if c > 0:
                        reduce(g, c - 1, par)
                    if before and c == AT_OUT:
                        project_out(g - 1)
                    if more and c == AT_RANK:
                        project_x(g + 1, 1 - par)
                    if c == AT_SKIP:
                        if before:
                            pe.wait_ge(resid3_ready, g)
                        skip(g, par)

            pe.wait_ge(diag_done, KT * (TAPS + 1))
            pe.wait_ge(pick_done, 1)
            pe.wait_ge(wqT_ready, 2 + 2 * FT + 4)
            turn(0, first=True)
            for half in range(2):
                project_in(0, 0, half, first=True)
            convolve(0)
            project_x(0, 0)
            project_dt(0)
            turn(1)
            spread(0, 0, 0)
            step(0, 0, before=False)
            with pe.Fori(0, (GROUPS - 4) // 2) as i:
                for half in range(2):
                    step(2 * i + 1 + half, 1 - half)
            step(GROUPS - 3, 1)
            step(GROUPS - 2, 0, turn_next=False)
            step(GROUPS - 1, 1, more=False, turn_next=False)
            reduce(GROUPS - 1, CHUNKS - 1, 1)
            project_out(GROUPS - 1)

        @block.tensor
        def _(pe):
            pe_tokens(pe)
            pe_attention(pe)
            pe_router(pe)
            pe_shared(pe)
            pe_experts(pe)
            pe_weights_down(pe)
            pe_ssm(pe)
            pe_ffn(pe)


def _constants():
    c = np.zeros((P, NCONST), np.float32)
    c[:, C_ID:C_ID + P] = np.eye(P)
    q, k = np.arange(S)[:, None], np.arange(S)[None, :]
    c[:S, C_MQ:C_MQ + S] = np.where(k > q, NEG, 0.0)
    c[:S, C_MK:C_MK + S] = np.where(k < q, NEG, 0.0)
    c[:S, C_UP:C_UP + S] = k > q
    c[:, C_REP:C_REP + 32] = np.tile(np.eye(32), (4, 1))
    c[:, C_E8:C_E8 + EXPERTS] = np.arange(EXPERTS) - EXPERTS
    c[:, C_K128:C_K128 + NK128] = ETILE * np.arange(NK128)
    c[:, C_TILE:C_TILE + ETILES] = np.arange(ETILES)
    c[:, C_RES:C_RES + EXPERTS * B] = np.arange(EXPERTS * B) % B > 0
    c[:, C_RES8:C_RES8 + EXPERTS] = 1.0
    return c


def _tiles(w, parts=P):
    return np.ascontiguousarray(w.reshape(-1, parts, w.shape[-1]).transpose(1, 0, 2))


def _layout(x, n):
    a = {}
    img = np.asarray(x["x"])
    a["patches"] = _tiles(np.ascontiguousarray(img.reshape(B, 6, 16, 6, 16, 3).transpose(2, 4, 5, 0, 1, 3)).reshape(PATCH, B * IMG))
    a["tok_w"] = _tiles(n["L0_tok_W_proj"].T)
    a["tok_b"] = n["L0_tok_b_proj"].reshape(KT, P).T
    a["pos"] = _tiles(n["L0_tok_pos_emb"].T)
    a["txt"] = n["txt"]
    qkv, qkv_b = n["L0_attn_qkv_w"], n["L0_attn_qkv_b"]
    a["qk_w"] = _tiles(qkv[:, :2 * D]).reshape(P, KT, 2 * KT, P)
    a["qk_b"] = qkv_b[:2 * D].reshape(2 * KT, P).T
    a["v_w"], a["v_b"] = _tiles(qkv[:, 2 * D:]), qkv_b[None, 2 * D:]
    ow = np.zeros((4, 32, QUADS, D), np.float32)
    ow[:, :HD] = n["L0_attn_out_w"].reshape(QUADS, 4, HD, D).transpose(1, 2, 0, 3)
    a["o_w"], a["o_b"] = ow.reshape(P, QUADS, D), n["L0_attn_out_b"][None]
    row, col = np.arange(P)[:, None], np.arange(P)[None, :]
    a["sum_pick"] = (row == col // 32 * 32 + HD).astype(np.float32)
    a["head_mask"] = (row // HD == np.arange(HT8)[None, :]).astype(np.float32)
    a["router_w"] = _tiles(n["L0_ffn_router"].T)

    def expert(gate, up, down):
        return np.concatenate([_tiles(w.T).reshape(P, -1) for w in (up, gate, down)], axis=1)

    a["sh_w"] = expert(n["L0_ffn_w_gate_s"], n["L0_ffn_w_up_s"], n["L0_ffn_w_down_s"])
    a["ex_w"] = np.stack([expert(n["L0_ffn_gate"][e], n["L0_ffn_up"][e], n["L0_ffn_down"][e]) for e in range(EXPERTS)])
    m = {k: n["L1_attn_" + k] for k in ("in_proj_w", "in_proj_b", "conv_w", "conv_b", "x_proj_w", "x_proj_b", "dt_proj_w",
                                        "dt_proj_b", "A_log", "D_param", "out_proj_w", "out_proj_b", "skip_proj_w", "skip_proj_b")}
    a["in_w"], a["in_b"] = _tiles(m["in_proj_w"].T), m["in_proj_b"].reshape(2 * KT, P).T
    a["conv_w"] = m["conv_w"].reshape(KT, P, TAPS).transpose(1, 0, 2)
    a["conv_b"] = m["conv_b"].reshape(KT, P).T
    a["rank_w"], a["rank_b"] = _tiles(m["x_proj_w"][:RANK].T), m["x_proj_b"][:RANK, None]
    a["bc_w"] = _tiles(np.tile(m["x_proj_w"][RANK:], (3, 1)).T)
    a["bc_b"] = np.tile(m["x_proj_b"][RANK:], 3)[:, None]
    a["dt_w"], a["dt_b"] = m["dt_proj_w"].T, m["dt_proj_b"].reshape(KT, P).T
    a["a_log"], a["d_par"] = m["A_log"], m["D_param"].reshape(KT, P).T
    a["out_w"], a["skip_w"] = _tiles(m["out_proj_w"].T), _tiles(m["skip_proj_w"].T)
    a["outskip_b"] = np.stack([m["out_proj_b"], m["skip_proj_b"]])
    a["f_gate"] = n["L1_ffn_w_gate"].reshape(FT, FP, D).transpose(1, 0, 2)
    a["f_up"] = n["L1_ffn_w_up"].reshape(FT, FP, D).transpose(1, 0, 2)
    a["f_down"] = _tiles(n["L1_ffn_w_down"])
    a["clip_x"], a["clip_h"] = n["L1_ffn_clip_x"][None], n["L1_ffn_clip_down"][None]
    a["const"] = _constants()
    return {k: np.ascontiguousarray(v) for k, v in a.items()}


def kernel(**inputs):
    import concourse.bacc as bacc
    from concourse.bass_utils import run_bass_kernel_spmd

    given = {k: np.asarray(v) for k, v in inputs.items()}
    arrays = _layout(given, given)
    nc = bacc.Bacc("TRN2", target_bir_lowering=False, num_devices=1)
    a = {k: nc.dram_tensor("in_" + k, v.shape, mybir.dt.from_np(v.dtype), kind="ExternalInput").ap() for k, v in arrays.items()}
    out = nc.dram_tensor("out", (B, S, D), F32, kind="ExternalOutput").ap()
    build(nc, a, out)
    result = run_bass_kernel_spmd(nc, [{"in_" + k: v for k, v in arrays.items()}], core_ids=[0])
    return result.results[0]["out"]
```
